# Optimizing a Trainium2 kernel written in Bass

```python
import numpy as np
import jax
import jax.numpy as jnp

def _softmax(x, axis=-1):
    return jax.nn.softmax(x, axis=axis)

def _gelu(x):
    return jax.nn.gelu(x, approximate=True)

def _silu(x):
    return jax.nn.silu(x)

def _sigmoid(x):
    return jax.nn.sigmoid(x)

def _layernorm(x, axis=-1, eps=1e-05):
    m = jnp.mean(x, axis=axis, keepdims=True)
    v = jnp.var(x, axis=axis, keepdims=True)
    return (x - m) / jnp.sqrt(v + eps)

def _scatter_add(tgt, idx, src, axis=0):
    return tgt.at[idx].add(src)

def _segment_sum(src, seg, n):
    return jax.ops.segment_sum(src, seg, n)
kernel_name = 'mk_xattn_ffn_d4_seqx_r8_5ffce7'

def setup_inputs(seed: int=0):
    np.random.seed(seed)
    _w = jnp.asarray

    def _rec_inputs():
        import jax
        import jax.numpy as jnp
        _rk = jax.random.key(seed)
        x = -0.0002928 + 1 * jax.random.normal(jax.random.fold_in(_rk, 1), (8, 256, 128), jnp.float32)
        _lenS = 256 - jax.random.randint(jax.random.fold_in(_rk, 7), (8,), 0, max(1, 256 // 4) + 1, jnp.int32)
        _lenS2 = 256 - jax.random.randint(jax.random.fold_in(_rk, 8), (8,), 0, max(1, 256 // 4) + 1, jnp.int32)
        _ctx_1024P = jax.random.normal(jax.random.fold_in(_rk, 11), (8, 16, 128), jnp.float32)
        _ctx_1024c = jax.random.dirichlet(jax.random.fold_in(_rk, 511), 0.3 * jnp.ones((16,), jnp.float32), (8, 256))
        _ctx_1024t = jnp.einsum('bsk,bkd->bsd', _ctx_1024c, _ctx_1024P)
        _ctx_1024t = _ctx_1024t * jax.lax.rsqrt(jnp.mean(jnp.square(_ctx_1024t)) + 1e-12) * 0.953939
        ctx_1024 = -1.39393e-06 + 0.999914 * (_ctx_1024t + 0.3 * jax.random.normal(jax.random.fold_in(_rk, 611), (8, 256, 128), jnp.float32))
        _validS = jnp.arange(256)[None, :] < _lenS[:, None]
        _validS2 = jnp.arange(256)[None, :] < _lenS2[:, None]
        _causal = jnp.tril(jnp.ones((256, 256), dtype=bool))
        mask_Bx1xSxS2_ik1 = jnp.where(jnp.broadcast_to(_validS2[:, None, None, :], (8, 1, 256, 256)), 1, 0).astype(jnp.int32)
        mask_Bx1x1xS2_if1 = jnp.where(jnp.ones((8, 1, 1, 256), dtype=bool), 1, 0).astype(jnp.int32)
        mask_1x1xSxS2_fk1 = jnp.where(jnp.broadcast_to(_validS2[0:1, None, None, :], (1, 1, 256, 256)), 1.0, 0.0).astype(jnp.float32)
        return (x, ctx_1024, mask_Bx1xSxS2_ik1, mask_Bx1x1xS2_if1, mask_1x1xSxS2_fk1)
    x, ctx_1024, mask_Bx1xSxS2_ik1, mask_Bx1x1xS2_if1, mask_1x1xSxS2_fk1 = _rec_inputs()

    def _L0_xattn_setup():
        import jax, jax.numpy as jnp
        import numpy as np
        B, S, E, NH = (2, 256, 128, 4)
        HD = E // NH

        def _mlstm_head(q, k, v, ig, fg, eps=1e-06):
            s, dh = q.shape
            log_f = jax.nn.log_sigmoid(fg)
            cs = jnp.concatenate([jnp.zeros((1, 1), log_f.dtype), jnp.cumsum(log_f, axis=0)], axis=0)
            neg = jnp.asarray(-0.7 * jnp.finfo(cs.dtype).max, cs.dtype)
            log_d = jnp.where(jnp.tri(s, dtype=bool), (cs - cs.T)[1:, 1:] + ig.T, neg)
            m = jnp.max(log_d, axis=-1, keepdims=True)
            d = jnp.exp(log_d - m)
            c = q @ (k.T / jnp.sqrt(dh)) * d
            n = jnp.maximum(jnp.sum(c, axis=-1, keepdims=True), jnp.exp(-m))
            return c / (n + eps) @ v
        key = jax.random.key(seed)
        ks = jax.random.split(key, 8)
        return {'q': jax.random.normal(ks[0], (B, S, E), jnp.float32), 'k': jax.random.normal(ks[1], (B, S, E), jnp.float32), 'v': jax.random.normal(ks[2], (B, S, E), jnp.float32), 'igate_kernel': jax.random.normal(ks[3], (3 * E, NH), jnp.float32) * 0.02, 'igate_bias': jax.random.normal(ks[4], (NH,), jnp.float32) * 0.1, 'fgate_kernel': jax.random.normal(ks[5], (3 * E, NH), jnp.float32) * 0.02, 'fgate_bias': jnp.linspace(3.0, 6.0, NH, dtype=jnp.float32), 'rms_scale': jax.random.normal(ks[6], (HD,), jnp.float32) * 0.02}
    _L0_xattn_all = _L0_xattn_setup()
    _L0_xattn_in = {k: v for k, v in _L0_xattn_all.items() if k in ('igate_kernel', 'igate_bias', 'fgate_kernel', 'fgate_bias', 'rms_scale')}
    del _L0_xattn_all

    def _L0_ffn_setup():
        import jax, jax.numpy as jnp
        import numpy as np
        QMAX = 127.0

        def _ste_round(v):
            return v + jax.lax.stop_gradient(jnp.round(v) - v)

        def _act_fake_quant(x, clip_factor):
            scale = jax.nn.sigmoid(clip_factor) * jnp.max(jnp.abs(x)) / QMAX
            return jnp.clip(_ste_round(x / scale), -QMAX - 1.0, QMAX) * scale

        def _weight_fake_quant(w):
            scale = jnp.max(jnp.abs(w), axis=1, keepdims=True) / QMAX
            return jnp.clip(_ste_round(w / scale), -QMAX - 1.0, QMAX) * scale
        key = jax.random.key(seed)
        k1, k2, k3, k4 = jax.random.split(key, 4)
        B, S, H, I = (8, 1024, 128, 352)
        return {'x': jax.random.normal(k1, (B, S, H), dtype=jnp.float32), 'clip_x': jnp.full((1,), 4.0, dtype=jnp.float32), 'clip_down': jnp.full((1,), 4.0, dtype=jnp.float32), 'w_gate': jax.random.normal(k2, (I, H), dtype=jnp.float32) * 0.02, 'w_up': jax.random.normal(k3, (I, H), dtype=jnp.float32) * 0.02, 'w_down': jax.random.normal(k4, (H, I), dtype=jnp.float32) * 0.02}
    _L0_ffn_all = _L0_ffn_setup()
    _L0_ffn_in = {k: v for k, v in _L0_ffn_all.items() if k in ('clip_x', 'clip_down', 'w_gate', 'w_up', 'w_down')}
    del _L0_ffn_all

    def _L1_xattn_setup():
        import jax, jax.numpy as jnp
        import numpy as np
        B, L, E, H = (2, 256, 128, 16)
        D = E // H
        key = jax.random.key(seed)
        ks = jax.random.split(key, 6)
        values = jax.random.normal(ks[0], (B, L, E), dtype=jnp.float32)
        keys = jax.random.normal(ks[1], (B, L, E), dtype=jnp.float32)
        query = jax.random.normal(ks[2], (B, L, E), dtype=jnp.float32)
        mask = jax.random.randint(ks[3], (B, 1, L, L), 0, 2, dtype=jnp.int32)
        W_out = jax.random.normal(ks[4], (E, E), dtype=jnp.float32) * 0.02
        b_out = jax.random.normal(ks[5], (E,), dtype=jnp.float32) * 0.02
        return {'values': values, 'keys': keys, 'query': query, 'mask': mask, 'W_out': W_out, 'b_out': b_out}
    _L1_xattn_all = _L1_xattn_setup()
    _L1_xattn_in = {k: v for k, v in _L1_xattn_all.items() if k in ('W_out', 'b_out')}
    del _L1_xattn_all

    def _L1_ffn_setup():
        import jax, jax.numpy as jnp
        import numpy as np
        BLOCK = 32
        W_BITS = 4
        ACT_BITS = 16

        def act_qdq(x):
            qmax = 2.0 ** (ACT_BITS - 1) - 1.0
            scale = jnp.maximum(jnp.max(jnp.abs(x)) / qmax, 1e-12)
            return jnp.clip(jnp.round(x / scale), -qmax - 1.0, qmax) * scale

        def fixed_qdq_u16(x):
            scale = 1.0 / 65536.0
            return jnp.clip(jnp.round(x / scale), 0.0, 65535.0) * scale

        def lpbq_dequant(w):
            O, I = w.shape
            qmax = 2.0 ** (W_BITS - 1) - 1.0
            wb = w.reshape(O, I // BLOCK, BLOCK)
            s = jnp.maximum(jnp.max(jnp.abs(wb), axis=-1, keepdims=True) / qmax, 1e-12)
            wq = jnp.clip(jnp.round(wb / s), -qmax - 1.0, qmax) * s
            return wq.reshape(O, I)
        key = jax.random.key(seed)
        k1, k2, k3, k4 = jax.random.split(key, 4)
        B, S, H, I = (2, 512, 128, 384)
        x = jax.random.normal(k1, (B, S, H), jnp.float32)
        w_gate = jax.random.normal(k2, (I, H), jnp.float32) * 0.02
        w_up = jax.random.normal(k3, (I, H), jnp.float32) * 0.02
        w_down = jax.random.normal(k4, (H, I), jnp.float32) * 0.02
        return {'x': x, 'w_gate': w_gate, 'w_up': w_up, 'w_down': w_down}
    _L1_ffn_all = _L1_ffn_setup()
    _L1_ffn_in = {k: v for k, v in _L1_ffn_all.items() if k in ('w_gate', 'w_up', 'w_down')}
    del _L1_ffn_all

    def _L2_xattn_setup():
        import jax, jax.numpy as jnp
        import numpy as np
        EMBED_SIZE = 128
        HEADS = 16
        HEAD_DIM = EMBED_SIZE // HEADS
        key = jax.random.key(seed)
        ks = jax.random.split(key, 8)
        N, S = (2, 256)
        inv = 1.0 / np.sqrt(HEAD_DIM)
        return {'values': jax.random.normal(ks[0], (N, S, EMBED_SIZE), dtype=jnp.float32), 'keys': jax.random.normal(ks[1], (N, S, EMBED_SIZE), dtype=jnp.float32), 'query': jax.random.normal(ks[2], (N, S, EMBED_SIZE), dtype=jnp.float32), 'mask': jnp.ones((N, 1, 1, S), dtype=jnp.int32), 'Wv': jax.random.normal(ks[3], (HEAD_DIM, HEAD_DIM), dtype=jnp.float32) * inv, 'Wk': jax.random.normal(ks[4], (HEAD_DIM, HEAD_DIM), dtype=jnp.float32) * inv, 'Wq': jax.random.normal(ks[5], (HEAD_DIM, HEAD_DIM), dtype=jnp.float32) * inv, 'Wo': jax.random.normal(ks[6], (EMBED_SIZE, EMBED_SIZE), dtype=jnp.float32) / np.sqrt(EMBED_SIZE), 'bo': jnp.zeros((EMBED_SIZE,), dtype=jnp.float32)}
    _L2_xattn_all = _L2_xattn_setup()
    _L2_xattn_in = {k: v for k, v in _L2_xattn_all.items() if k in ('Wv', 'Wk', 'Wq', 'Wo', 'bo')}
    del _L2_xattn_all

    def _L2_ffn_setup():
        import jax, jax.numpy as jnp
        import numpy as np
        DIM = 128
        DEPTH = 6
        HEADS = 16
        DIM_HEAD = 64
        WINDOW = 32
        INNER = HEADS * DIM_HEAD
        DIM_INNER = int(DIM * 4 * 2 / 3)
        QK_SCALE = 8.0

        def shift_tokens(t):
            a, s = jnp.split(t, 2, -1)
            s = jnp.pad(s, ((0, 0), (1, 0), (0, 0)))[:, :-1]
            return jnp.concatenate([a, s], -1)

        def l2norm(t):
            return t / jnp.maximum(jnp.linalg.norm(t, axis=-1, keepdims=True), 1e-12)

        def rotate_half(x):
            x1, x2 = jnp.split(x, 2, -1)
            return jnp.concatenate([-x2, x1], -1)

        def rotary_tables(n):
            half = jnp.arange(0, DIM_HEAD, 2, dtype=jnp.float32)
            inv_freq = 1.0 / 10000.0 ** (half / DIM_HEAD)
            t = jnp.arange(n, dtype=jnp.float32)
            freqs = t[:, None] * inv_freq[None, :]
            freqs = jnp.concatenate([freqs, freqs], -1)
            base_scale = (half + 0.4 * DIM_HEAD) / (1.4 * DIM_HEAD)
            power = (t - n // 2) / (WINDOW // 2)
            scale = base_scale[None, :] ** power[:, None]
            scale = jnp.concatenate([scale, scale], -1)
            return (freqs, scale)

        def local_attention(q, k, v):
            b, h, n, d = q.shape
            w = WINDOW
            nw = n // w
            bq = q.reshape(b, h, nw, w, d)
            bk = k.reshape(b, h, nw, w, d)
            bv = v.reshape(b, h, nw, w, d)

            def look(t):
                p = jnp.pad(t, ((0, 0), (0, 0), (1, 0), (0, 0), (0, 0)))
                return jnp.concatenate([p[:, :, :nw], p[:, :, 1:]], axis=3)
            bk2, bv2 = (look(bk), look(bv))
            seq = jnp.arange(n).reshape(nw, w)
            seq_p = jnp.pad(seq, ((1, 0), (0, 0)), constant_values=-1)
            jt = jnp.concatenate([seq_p[:nw], seq_p[1:]], axis=1)
            it = seq[:, :, None]
            jb = jt[:, None, :]
            mask = (it < jb) | (it > jb + w) | (jb == -1)
            sim = jnp.einsum('bhwie,bhwje->bhwij', bq, bk2) * QK_SCALE
            sim = jnp.where(mask, -jnp.finfo(sim.dtype).max, sim)
            attn = jax.nn.softmax(sim, -1)
            out = jnp.einsum('bhwij,bhwje->bhwie', attn, bv2)
            return out.reshape(b, h, n, d)

        def attn_layer(x, Wqkv, qs, ksc, Wo):
            b, n, _ = x.shape
            qkv = x @ Wqkv
            q, k, v = jnp.split(qkv, 3, -1)
            sh = lambda t: t.reshape(b, n, HEADS, DIM_HEAD).transpose(0, 2, 1, 3)
            q, k, v = (sh(q), sh(k), sh(v))
            q = l2norm(q) * qs
            k = l2norm(k) * ksc
            freqs, scale = rotary_tables(n)
            cos, sin = (jnp.cos(freqs), jnp.sin(freqs))
            q = q * cos * scale + rotate_half(q) * sin * scale
            inv = 1.0 / scale
            k = k * cos * inv + rotate_half(k) * sin * inv
            out = local_attention(q, k, v)
            out = out.transpose(0, 2, 1, 3).reshape(b, n, INNER)
            return out @ Wo

        def ffn_layer(x, g, bln, W1, b1, W2, b2):
            mu = x.mean(-1, keepdims=True)
            var = ((x - mu) ** 2).mean(-1, keepdims=True)
            xn = (x - mu) / jnp.sqrt(var + 1e-05) * g + bln
            hg = xn @ W1 + b1
            a, gate = jnp.split(hg, 2, -1)
            return a * jax.nn.gelu(gate, approximate=False) @ W2 + b2
        key = jax.random.key(seed)
        ks = jax.random.split(key, 8)
        B, N = (2, 256)
        init = lambda k, shape: jax.random.normal(k, shape, jnp.float32) * 0.02
        return {'x': jax.random.normal(ks[0], (B, N, DIM), jnp.float32), 'Wqkv': init(ks[1], (DEPTH, DIM, 3 * INNER)), 'q_scale': jnp.ones((DEPTH, DIM_HEAD), jnp.float32), 'k_scale': jnp.ones((DEPTH, DIM_HEAD), jnp.float32), 'Wo': init(ks[2], (DEPTH, INNER, DIM)), 'ln_g': jnp.ones((DEPTH, DIM), jnp.float32), 'ln_b': jnp.zeros((DEPTH, DIM), jnp.float32), 'W1': init(ks[3], (DEPTH, DIM, 2 * DIM_INNER)), 'b1': jnp.zeros((DEPTH, 2 * DIM_INNER), jnp.float32), 'W2': init(ks[4], (DEPTH, DIM_INNER, DIM)), 'b2': jnp.zeros((DEPTH, DIM), jnp.float32)}
    _L2_ffn_all = _L2_ffn_setup()
    _L2_ffn_in = {k: v for k, v in _L2_ffn_all.items() if k in ('Wqkv', 'q_scale', 'k_scale', 'Wo', 'ln_g', 'ln_b', 'W1', 'b1', 'W2', 'b2')}
    del _L2_ffn_all

    def _L3_xattn_setup():
        import jax, jax.numpy as jnp
        import numpy as np
        D_MODEL = 128
        NUM_HEADS = 16
        DEPTH = D_MODEL // NUM_HEADS
        B, S = (4, 256)

        def _split_heads(x):
            b, s, _ = x.shape
            return x.reshape(b, s, NUM_HEADS, DEPTH).transpose(0, 2, 1, 3)
        key = jax.random.key(seed)
        ks = jax.random.split(key, 12)
        scale = 1.0 / np.sqrt(D_MODEL)
        inp = {'q': jax.random.normal(ks[0], (B, S, D_MODEL), jnp.float32), 'k': jax.random.normal(ks[1], (B, S, D_MODEL), jnp.float32), 'v': jax.random.normal(ks[2], (B, S, D_MODEL), jnp.float32), 'mask': jnp.triu(jnp.ones((S, S), jnp.float32), k=1)[None, None, :, :], 'wq': jax.random.normal(ks[3], (D_MODEL, D_MODEL), jnp.float32) * scale, 'bq': jnp.zeros((D_MODEL,), jnp.float32), 'wk': jax.random.normal(ks[4], (D_MODEL, D_MODEL), jnp.float32) * scale, 'bk': jnp.zeros((D_MODEL,), jnp.float32), 'wv': jax.random.normal(ks[5], (D_MODEL, D_MODEL), jnp.float32) * scale, 'bv': jnp.zeros((D_MODEL,), jnp.float32), 'wo': jax.random.normal(ks[6], (D_MODEL, D_MODEL), jnp.float32) * scale, 'bo': jnp.zeros((D_MODEL,), jnp.float32)}
        return inp
    _L3_xattn_all = _L3_xattn_setup()
    _L3_xattn_in = {k: v for k, v in _L3_xattn_all.items() if k in ('wq', 'bq', 'wk', 'bk', 'wv', 'bv', 'wo', 'bo')}
    del _L3_xattn_all

    def _L3_ffn_setup():
        import jax, jax.numpy as jnp
        import numpy as np
        EPS = 1e-05

        def _layernorm(x, w, b):
            mu = jnp.mean(x, axis=-1, keepdims=True)
            var = jnp.mean((x - mu) ** 2, axis=-1, keepdims=True)
            return (x - mu) * jax.lax.rsqrt(var + EPS) * w + b

        def _rope_tables(T, D, base=10000.0):
            inv_freq = 1.0 / base ** (jnp.arange(0, D, 2, dtype=jnp.float32) / D)
            t = jnp.arange(T, dtype=jnp.float32)
            freqs = jnp.einsum('i,j->ij', t, inv_freq)
            emb = jnp.concatenate([freqs, freqs], axis=-1)
            return (jnp.cos(emb), jnp.sin(emb))

        def _rotate_half(x):
            x1, x2 = (x[..., :x.shape[-1] // 2], x[..., x.shape[-1] // 2:])
            return jnp.concatenate([-x2, x1], axis=-1)

        def _attn(x, ln_w, ln_b, conv_w, attn_w, proj_w, n_head):
            B, T, C = x.shape
            D = C // n_head
            h = _layernorm(x, ln_w, ln_b)
            hc = jnp.transpose(h, (0, 2, 1))
            hc = jnp.pad(hc, ((0, 0), (0, 0), (2, 0)))
            hc = jax.lax.conv_general_dilated(hc, conv_w, window_strides=(1,), padding='VALID', dimension_numbers=('NCH', 'OIH', 'NCH'), feature_group_count=C)
            h = jnp.transpose(hc, (0, 2, 1))
            qkv = h @ attn_w
            q, k, v = jnp.split(qkv, 3, axis=-1)
            q = q.reshape(B, T, n_head, D)
            k = k.reshape(B, T, n_head, D)
            v = v.reshape(B, T, n_head, D)
            cos, sin = _rope_tables(T, D)
            cos = cos[None, :, None, :]
            sin = sin[None, :, None, :]
            q = q * cos + _rotate_half(q) * sin
            k = k * cos + _rotate_half(k) * sin
            scores = jnp.einsum('bqhd,bkhd->bhqk', q, k) / jnp.sqrt(jnp.float32(D))
            causal = jnp.tril(jnp.ones((T, T), dtype=bool))
            scores = jnp.where(causal, scores, jnp.float32(-1e+30))
            p = jax.nn.softmax(scores, axis=-1)
            y = jnp.einsum('bhqk,bkhd->bqhd', p, v).reshape(B, T, C)
            return y @ proj_w

        def _moe(x, ln_w, ln_b, router_w, expert_wv, expert_proj):
            h = _layernorm(x, ln_w, ln_b)
            logits = h @ router_w
            expert_idx = jnp.argmax(logits, axis=-1)
            E = router_w.shape[-1]
            out = jnp.zeros_like(x)
            for e in range(E):
                gv = h @ expert_wv[e]
                gate_raw, value = jnp.split(gv, 2, axis=-1)
                y = gate_raw * jax.nn.sigmoid(gate_raw) * value @ expert_proj[e]
                out = out + jnp.where((expert_idx == e)[..., None], y, 0.0)
            return out
        C, H, E, B, T = (128, 16, 4, 4, 128)
        Dff = 4 * C
        key = jax.random.key(seed)
        ks = jax.random.split(key, 8)
        s = 0.02
        return {'x': jax.random.normal(ks[0], (B, T, C), dtype=jnp.float32), 'ln1_w': jnp.ones((C,), jnp.float32), 'ln1_b': jnp.zeros((C,), jnp.float32), 'ln2_w': jnp.ones((C,), jnp.float32), 'ln2_b': jnp.zeros((C,), jnp.float32), 'conv_w': jax.random.normal(ks[1], (C, 1, 3), dtype=jnp.float32) * 0.1, 'attn_w': jax.random.normal(ks[2], (C, 3 * C), dtype=jnp.float32) * s, 'proj_w': jax.random.normal(ks[3], (C, C), dtype=jnp.float32) * s, 'router_w': jax.random.normal(ks[4], (C, E), dtype=jnp.float32) * s, 'expert_wv': jax.random.normal(ks[5], (E, C, 2 * Dff), dtype=jnp.float32) * s, 'expert_proj': jax.random.normal(ks[6], (E, Dff, C), dtype=jnp.float32) * s}
    _L3_ffn_all = _L3_ffn_setup()
    _L3_ffn_in = {k: v for k, v in _L3_ffn_all.items() if k in ('ln1_w', 'ln1_b', 'ln2_w', 'ln2_b', 'conv_w', 'attn_w', 'proj_w', 'router_w', 'expert_wv', 'expert_proj')}
    del _L3_ffn_all
    return {'x': x, 'ctx_1024': ctx_1024, 'mask_Bx1xSxS2_ik1': mask_Bx1xSxS2_ik1, 'mask_Bx1x1xS2_if1': mask_Bx1x1xS2_if1, 'mask_1x1xSxS2_fk1': mask_1x1xSxS2_fk1, 'L0_xattn_igate_kernel': _L0_xattn_in['igate_kernel'], 'L0_xattn_igate_bias': _L0_xattn_in['igate_bias'], 'L0_xattn_fgate_kernel': _L0_xattn_in['fgate_kernel'], 'L0_xattn_fgate_bias': _L0_xattn_in['fgate_bias'], 'L0_xattn_rms_scale': _L0_xattn_in['rms_scale'], 'L0_ffn_clip_x': _L0_ffn_in['clip_x'], 'L0_ffn_clip_down': _L0_ffn_in['clip_down'], 'L0_ffn_w_gate': _L0_ffn_in['w_gate'], 'L0_ffn_w_up': _L0_ffn_in['w_up'], 'L0_ffn_w_down': _L0_ffn_in['w_down'], 'L1_xattn_W_out': _L1_xattn_in['W_out'], 'L1_xattn_b_out': _L1_xattn_in['b_out'], 'L1_ffn_w_gate': _L1_ffn_in['w_gate'], 'L1_ffn_w_up': _L1_ffn_in['w_up'], 'L1_ffn_w_down': _L1_ffn_in['w_down'], 'L2_xattn_Wv': _L2_xattn_in['Wv'], 'L2_xattn_Wk': _L2_xattn_in['Wk'], 'L2_xattn_Wq': _L2_xattn_in['Wq'], 'L2_xattn_Wo': _L2_xattn_in['Wo'], 'L2_xattn_bo': _L2_xattn_in['bo'], 'L2_ffn_Wqkv': _L2_ffn_in['Wqkv'], 'L2_ffn_q_scale': _L2_ffn_in['q_scale'], 'L2_ffn_k_scale': _L2_ffn_in['k_scale'], 'L2_ffn_Wo': _L2_ffn_in['Wo'], 'L2_ffn_ln_g': _L2_ffn_in['ln_g'], 'L2_ffn_ln_b': _L2_ffn_in['ln_b'], 'L2_ffn_W1': _L2_ffn_in['W1'], 'L2_ffn_b1': _L2_ffn_in['b1'], 'L2_ffn_W2': _L2_ffn_in['W2'], 'L2_ffn_b2': _L2_ffn_in['b2'], 'L3_xattn_wq': _L3_xattn_in['wq'], 'L3_xattn_bq': _L3_xattn_in['bq'], 'L3_xattn_wk': _L3_xattn_in['wk'], 'L3_xattn_bk': _L3_xattn_in['bk'], 'L3_xattn_wv': _L3_xattn_in['wv'], 'L3_xattn_bv': _L3_xattn_in['bv'], 'L3_xattn_wo': _L3_xattn_in['wo'], 'L3_xattn_bo': _L3_xattn_in['bo'], 'L3_ffn_ln1_w': _L3_ffn_in['ln1_w'], 'L3_ffn_ln1_b': _L3_ffn_in['ln1_b'], 'L3_ffn_ln2_w': _L3_ffn_in['ln2_w'], 'L3_ffn_ln2_b': _L3_ffn_in['ln2_b'], 'L3_ffn_conv_w': _L3_ffn_in['conv_w'], 'L3_ffn_attn_w': _L3_ffn_in['attn_w'], 'L3_ffn_proj_w': _L3_ffn_in['proj_w'], 'L3_ffn_router_w': _L3_ffn_in['router_w'], 'L3_ffn_expert_wv': _L3_ffn_in['expert_wv'], 'L3_ffn_expert_proj': _L3_ffn_in['expert_proj']}

def reference(x, ctx_1024, mask_Bx1xSxS2_ik1, mask_Bx1x1xS2_if1, mask_1x1xSxS2_fk1, L0_xattn_igate_kernel, L0_xattn_igate_bias, L0_xattn_fgate_kernel, L0_xattn_fgate_bias, L0_xattn_rms_scale, L0_ffn_clip_x, L0_ffn_clip_down, L0_ffn_w_gate, L0_ffn_w_up, L0_ffn_w_down, L1_xattn_W_out, L1_xattn_b_out, L1_ffn_w_gate, L1_ffn_w_up, L1_ffn_w_down, L2_xattn_Wv, L2_xattn_Wk, L2_xattn_Wq, L2_xattn_Wo, L2_xattn_bo, L2_ffn_Wqkv, L2_ffn_q_scale, L2_ffn_k_scale, L2_ffn_Wo, L2_ffn_ln_g, L2_ffn_ln_b, L2_ffn_W1, L2_ffn_b1, L2_ffn_W2, L2_ffn_b2, L3_xattn_wq, L3_xattn_bq, L3_xattn_wk, L3_xattn_bk, L3_xattn_wv, L3_xattn_bv, L3_xattn_wo, L3_xattn_bo, L3_ffn_ln1_w, L3_ffn_ln1_b, L3_ffn_ln2_w, L3_ffn_ln2_b, L3_ffn_conv_w, L3_ffn_attn_w, L3_ffn_proj_w, L3_ffn_router_w, L3_ffn_expert_wv, L3_ffn_expert_proj):
    import jax
    import jax.numpy as jnp

    def _L0_xattn_ref(q, k, v, igate_kernel, igate_bias, fgate_kernel, fgate_bias, rms_scale):
        import jax, jax.numpy as jnp
        import numpy as np
        B, S, E, NH = (2, 256, 128, 4)
        HD = E // NH

        def _mlstm_head(q, k, v, ig, fg, eps=1e-06):
            s, dh = q.shape
            log_f = jax.nn.log_sigmoid(fg)
            cs = jnp.concatenate([jnp.zeros((1, 1), log_f.dtype), jnp.cumsum(log_f, axis=0)], axis=0)
            neg = jnp.asarray(-0.7 * jnp.finfo(cs.dtype).max, cs.dtype)
            log_d = jnp.where(jnp.tri(s, dtype=bool), (cs - cs.T)[1:, 1:] + ig.T, neg)
            m = jnp.max(log_d, axis=-1, keepdims=True)
            d = jnp.exp(log_d - m)
            c = q @ (k.T / jnp.sqrt(dh)) * d
            n = jnp.maximum(jnp.sum(c, axis=-1, keepdims=True), jnp.exp(-m))
            return c / (n + eps) @ v
        b, s, e = q.shape
        nh = igate_kernel.shape[1]
        hd = e // nh
        gate_in = jnp.concatenate((q, k, v), axis=-1)
        ig = (gate_in @ igate_kernel + igate_bias).swapaxes(-1, -2)[..., None]
        fg = (gate_in @ fgate_kernel + fgate_bias).swapaxes(-1, -2)[..., None]
        qh = q.reshape(b, s, nh, hd).swapaxes(1, 2)
        kh = k.reshape(b, s, nh, hd).swapaxes(1, 2)
        vh = v.reshape(b, s, nh, hd).swapaxes(1, 2)
        h = jax.vmap(jax.vmap(_mlstm_head))(qh, kh, vh, ig, fg)
        var = jnp.mean(jnp.square(h.astype(jnp.float32)), axis=-1, keepdims=True)
        h = (h * jax.lax.rsqrt(var + 1e-06)).astype(h.dtype) * (1.0 + rms_scale)
        return h.swapaxes(1, 2).reshape(b, s, e)

    def _L0_ffn_ref(x, clip_x, clip_down, w_gate, w_up, w_down):
        import jax, jax.numpy as jnp
        import numpy as np
        QMAX = 127.0

        def _ste_round(v):
            return v + jax.lax.stop_gradient(jnp.round(v) - v)

        def _act_fake_quant(x, clip_factor):
            scale = jax.nn.sigmoid(clip_factor) * jnp.max(jnp.abs(x)) / QMAX
            return jnp.clip(_ste_round(x / scale), -QMAX - 1.0, QMAX) * scale

        def _weight_fake_quant(w):
            scale = jnp.max(jnp.abs(w), axis=1, keepdims=True) / QMAX
            return jnp.clip(_ste_round(w / scale), -QMAX - 1.0, QMAX) * scale
        xq = _act_fake_quant(x, clip_x[0])
        gate = jnp.einsum('bsh,ih->bsi', xq, _weight_fake_quant(w_gate))
        up = jnp.einsum('bsh,ih->bsi', xq, _weight_fake_quant(w_up))
        h = _act_fake_quant(jax.nn.silu(gate) * up, clip_down[0])
        return jnp.einsum('bsi,hi->bsh', h, _weight_fake_quant(w_down))

    def _L1_xattn_ref(values, keys, query, mask, W_out, b_out):
        import jax, jax.numpy as jnp
        import numpy as np
        B, L, E, H = (2, 256, 128, 16)
        D = E // H
        b, l, e = query.shape
        v = values.reshape(b, l, H, D)
        k = keys.reshape(b, l, H, D)
        q = query.reshape(b, l, H, D)
        scores = jnp.einsum('bqhd,bkhd->bhqk', q, k)
        scores = jnp.where(mask == 0, jnp.float32(-1e+20), scores)
        attn = jax.nn.softmax(scores / jnp.float32(E ** 0.5), axis=3)
        out = jnp.einsum('bhqk,bkhd->bqhd', attn, v).reshape(b, l, e)
        out = out @ W_out.T + b_out
        return out

    def _L1_ffn_ref(x, w_gate, w_up, w_down):
        import jax, jax.numpy as jnp
        import numpy as np
        BLOCK = 32
        W_BITS = 4
        ACT_BITS = 16

        def act_qdq(x):
            qmax = 2.0 ** (ACT_BITS - 1) - 1.0
            scale = jnp.maximum(jnp.max(jnp.abs(x)) / qmax, 1e-12)
            return jnp.clip(jnp.round(x / scale), -qmax - 1.0, qmax) * scale

        def fixed_qdq_u16(x):
            scale = 1.0 / 65536.0
            return jnp.clip(jnp.round(x / scale), 0.0, 65535.0) * scale

        def lpbq_dequant(w):
            O, I = w.shape
            qmax = 2.0 ** (W_BITS - 1) - 1.0
            wb = w.reshape(O, I // BLOCK, BLOCK)
            s = jnp.maximum(jnp.max(jnp.abs(wb), axis=-1, keepdims=True) / qmax, 1e-12)
            wq = jnp.clip(jnp.round(wb / s), -qmax - 1.0, qmax) * s
            return wq.reshape(O, I)
        x = act_qdq(x)
        up = act_qdq(x @ lpbq_dequant(w_up).T)
        gate = act_qdq(x @ lpbq_dequant(w_gate).T)
        sig = fixed_qdq_u16(jax.nn.sigmoid(gate))
        gate = act_qdq(gate * sig)
        o = act_qdq(gate * up)
        return o @ lpbq_dequant(w_down).T

    def _L2_xattn_ref(values, keys, query, mask, Wv, Wk, Wq, Wo, bo):
        import jax, jax.numpy as jnp
        import numpy as np
        EMBED_SIZE = 128
        HEADS = 16
        HEAD_DIM = EMBED_SIZE // HEADS
        N, S, E = query.shape
        H, D = (HEADS, HEAD_DIM)
        v = values.reshape(N, S, H, D)
        k = keys.reshape(N, S, H, D)
        q = query.reshape(N, S, H, D)
        v = jnp.einsum('nshd,ed->nshe', v, Wv)
        k = jnp.einsum('nshd,ed->nshe', k, Wk)
        q = jnp.einsum('nshd,ed->nshe', q, Wq)
        energy = jnp.einsum('nqhd,nkhd->nhqk', q, k)
        energy = jnp.where(mask == 0, jnp.asarray(-1e+20, energy.dtype), energy)
        attn = jax.nn.softmax(energy / jnp.sqrt(jnp.asarray(E, energy.dtype)), axis=-1)
        out = jnp.einsum('nhql,nlhd->nqhd', attn, v).reshape(N, S, H * D)
        return out @ Wo.T + bo

    def _L2_ffn_ref(x, Wqkv, q_scale, k_scale, Wo, ln_g, ln_b, W1, b1, W2, b2):
        import jax, jax.numpy as jnp
        import numpy as np
        DIM = 128
        DEPTH = 6
        HEADS = 16
        DIM_HEAD = 64
        WINDOW = 32
        INNER = HEADS * DIM_HEAD
        DIM_INNER = int(DIM * 4 * 2 / 3)
        QK_SCALE = 8.0

        def shift_tokens(t):
            a, s = jnp.split(t, 2, -1)
            s = jnp.pad(s, ((0, 0), (1, 0), (0, 0)))[:, :-1]
            return jnp.concatenate([a, s], -1)

        def l2norm(t):
            return t / jnp.maximum(jnp.linalg.norm(t, axis=-1, keepdims=True), 1e-12)

        def rotate_half(x):
            x1, x2 = jnp.split(x, 2, -1)
            return jnp.concatenate([-x2, x1], -1)

        def rotary_tables(n):
            half = jnp.arange(0, DIM_HEAD, 2, dtype=jnp.float32)
            inv_freq = 1.0 / 10000.0 ** (half / DIM_HEAD)
            t = jnp.arange(n, dtype=jnp.float32)
            freqs = t[:, None] * inv_freq[None, :]
            freqs = jnp.concatenate([freqs, freqs], -1)
            base_scale = (half + 0.4 * DIM_HEAD) / (1.4 * DIM_HEAD)
            power = (t - n // 2) / (WINDOW // 2)
            scale = base_scale[None, :] ** power[:, None]
            scale = jnp.concatenate([scale, scale], -1)
            return (freqs, scale)

        def local_attention(q, k, v):
            b, h, n, d = q.shape
            w = WINDOW
            nw = n // w
            bq = q.reshape(b, h, nw, w, d)
            bk = k.reshape(b, h, nw, w, d)
            bv = v.reshape(b, h, nw, w, d)

            def look(t):
                p = jnp.pad(t, ((0, 0), (0, 0), (1, 0), (0, 0), (0, 0)))
                return jnp.concatenate([p[:, :, :nw], p[:, :, 1:]], axis=3)
            bk2, bv2 = (look(bk), look(bv))
            seq = jnp.arange(n).reshape(nw, w)
            seq_p = jnp.pad(seq, ((1, 0), (0, 0)), constant_values=-1)
            jt = jnp.concatenate([seq_p[:nw], seq_p[1:]], axis=1)
            it = seq[:, :, None]
            jb = jt[:, None, :]
            mask = (it < jb) | (it > jb + w) | (jb == -1)
            sim = jnp.einsum('bhwie,bhwje->bhwij', bq, bk2) * QK_SCALE
            sim = jnp.where(mask, -jnp.finfo(sim.dtype).max, sim)
            attn = jax.nn.softmax(sim, -1)
            out = jnp.einsum('bhwij,bhwje->bhwie', attn, bv2)
            return out.reshape(b, h, n, d)

        def attn_layer(x, Wqkv, qs, ksc, Wo):
            b, n, _ = x.shape
            qkv = x @ Wqkv
            q, k, v = jnp.split(qkv, 3, -1)
            sh = lambda t: t.reshape(b, n, HEADS, DIM_HEAD).transpose(0, 2, 1, 3)
            q, k, v = (sh(q), sh(k), sh(v))
            q = l2norm(q) * qs
            k = l2norm(k) * ksc
            freqs, scale = rotary_tables(n)
            cos, sin = (jnp.cos(freqs), jnp.sin(freqs))
            q = q * cos * scale + rotate_half(q) * sin * scale
            inv = 1.0 / scale
            k = k * cos * inv + rotate_half(k) * sin * inv
            out = local_attention(q, k, v)
            out = out.transpose(0, 2, 1, 3).reshape(b, n, INNER)
            return out @ Wo

        def ffn_layer(x, g, bln, W1, b1, W2, b2):
            mu = x.mean(-1, keepdims=True)
            var = ((x - mu) ** 2).mean(-1, keepdims=True)
            xn = (x - mu) / jnp.sqrt(var + 1e-05) * g + bln
            hg = xn @ W1 + b1
            a, gate = jnp.split(hg, 2, -1)
            return a * jax.nn.gelu(gate, approximate=False) @ W2 + b2
        for i in range(DEPTH):
            x = attn_layer(shift_tokens(x), Wqkv[i], q_scale[i], k_scale[i], Wo[i]) + x
            x = ffn_layer(shift_tokens(x), ln_g[i], ln_b[i], W1[i], b1[i], W2[i], b2[i]) + x
        return x

    def _L3_xattn_ref(q, k, v, mask, wq, bq, wk, bk, wv, bv, wo, bo):
        import jax, jax.numpy as jnp
        import numpy as np
        D_MODEL = 128
        NUM_HEADS = 16
        DEPTH = D_MODEL // NUM_HEADS
        B, S = (4, 256)

        def _split_heads(x):
            b, s, _ = x.shape
            return x.reshape(b, s, NUM_HEADS, DEPTH).transpose(0, 2, 1, 3)
        qh = _split_heads(q @ wq + bq)
        kh = _split_heads(k @ wk + bk)
        vh = _split_heads(v @ wv + bv)
        inv_sqrt_dk = 1.0 / jnp.sqrt(jnp.asarray(DEPTH, jnp.float32))
        logits = jnp.einsum('bhqd,bhkd->bhqk', qh, kh) * inv_sqrt_dk
        logits = logits + mask * -1000000000.0
        attn = jax.nn.softmax(logits, axis=-1)
        out = jnp.einsum('bhqk,bhkd->bhqd', attn, vh)
        out = out.transpose(0, 2, 1, 3).reshape(q.shape[0], -1, D_MODEL)
        return out @ wo + bo

    def _L3_ffn_ref(x, ln1_w, ln1_b, ln2_w, ln2_b, conv_w, attn_w, proj_w, router_w, expert_wv, expert_proj):
        import jax, jax.numpy as jnp
        import numpy as np
        EPS = 1e-05

        def _layernorm(x, w, b):
            mu = jnp.mean(x, axis=-1, keepdims=True)
            var = jnp.mean((x - mu) ** 2, axis=-1, keepdims=True)
            return (x - mu) * jax.lax.rsqrt(var + EPS) * w + b

        def _rope_tables(T, D, base=10000.0):
            inv_freq = 1.0 / base ** (jnp.arange(0, D, 2, dtype=jnp.float32) / D)
            t = jnp.arange(T, dtype=jnp.float32)
            freqs = jnp.einsum('i,j->ij', t, inv_freq)
            emb = jnp.concatenate([freqs, freqs], axis=-1)
            return (jnp.cos(emb), jnp.sin(emb))

        def _rotate_half(x):
            x1, x2 = (x[..., :x.shape[-1] // 2], x[..., x.shape[-1] // 2:])
            return jnp.concatenate([-x2, x1], axis=-1)

        def _attn(x, ln_w, ln_b, conv_w, attn_w, proj_w, n_head):
            B, T, C = x.shape
            D = C // n_head
            h = _layernorm(x, ln_w, ln_b)
            hc = jnp.transpose(h, (0, 2, 1))
            hc = jnp.pad(hc, ((0, 0), (0, 0), (2, 0)))
            hc = jax.lax.conv_general_dilated(hc, conv_w, window_strides=(1,), padding='VALID', dimension_numbers=('NCH', 'OIH', 'NCH'), feature_group_count=C)
            h = jnp.transpose(hc, (0, 2, 1))
            qkv = h @ attn_w
            q, k, v = jnp.split(qkv, 3, axis=-1)
            q = q.reshape(B, T, n_head, D)
            k = k.reshape(B, T, n_head, D)
            v = v.reshape(B, T, n_head, D)
            cos, sin = _rope_tables(T, D)
            cos = cos[None, :, None, :]
            sin = sin[None, :, None, :]
            q = q * cos + _rotate_half(q) * sin
            k = k * cos + _rotate_half(k) * sin
            scores = jnp.einsum('bqhd,bkhd->bhqk', q, k) / jnp.sqrt(jnp.float32(D))
            causal = jnp.tril(jnp.ones((T, T), dtype=bool))
            scores = jnp.where(causal, scores, jnp.float32(-1e+30))
            p = jax.nn.softmax(scores, axis=-1)
            y = jnp.einsum('bhqk,bkhd->bqhd', p, v).reshape(B, T, C)
            return y @ proj_w

        def _moe(x, ln_w, ln_b, router_w, expert_wv, expert_proj):
            h = _layernorm(x, ln_w, ln_b)
            logits = h @ router_w
            expert_idx = jnp.argmax(logits, axis=-1)
            E = router_w.shape[-1]
            out = jnp.zeros_like(x)
            for e in range(E):
                gv = h @ expert_wv[e]
                gate_raw, value = jnp.split(gv, 2, axis=-1)
                y = gate_raw * jax.nn.sigmoid(gate_raw) * value @ expert_proj[e]
                out = out + jnp.where((expert_idx == e)[..., None], y, 0.0)
            return out
        n_head = 16
        x = x + _attn(x, ln1_w, ln1_b, conv_w, attn_w, proj_w, n_head)
        x = x + _moe(x, ln2_w, ln2_b, router_w, expert_wv, expert_proj)
        return x
    x = x + _L0_xattn_ref(_layernorm(x, axis=-1), ctx_1024, ctx_1024, L0_xattn_igate_kernel, L0_xattn_igate_bias, L0_xattn_fgate_kernel, L0_xattn_fgate_bias, L0_xattn_rms_scale)
    x = x + _L0_ffn_ref(_layernorm(x, axis=-1), L0_ffn_clip_x, L0_ffn_clip_down, L0_ffn_w_gate, L0_ffn_w_up, L0_ffn_w_down)
    x = x + _L1_xattn_ref(ctx_1024, ctx_1024, _layernorm(x, axis=-1), mask_Bx1xSxS2_ik1, L1_xattn_W_out, L1_xattn_b_out)
    x = x + _L1_ffn_ref(_layernorm(x, axis=-1), L1_ffn_w_gate, L1_ffn_w_up, L1_ffn_w_down)
    x = x + _L2_xattn_ref(ctx_1024, ctx_1024, _layernorm(x, axis=-1), mask_Bx1x1xS2_if1, L2_xattn_Wv, L2_xattn_Wk, L2_xattn_Wq, L2_xattn_Wo, L2_xattn_bo)
    x = x + _L2_ffn_ref(_layernorm(x, axis=-1), L2_ffn_Wqkv, L2_ffn_q_scale, L2_ffn_k_scale, L2_ffn_Wo, L2_ffn_ln_g, L2_ffn_ln_b, L2_ffn_W1, L2_ffn_b1, L2_ffn_W2, L2_ffn_b2)
    x = x + _L3_xattn_ref(_layernorm(x, axis=-1), ctx_1024, ctx_1024, mask_1x1xSxS2_fk1, L3_xattn_wq, L3_xattn_bq, L3_xattn_wk, L3_xattn_bk, L3_xattn_wv, L3_xattn_bv, L3_xattn_wo, L3_xattn_bo)
    x = x + _L3_ffn_ref(_layernorm(x, axis=-1), L3_ffn_ln1_w, L3_ffn_ln1_b, L3_ffn_ln2_w, L3_ffn_ln2_b, L3_ffn_conv_w, L3_ffn_attn_w, L3_ffn_proj_w, L3_ffn_router_w, L3_ffn_expert_wv, L3_ffn_expert_proj)
    return x

_drawn_inputs = setup_inputs


def setup_inputs(seed=0):
    import zlib

    import numpy as np

    out = dict(_drawn_inputs(seed))
    spreads = {'L2_xattn_bo': (0.0, 0.1),
     'L2_ffn_q_scale': (1.0, 0.6),
     'L2_ffn_k_scale': (1.0, 0.6),
     'L2_ffn_ln_g': (1.0, 0.6),
     'L2_ffn_ln_b': (0.0, 0.8),
     'L2_ffn_b1': (0.0, 0.8),
     'L2_ffn_b2': (0.0, 0.1),
     'L3_xattn_bq': (0.0, 0.8),
     'L3_xattn_bk': (0.0, 0.8),
     'L3_xattn_bv': (0.0, 0.1),
     'L3_xattn_bo': (0.0, 0.1),
     'L3_ffn_ln1_w': (1.0, 0.6),
     'L3_ffn_ln1_b': (0.0, 0.8),
     'L3_ffn_ln2_w': (1.0, 0.6),
     'L3_ffn_ln2_b': (0.0, 0.8)}
    factors = {'L0_xattn_igate_bias': 8.0,
     'L0_xattn_fgate_kernel': 3.108,
     'L0_xattn_rms_scale': 4.239,
     'L0_ffn_w_gate': 8.0,
     'L0_ffn_w_up': 8.0,
     'L0_ffn_w_down': 8.0,
     'L1_xattn_b_out': 4.386,
     'L1_ffn_w_gate': 8.0,
     'L1_ffn_w_up': 8.0,
     'L1_ffn_w_down': 8.0,
     'L2_ffn_W1': 5.19,
     'L2_ffn_W2': 5.118,
     'L3_ffn_conv_w': 8.0,
     'L3_ffn_attn_w': 8.0,
     'L3_ffn_proj_w': 8.0,
     'L3_ffn_router_w': 8.0,
     'L3_ffn_expert_wv': 8.0,
     'L3_ffn_expert_proj': 8.0}
    for name, (base, spread) in spreads.items():
        noise = np.random.default_rng([zlib.crc32(name.encode()), seed]).standard_normal(out[name].shape)
        drawn = base * np.exp(spread * noise) if base else spread * noise
        out[name] = jnp.asarray(drawn.astype(out[name].dtype))
    for name, factor in factors.items():
        out[name] = (out[name] * factor).astype(out[name].dtype)
    return out
```

```python
from contextlib import ExitStack

import numpy as np

import concourse.bass as bass
from concourse import mybir

ALU = mybir.AluOpType
ACT = mybir.ActivationFunctionType
F32 = mybir.dt.float32
BF16 = mybir.dt.bfloat16
I32 = mybir.dt.int32
AX = mybir.AxisListType

P = 128
B, S, E = 8, 256, 128
TOK = B * S
NT = TOK // P
CH = 512
NCH = TOK // CH
LN_EPS = 1e-5


class Steps:

    def __init__(self, eng, sem, base=0):
        self.eng, self.sem, self.base, self.n = eng, sem, base, 0

    def then(self, ins):
        self.n += 1
        ins.then_inc(self.sem, 1)
        self.eng.wait_ge(self.sem, self.base + self.n)


class Core:
    pass


def sbuf(nc, stack):
    return lambda name, shape, dt=F32: stack.enter_context(nc.sbuf_tensor(f"{name}_{nc.next_id()}", shape, dt))


def run_stage(nc, names, body):
    with ExitStack() as ctx:
        handles = [ctx.enter_context(nc.semaphore(f"{n}_{nc.next_id()}")) for n in names]
        body(*handles)
        nums = sorted(h.num for h in handles)
        first = nums[0]
        for n, after in zip(nums, nums[1:] + [None]):
            if after != n + 1:
                nc.gpsimd.sem_clear(range(first, n + 1))
                first = after
        nc.all_engine_barrier()


def load_inputs(nc, C):
    def body(loaded, turned, kept):
        with nc.sbuf_tensor("x_rows", [P, NT, E], F32) as x_rows, nc.Block() as block:
            @block.sync
            def _(sp):
                sp.dma_start(C.ident[:, :], C.c["ident"]).then_inc(loaded, 16)
                sp.dma_start(C.identb[:, :], C.c["identb"]).then_inc(loaded, 16)
                sp.dma_start(x_rows[:, :, :], C.i["x"].rearrange("b (h p) d -> p (b h) d", p=P)).then_inc(loaded, 16)
                sp.dma_start(C.CN[:, :, :], C.i["ctx_1024"].rearrange("b (h p) d -> p (b h) d", p=P)).then_inc(loaded, 16)

            @block.tensor
            def _(pe):
                pe.wait_ge(loaded, 64)
                for n, src in enumerate((x_rows, C.CN)):
                    for t in range(NT):
                        last = nc.tensor.transpose(C.ps[n * 4 + t // 4][:, (t % 4) * P:(t % 4 + 1) * P], src[:, t, :], C.ident[:, :])
                        if t % 4 == 3:
                            last.then_inc(turned, 1)

            @block.vector
            def _(dve):
                nc.vector.memset(C.mean_w[:, :], 1.0 / E)
                nc.vector.memset(C.eps[:, :], LN_EPS)
                nc.vector.memset(C.one[:, :], 1.0)
                for q in range(8):
                    dve.wait_ge(turned, q + 1)
                    dst = C.XT if q < 4 else C.CT
                    nc.vector.tensor_copy(dst[:, (q % 4) * CH:(q % 4 + 1) * CH], C.ps[q][:, :]).then_inc(kept, 1)
    run_stage(nc, ["loaded", "turned", "kept"], body)


def layer_norm(nc, C, HT, gain=None, shift=None, src=None):
    src = C.XT if src is None else src

    def body(mean_ready, centred, squared, var_ready, root_ready, normed, own, act_own):
        with ExitStack() as s:
            sb = sbuf(nc, s)
            xc = sb("xc", [P, 2, CH])
            sq = sb("sq", [P, 2, CH])
            y = sb("y", [P, 2, CH])
            y2 = sb("y2", [P, 2, CH])
            ln = sb("ln", [P, 2, CH])
            tt = sb("tt", [P, 2, CH])
            block = s.enter_context(nc.Block())

            @block.tensor
            def _(pe):
                with pe.Fori(0, NCH // 2) as i:
                    for p in range(2):
                        nc.tensor.matmul(C.ps[p][:, :], C.mean_w[:, :], src[:, bass.ds(i * (2 * CH) + p * CH, CH)], start=True, stop=True).then_inc(mean_ready, 1)
                    for p in range(2):
                        pe.wait_ge(squared, i * 2 + (p + 1))
                        nc.tensor.matmul(C.ps[2 + p][:, :], C.mean_w[:, :], sq[:, p, :], start=True, stop=True).then_inc(var_ready, 1)
                    pe.wait_ge(normed, i * 2 + 2)

            @block.vector
            def _(dve):
                with dve.Fori(0, NCH // 2) as i:
                    for p in range(2):
                        dve.wait_ge(mean_ready, i * 2 + (p + 1))
                        nc.vector.tensor_tensor(xc[:, p, :], src[:, bass.ds(i * (2 * CH) + p * CH, CH)], C.ps[p][:, :], ALU.subtract).then_inc(centred, 1)
                    st = Steps(dve, own, i * (10 if gain is not None else 8))
                    for p in range(2):
                        dve.wait_ge(root_ready, i * 2 + (p + 1))
                        st.then(nc.vector.scalar_tensor_tensor(tt[:, p, :], C.ps[2 + p][:, :], LN_EPS, y2[:, p, :], ALU.add, ALU.mult))
                        st.then(nc.vector.tensor_scalar(tt[:, p, :], tt[:, p, :], -0.5, 0.5, ALU.mult, ALU.add))
                        st.then(nc.vector.tensor_tensor(xc[:, p, :], xc[:, p, :], y[:, p, :], ALU.mult))
                        st.then(nc.vector.tensor_tensor(tt[:, p, :], xc[:, p, :], tt[:, p, :], ALU.mult))
                        out = HT[:, bass.ds(i * (2 * CH) + p * CH, CH)]
                        if gain is None:
                            nc.vector.tensor_tensor(out, xc[:, p, :], tt[:, p, :], ALU.add).then_inc(normed, 1)
                        else:
                            st.then(nc.vector.tensor_tensor(xc[:, p, :], xc[:, p, :], tt[:, p, :], ALU.add))
                            nc.vector.tensor_scalar(out, xc[:, p, :], gain, shift, ALU.mult, ALU.add).then_inc(normed, 1)

            @block.scalar
            def _(act):
                nc.scalar.preload_act_table_set(LN_EXP)
                with act.Fori(0, NCH // 2) as i:
                    for p in range(2):
                        act.wait_ge(centred, i * 2 + (p + 1))
                        nc.scalar.activation(sq[:, p, :], xc[:, p, :], ACT.Square).then_inc(squared, 1)
                    st = Steps(act, act_own, i * 4)
                    for p in range(2):
                        act.wait_ge(var_ready, i * 2 + (p + 1))
                        st.then(nc.scalar.activation(ln[:, p, :], C.ps[2 + p][:, :], ACT.Ln, bias=C.eps[:, :]))
                        st.then(nc.scalar.activation(y[:, p, :], ln[:, p, :], ACT.Exp, scale=-0.5))
                        nc.scalar.activation(y2[:, p, :], y[:, p, :], ACT.Square).then_inc(root_ready, 1)
    run_stage(nc, ["mean_ready", "centred", "squared", "var_ready", "root_ready", "normed", "own", "act_own"], body)


def store_output(nc, C, src):
    def body(turned, kept, stored):
        with nc.sbuf_tensor("y_rows", [P, NT, E], F32) as y_rows, nc.Block() as block:
            @block.tensor
            def _(pe):
                for t in range(NT):
                    last = nc.tensor.transpose(C.ps[t // 4][:, (t % 4) * P:(t % 4 + 1) * P], src[:, t * P:(t + 1) * P], C.ident[:, :])
                    if t % 4 == 3:
                        last.then_inc(turned, 1)

            @block.vector
            def _(dve):
                for q in range(4):
                    dve.wait_ge(turned, q + 1)
                    nc.vector.tensor_copy(y_rows[:, 4 * q:4 * q + 4, :], C.ps[q][:, :].rearrange("p (t d) -> p t d", t=4)).then_inc(kept, 1)

            @block.sync
            def _(sp):
                rows = C.out.rearrange("b (h p) d -> p (b h) d", p=P)
                for q in range(4):
                    sp.wait_ge(kept, q + 1)
                    sp.dma_start(rows[:, 4 * q:4 * q + 4, :], y_rows[:, 4 * q:4 * q + 4, :]).then_inc(stored, 16)
                sp.wait_ge(stored, 64)
    run_stage(nc, ["turned", "kept", "stored"], body)


L0_NH = 4
L0_HD = E // L0_NH
NEG = -1e30
MAGIC = 12582912.0
LOG2E = float(1.0 / np.log(2.0))
LN2_HI = 0.693145751953125
LN2_LO = float(np.log(2.0) - LN2_HI)
EXP1 = 2.0 ** 23


def split_exponent(nc, st, x, n, r):
    st.then(nc.vector.tensor_scalar(n, x, LOG2E, MAGIC, ALU.mult, ALU.add))
    st.then(nc.vector.tensor_scalar(n, n, MAGIC, None, ALU.subtract))
    st.then(nc.vector.scalar_tensor_tensor(r, n, -LN2_HI, x, ALU.mult, ALU.add))
    st.then(nc.vector.scalar_tensor_tensor(r, n, -LN2_LO, r, ALU.mult, ALU.add))


def eighth_power(nc, st, e):
    st.then(nc.vector.tensor_tensor(e, e, e, ALU.mult))
    st.then(nc.vector.tensor_tensor(e, e, e, ALU.mult))
    st.then(nc.vector.tensor_tensor(e, e, e, ALU.mult))

LN_EXP = "natural_log_exp_and_others"


def mlstm_gates(nc, C, G):
    def body(loaded, projected, u_split, exp_ready, own, w_ready, softplus_ready, lf_ready, lf_turned, cs_ready, cs_turned, M_ready, M_turned, m_ready, floor_ready):
        with ExitStack() as s:
            sb = sbuf(nc, s)
            gk = sb("gk", [P, 3, 2 * L0_NH])
            gb = sb("gb", [P, 2 * L0_NH])
            gate = sb("gate", [P, NT, 2 * L0_NH])
            ig, u, z, w, lw, lf, cs, m, n, r, ez = (sb(k, [P, NT, L0_NH]) for k in ("ig", "u", "z", "w", "lw", "log_f", "csum", "m", "n", "r", "ez"))
            a_col = sb("a_col", [P, NT * L0_NH])
            n2, r2, n3, r3 = (sb(k, [P, NT * L0_NH]) for k in ("n_a", "r_a", "n_M", "r_M"))
            pow2 = sb("pow2", [P, NT * L0_NH], I32)
            q_a = sb("q_a", [P, NT * L0_NH])
            ones = sb("ones", [L0_NH, TOK])
            rows_cs, rows_a = sb("rows_cs", [L0_NH, TOK]), sb("rows_a", [L0_NH, TOK])
            rows_M = sb("rows_M", [L0_NH, TOK])
            block = s.enter_context(nc.Block())
            flat = lambda t: t[:, :, :].rearrange("p t h -> p (t h)")
            bankG, bankC, bankM = C.ps[0], C.ps[1], C.ps[6]
            bankR = C.psum[0:L0_NH, 2:6, :].rearrange("p k c -> p (k c)")
            GV = bankG[:, 0:NT * 2 * L0_NH].rearrange("p (t g) -> p t g", t=NT)

            @block.sync
            def _(sp):
                for k, g in enumerate(("i", "f")):
                    h = slice(k * L0_NH, (k + 1) * L0_NH)
                    sp.dma_start(gk[:, :, h], C.i[f"L0_xattn_{g}gate_kernel"].rearrange("(c p) h -> p c h", p=P)).then_inc(loaded, 16)
                    sp.dma_start(gb[:, h], C.i[f"L0_xattn_{g}gate_bias"].unsqueeze(0).to_broadcast([P, L0_NH])).then_inc(loaded, 16)

            @block.tensor
            def _(pe):
                pe.wait_ge(loaded, 64)
                for t in range(NT):
                    for k, src in enumerate((C.HT, C.CT, C.CT)):
                        last = nc.tensor.matmul(GV[:, t, :], src[:, t * P:(t + 1) * P], gk[:, k, :], start=(k == 0), stop=(k == 2))
                last.then_inc(projected, 1)
                pe.wait_ge(lf_ready, 1)
                for t in range(NT):
                    last = nc.tensor.transpose(bankR[:, t * P:(t + 1) * P], lf[:, t, :], C.ident[:, :])
                last.then_inc(lf_turned, 1)
                pe.wait_ge(cs_ready, 1)
                for t in range(NT):
                    nc.tensor.transpose(bankR[:, t * P:(t + 1) * P], ig[:, t, :], C.ident[:, :])
                    last = nc.tensor.transpose(bankC[:, t * L0_NH:(t + 1) * L0_NH], rows_cs[:, t * P:(t + 1) * P], C.ident[0:L0_NH, 0:L0_NH])
                last.then_inc(cs_turned, 1)
                pe.wait_ge(M_ready, 1)
                for t in range(NT):
                    last = nc.tensor.transpose(bankM[:, t * L0_NH:(t + 1) * L0_NH], rows_M[:, t * P:(t + 1) * P], C.ident[0:L0_NH, 0:L0_NH])
                last.then_inc(M_turned, 1)

            @block.scalar
            def _(act):
                nc.scalar.preload_act_table_set(LN_EXP)
                act.wait_ge(u_split, 1)
                nc.scalar.activation(flat(ez), flat(r), ACT.Exp, scale=0.125).then_inc(exp_ready, 1)
                act.wait_ge(w_ready, 1)
                nc.scalar.activation(flat(lw), flat(w), ACT.Ln).then_inc(softplus_ready, 1)
                act.wait_ge(m_ready, 1)
                nc.scalar.activation(G.em_col[:, :], flat(m), ACT.Exp, scale=-1.0)
                nc.scalar.activation(G.key_factor[:, :], r2[:, :], ACT.Exp, scale=0.125)
                nc.scalar.activation(G.query_factor[:, :], r3[:, :], ACT.Exp, scale=-0.125).then_inc(floor_ready, 1)

            @block.vector
            def _(dve):
                st = Steps(dve, own)
                nc.vector.memset(ones[:, :], 1.0)
                dve.wait_ge(projected, 1)
                nc.vector.tensor_tensor(ig[:, :, :], GV[:, :, 0:L0_NH], gb[:, 0:L0_NH].unsqueeze(1).to_broadcast([P, NT, L0_NH]), ALU.add)
                st.then(nc.vector.tensor_tensor(gate[:, :, :], GV, gb[:, :].unsqueeze(1).to_broadcast([P, NT, 2 * L0_NH]), ALU.add))
                f = gate[:, :, L0_NH:2 * L0_NH]
                st.then(nc.vector.tensor_scalar(u[:, :, :], f, -1.0, None, ALU.mult))
                st.then(nc.vector.tensor_tensor(u[:, :, :], u[:, :, :], f, ALU.min))
                st.then(nc.vector.tensor_scalar(u[:, :, :], u[:, :, :], -80.0, None, ALU.max))
                split_exponent(nc, st, flat(u), flat(n), flat(r))
                nc.vector.tensor_scalar(pow2[:, :], flat(n), 127.0, EXP1, ALU.add, ALU.mult).then_inc(u_split, 1)
                dve.wait_ge(exp_ready, 1)
                dve.wait_ge(u_split, 1)
                eighth_power(nc, st, flat(ez))
                st.then(nc.vector.tensor_tensor(flat(z), flat(ez), pow2[:, :].bitcast(F32), ALU.mult))
                nc.vector.tensor_scalar(flat(w), flat(z), 1.0, None, ALU.add).then_inc(w_ready, 1)
                dve.wait_ge(w_ready, 1)
                st.then(nc.vector.scalar_tensor_tensor(flat(z), flat(w), 1.0, flat(z), ALU.subtract, ALU.subtract))
                st.then(nc.vector.reciprocal(flat(r), flat(w)))
                st.then(nc.vector.tensor_tensor(flat(z), flat(z), flat(r), ALU.mult))
                dve.wait_ge(softplus_ready, 1)
                st.then(nc.vector.tensor_tensor(flat(z), flat(lw), flat(z), ALU.subtract))
                nc.vector.scalar_tensor_tensor(lf[:, :, :], f, 0.0, z[:, :, :], ALU.min, ALU.subtract).then_inc(lf_ready, 1)
                dve.wait_ge(lf_turned, 1)
                st.then(nc.vector.tensor_copy(rows_a[:, :], bankR))
                for b in range(B):
                    c = slice(b * S, (b + 1) * S)
                    last = nc.vector.tensor_tensor_scan(rows_cs[:, c], ones[:, c], rows_a[:, c], 0.0, ALU.mult, ALU.add)
                last.then_inc(cs_ready, 1)
                dve.wait_ge(cs_turned, 1)
                nc.vector.tensor_tensor(rows_a[:, :], bankR, rows_cs[:, :], ALU.subtract)
                st.then(nc.vector.tensor_copy(flat(cs), bankC[:, 0:NT * L0_NH]))
                st.then(nc.vector.tensor_tensor(a_col[:, :], flat(ig), flat(cs), ALU.subtract))
                st.then(nc.vector.tensor_scalar(n2[:, :], a_col[:, :], LOG2E, MAGIC, ALU.mult, ALU.add))
                st.then(nc.vector.tensor_scalar(n2[:, :], n2[:, :], MAGIC, None, ALU.subtract))
                st.then(nc.vector.scalar_tensor_tensor(q_a[:, :], n2[:, :], LN2_HI, flat(cs), ALU.mult, ALU.add))
                st.then(nc.vector.tensor_tensor(r2[:, :], flat(ig), q_a[:, :], ALU.subtract))
                st.then(nc.vector.scalar_tensor_tensor(r2[:, :], n2[:, :], -LN2_LO, r2[:, :], ALU.mult, ALU.add))
                nc.vector.tensor_scalar(G.key_exponent[:, :], n2[:, :], 127.0, EXP1, ALU.add, ALU.mult)
                for b in range(B):
                    c = slice(b * S, (b + 1) * S)
                    last = nc.vector.tensor_tensor_scan(rows_M[:, c], rows_a[:, c], rows_a[:, c], -3e38, ALU.max, ALU.max)
                last.then_inc(M_ready, 1)
                dve.wait_ge(M_ready, 1)
                st.then(nc.vector.tensor_scalar(G.query_exponent[:, :], rows_M[:, :], LOG2E, MAGIC, ALU.mult, ALU.add))
                st.then(nc.vector.tensor_scalar(G.query_exponent[:, :], G.query_exponent[:, :], MAGIC, -EXP1, ALU.subtract, ALU.mult))
                dve.wait_ge(M_turned, 1)
                st.then(nc.vector.tensor_copy(z[:, :, :].rearrange("p t h -> p (t h)"), bankM[:, 0:NT * L0_NH]))
                split_exponent(nc, st, flat(z), n3[:, :], r3[:, :])
                nc.vector.tensor_tensor(flat(m), flat(cs), flat(z), ALU.add).then_inc(m_ready, 1)
                dve.wait_ge(floor_ready, 1)
                eighth_power(nc, st, G.key_factor[:, :])
                eighth_power(nc, st, G.query_factor[:, :])
    run_stage(nc, ["loaded", "projected", "u_split", "exp_ready", "own", "w_ready", "softplus_ready", "lf_ready", "lf_turned", "cs_ready", "cs_turned", "M_ready", "M_turned", "m_ready",
                   "floor_ready"], body)


def mlstm_heads(nc, C, G):
    NH, HD = L0_NH, L0_HD
    DS = 12
    def body(loaded, staged, d_ready, s_ready, d_made, c_ready, pv_ready, ln_ready, root_ready, o_ready, o_turned, added, own, act_own):
        with ExitStack() as s:
            sb = sbuf(nc, s)
            maskb = sb("maskb", [P, P], BF16)
            sel = sb("sel", [NH, NH, P])
            rms = sb("rms", [P, 1])
            ab = sb("ab", [P, 8])
            qs, ks = sb("qs", [P, S]), sb("ks", [P, S])
            ms = sb("ms", [NH, S])
            VA = sb("VA", [P, 2, NH, HD + 1])
            dm = sb("dm", [P, NH, 384], I32)
            cT = sb("cT", [P, NH, 384])
            nrm, ssq, v0, y, y2, t2 = (sb(n, [P, 8]) for n in ("nrm", "ssq", "v0", "y8", "y28", "t28"))
            o, osq = sb("o", [P, 2, NH, HD]), sb("osq", [P, 2, NH, HD])
            block = s.enter_context(nc.Block())
            bankD, bankS, bankO, bankT = C.ps[0:2], C.ps[2:4], C.ps[4], C.ps[5]

            @block.sync
            def _(sp):
                sp.dma_start(maskb[:, :], C.c["causal_kq"]).then_inc(loaded, 16)
                sp.dma_start(sel[:, :, :], C.c["head_rows"]).then_inc(loaded, 16)
                for h in range(NH):
                    sp.dma_start(rms[h * HD:(h + 1) * HD, :], C.i["L0_xattn_rms_scale"].unsqueeze(1)).then_inc(loaded, 16)

            @block.tensor
            def _(pe):
                pe.wait_ge(loaded, 16 * 6)
                with pe.Fori(0, B) as b:
                    def values(h):
                        pe.wait_ge(c_ready, b * NH + (h + 1))
                        nc.tensor.matmul(bankO[:, h * 33:(h + 1) * 33], cT[:, h, 0:P], VA[:, 0, h, :], start=True, stop=True, skip_group_check=True)
                        nc.tensor.matmul(bankO[:, (4 + h) * 33:(5 + h) * 33], cT[:, h, P:2 * P], VA[:, 0, h, :], start=True, stop=False, skip_group_check=True)
                        return nc.tensor.matmul(bankO[:, (4 + h) * 33:(5 + h) * 33], cT[:, h, 2 * P:3 * P], VA[:, 1, h, :], start=False, stop=True, skip_group_check=True)
                    pe.wait_ge(staged, b * 4 + 4)
                    for h in range(NH):
                        g = slice(32 * h, 32 * h + 32)
                        if h >= 2:
                            pe.wait_ge(d_made, b * NH + (h - 1))
                        D = bankD[h % 2]
                        nc.tensor.matmul(D[:, 0:S], sel[:, h, :], ms[:, :], start=True, stop=False, skip_group_check=True)
                        nc.tensor.matmul(D[:, S:S + P], sel[:, h, :], ms[:, P:S], start=False, stop=False, skip_group_check=True)
                        nc.tensor.matmul(D[:, 0:P], C.identb[:, :], maskb[:, :], start=False, stop=False, skip_group_check=True)
                        nc.tensor.matmul(D[:, S:S + P], C.identb[:, :], maskb[:, :], start=False, stop=True, skip_group_check=True).then_inc(d_ready, 1)
                        if h >= 2:
                            pe.wait_ge(c_ready, b * NH + (h - 1))
                        Z = bankS[h % 2]
                        nc.tensor.matmul(Z[:, 0:S], ks[g, 0:P], qs[g, :], start=True, stop=True, skip_group_check=True)
                        nc.tensor.matmul(Z[:, S:S + P], ks[g, P:S], qs[g, P:S], start=True, stop=True, skip_group_check=True).then_inc(s_ready, 1)
                        if h >= 1:
                            values(h - 1)
                    values(NH - 1).then_inc(pv_ready, 1)
                    pe.wait_ge(o_ready, b + 1)
                    for t in range(2):
                        last = nc.tensor.transpose(bankT[:, t * P:(t + 1) * P], o[:, t, :, :].rearrange("p h d -> p (h d)"), C.ident[:, :])
                    last.then_inc(o_turned, 1)

            @block.scalar
            def _(act):
                nc.scalar.preload_act_table_set(LN_EXP)
                with act.Fori(0, B) as b:
                    act.wait_ge(ln_ready, b + 1)
                    st = Steps(act, act_own, b * 2)
                    st.then(nc.scalar.activation(y2[:, :], v0[:, :], ACT.Ln))
                    st.then(nc.scalar.activation(y[:, :], y2[:, :], ACT.Exp, scale=-0.5))
                    nc.scalar.activation(y2[:, :], y[:, :], ACT.Square).then_inc(root_ready, 1)

            @block.vector
            def _(dve):
                dve.wait_ge(loaded, 16 * 6)
                st0 = Steps(dve, own)
                st0.then(nc.vector.tensor_scalar(rms[:, :], rms[:, :], 1.0, None, ALU.add))
                with dve.Fori(0, B) as b:
                    nc.vector.tensor_copy(ms[:, :], G.query_exponent[:, bass.ds(b * S, S)]).then_inc(staged, 1)
                    nc.vector.tensor_copy(qs[:, :], C.HT[:, bass.ds(b * S, S)]).then_inc(staged, 1)
                    nc.vector.tensor_scalar(ks[:, :], C.CT[:, bass.ds(b * S, S)], float(HD) ** -0.5, None, ALU.mult).then_inc(staged, 1)
                    nc.vector.tensor_copy(ab[:, :], G.key_exponent[:, bass.ds(b * 8, 8)])
                    kf = G.key_factor[:, bass.ds(b * 8, 8)]
                    nc.vector.tensor_copy(VA[:, :, :, HD].rearrange("p t h -> p (t h)"), kf)
                    nc.vector.tensor_tensor(VA[:, :, :, 0:HD].rearrange("p t h d -> p (t h) d"), C.CN[:, bass.ds(b * 2, 2), :].rearrange("p t (h d) -> p (t h) d", h=NH), kf.unsqueeze(2).to_broadcast([P, 8, HD]), ALU.mult).then_inc(staged, 1)
                    for h in range(NH):
                        dve.wait_ge(d_ready, b * NH + (h + 1))
                        nc.vector.tensor_scalar(dm[:, h, 0:S], bankD[h % 2][:, 0:S], ab[:, h:h + 1], 0.0, ALU.add, ALU.max)
                        nc.vector.tensor_scalar(dm[:, h, S:S + P], bankD[h % 2][:, S:S + P], ab[:, 4 + h:5 + h], 0.0, ALU.add, ALU.max).then_inc(d_made, 1)
                        dve.wait_ge(d_made, b * NH + (h + 1))
                        dve.wait_ge(s_ready, b * NH + (h + 1))
                        nc.vector.tensor_tensor(cT[:, h, :], bankS[h % 2][:, 0:384], dm[:, h, :].bitcast(F32), ALU.mult).then_inc(c_ready, 1)
                    dve.wait_ge(pv_ready, b + 1)
                    st = Steps(dve, own, b * DS + 1)
                    O = bankO[:, 0:8 * 33].rearrange("p (t h e) -> p t h e", t=2, h=NH)
                    qf = G.query_factor[:, bass.ds(b * 8, 8)]
                    st.then(nc.vector.tensor_tensor(nrm[:, :].rearrange("p (t h) -> p t h", t=2), O[:, :, :, HD], qf.rearrange("p (t h) -> p t h", t=2), ALU.mult))
                    st.then(nc.vector.tensor_tensor(nrm[:, :], nrm[:, :], G.em_col[:, bass.ds(b * 8, 8)], ALU.max))
                    st.then(nc.vector.tensor_scalar(nrm[:, :], nrm[:, :], 1e-6, None, ALU.add))
                    st.then(nc.vector.reciprocal(nrm[:, :], nrm[:, :]))
                    st.then(nc.vector.tensor_tensor(nrm[:, :], nrm[:, :], qf, ALU.mult))
                    st.then(nc.vector.tensor_tensor(o[:, :, :, :].rearrange("p t h d -> p (t h) d"), O[:, :, :, 0:HD].rearrange("p t h d -> p (t h) d"), nrm[:, :].unsqueeze(2).to_broadcast([P, 8, HD]), ALU.mult))
                    st.then(nc.vector.tensor_tensor(osq[:, :, :, :], o[:, :, :, :], o[:, :, :, :], ALU.mult))
                    st.then(nc.vector.tensor_reduce(ssq[:, :], osq[:, :, :, :].rearrange("p t h d -> p (t h) d"), AX.X, ALU.add))
                    nc.vector.tensor_scalar(v0[:, :], ssq[:, :], 1.0 / HD, 1e-6, ALU.mult, ALU.add).then_inc(ln_ready, 1)
                    dve.wait_ge(root_ready, b + 1)
                    dve.wait_ge(ln_ready, b + 1)
                    st.then(nc.vector.tensor_tensor(t2[:, :], v0[:, :], y2[:, :], ALU.mult))
                    st.then(nc.vector.tensor_scalar(t2[:, :], t2[:, :], -0.5, 0.5, ALU.mult, ALU.add))
                    st.then(nc.vector.tensor_tensor(t2[:, :], t2[:, :], y[:, :], ALU.mult))
                    st.then(nc.vector.tensor_tensor(t2[:, :], t2[:, :], y[:, :], ALU.add))
                    nc.vector.tensor_tensor(o[:, :, :, :].rearrange("p t h d -> p (t h) d"), o[:, :, :, :].rearrange("p t h d -> p (t h) d"), t2[:, :].unsqueeze(2).to_broadcast([P, 8, HD]), ALU.mult).then_inc(o_ready, 1)
                    dve.wait_ge(o_turned, b + 1)
                    xs = C.XT[:, bass.ds(b * S, S)]
                    nc.vector.scalar_tensor_tensor(xs, bankT[:, 0:S], rms[:, :], xs, ALU.mult, ALU.add).then_inc(added, 1)
                    assert st.n == DS, st.n
    run_stage(nc, ["loaded", "staged", "d_ready", "s_ready", "d_made", "c_ready", "pv_ready", "ln_ready", "root_ready", "o_ready", "o_turned", "added", "own", "act_own"], body)


def l0_xattn(nc, C):
    layer_norm(nc, C, C.HT)
    G = Core()
    with ExitStack() as s:
        sb = sbuf(nc, s)
        G.query_exponent = sb("query_exponent", [L0_NH, TOK])
        G.em_col, G.key_factor, G.query_factor, G.key_exponent = (sb(n, [P, NT * L0_NH]) for n in ("em_col", "key_factor", "query_factor", "key_exponent"))
        mlstm_gates(nc, C, G)
        mlstm_heads(nc, C, G)




def over(nc, st, x, t, d, k):
    st.then(nc.vector.tensor_scalar(t, x, 1.0 / k, None, ALU.mult))
    st.then(nc.vector.scalar_tensor_tensor(d, t, -(k + 1.0), x, ALU.mult, ALU.add))
    st.then(nc.vector.tensor_tensor(d, d, t, ALU.add))
    st.then(nc.vector.scalar_tensor_tensor(t, d, 1.0 / k, t, ALU.mult, ALU.add))

RMAX = bass.bass_isa.ReduceOp.max
L0_I = 352
L0_IT = [(0, 128), (128, 128), (256, 96)]


def l0_ffn_weights(nc, C, F):
    WEIGHTS_DONE = 26

    def body(loaded, spread, sig_ready, turned, own):
        with ExitStack() as s:
            sb = sbuf(nc, s)
            wr = sb("wr", [P, 2, 3, E])
            wd = sb("wd", [P, L0_I])
            wi = sb("wi", [P, 2, 3, E], BF16)
            wdi = sb("wdi", [P, L0_I], BF16)
            tmp = sb("tmp", [P, 2, 3, E])
            nclip, nn, rc, ez = (sb(k, [P, 2]) for k in ("neg_clip", "n_clip", "r_clip", "exp_clip"))
            pow2 = sb("pow2_clip", [P, 2], I32)
            rem, t127 = sb("rem", [P, 8]), sb("t127", [P, 8])
            inv, invd, mx, am = sb("inv", [P, 2, 3]), sb("invd", [P, 1]), sb("mx", [P, 1]), sb("am", [P, 1])
            block = s.enter_context(nc.Block())

            @block.sync
            def _(sp):
                for n, name in enumerate(("gate", "up")):
                    w = C.i[f"L0_ffn_w_{name}"]
                    sp.dma_start(wr[:, n, 0:2, :], w[0:256, :].rearrange("(t p) h -> p t h", p=P)).then_inc(loaded, 16)
                    sp.dma_start(wr[0:96, n, 2, :], w[256:L0_I, :]).then_inc(loaded, 16)
                    sp.dma_start(wr[96:P, n, 2, :], w[0:32, :]).then_inc(loaded, 16)
                sp.dma_start(wd[:, :], C.i["L0_ffn_w_down"]).then_inc(loaded, 16)
                for n, name in enumerate(("x", "down")):
                    sp.dma_start(F.clip[:, n:n + 1], C.i[f"L0_ffn_clip_{name}"].unsqueeze(0).to_broadcast([P, 1])).then_inc(loaded, 16)

            @block.scalar
            def _(act):
                act.wait_ge(own, 5)
                nc.scalar.activation(ez[:, :], rc[:, :], ACT.Exp, scale=0.125).then_inc(sig_ready, 1)

            @block.gpsimd
            def _(pool):
                pool.wait_ge(own, 6)
                nc.gpsimd.partition_all_reduce(am[:, :], mx[:, :], P, RMAX).then_inc(spread, 1)

            @block.vector
            def _(dve):
                st = Steps(dve, own)
                dve.wait_ge(loaded, 16 * 9)
                st.then(nc.vector.tensor_scalar(nclip[:, :], F.clip[:, :], -1.0, 80.0, ALU.mult, ALU.min))
                split_exponent(nc, st, nclip[:, :], nn[:, :], rc[:, :])
                st.then(nc.vector.tensor_reduce(mx[:, :], C.HT[:, :], AX.X, ALU.max, apply_absolute_value=True))
                st.then(nc.vector.tensor_reduce(F.sw[:, :, :], wr[:, :, :, :], AX.X, ALU.max, apply_absolute_value=True))
                st.then(nc.vector.tensor_reduce(F.swd[:, :], wd[:, :], AX.X, ALU.max, apply_absolute_value=True))
                sw6 = F.sw[:, :, :].rearrange("p a t -> p (a t)")
                over(nc, st, sw6, t127[:, 0:6], rem[:, 0:6], 127.0)
                st.then(nc.vector.tensor_copy(sw6, t127[:, 0:6]))
                over(nc, st, F.swd[:, :], t127[:, 7:8], rem[:, 7:8], 127.0)
                st.then(nc.vector.tensor_copy(F.swd[:, :], t127[:, 7:8]))
                st.then(nc.vector.reciprocal(inv[:, :, :], F.sw[:, :, :]))
                st.then(nc.vector.reciprocal(invd[:, :], F.swd[:, :]))
                W = lambda t: t[:, :, :, :].rearrange("p a t h -> p (a t) h")
                st.then(nc.vector.tensor_tensor(W(tmp), W(wr), inv[:, :, :].rearrange("p a t -> p (a t)").unsqueeze(2).to_broadcast([P, 6, E]), ALU.mult))
                st.then(nc.vector.tensor_scalar(W(tmp), W(tmp), -128.0, 127.0, ALU.max, ALU.min))
                st.then(nc.vector.tensor_scalar(W(wi), W(tmp), MAGIC, MAGIC, ALU.add, ALU.subtract))
                st.then(nc.vector.tensor_scalar(wd[:, :], wd[:, :], invd[:, :], -128.0, ALU.mult, ALU.max))
                st.then(nc.vector.tensor_scalar(wd[:, :], wd[:, :], 127.0, MAGIC, ALU.min, ALU.add))
                st.then(nc.vector.tensor_scalar(wdi[:, :], wd[:, :], MAGIC, None, ALU.subtract))
                assert st.n == WEIGHTS_DONE
                dve.wait_ge(sig_ready, 1)
                dve.wait_ge(spread, 1)
                eighth_power(nc, st, ez[:, :])
                st.then(nc.vector.tensor_scalar(nn[:, :], nn[:, :], -126.0, 127.0, ALU.max, ALU.add))
                st.then(nc.vector.tensor_scalar(pow2[:, :], nn[:, :], EXP1, None, ALU.mult))
                st.then(nc.vector.tensor_tensor(ez[:, :], ez[:, :], pow2[:, :].bitcast(F32), ALU.mult))
                st.then(nc.vector.tensor_scalar(ez[:, :], ez[:, :], 1.0, None, ALU.add))
                st.then(nc.vector.reciprocal(F.clip[:, :], ez[:, :]))
                st.then(nc.vector.tensor_scalar(mx[:, :], am[:, :], F.clip[:, 0:1], None, ALU.mult))
                over(nc, st, mx[:, :], am[:, :], rem[:, 6:7], 127.0)
                st.then(nc.vector.reciprocal(mx[:, :], am[:, :]))
                st.then(nc.vector.tensor_scalar(F.sw[:, :, :], F.sw[:, :, :], am[:, :], None, ALU.mult))
                st.then(nc.vector.tensor_scalar(F.XF[:, :], C.HT[:, :], mx[:, :], -128.0, ALU.mult, ALU.max))
                st.then(nc.vector.tensor_scalar(F.XF[:, :], F.XF[:, :], 127.0, MAGIC, ALU.min, ALU.add))
                nc.vector.tensor_scalar(F.XQ[:, :], F.XF[:, :], MAGIC, None, ALU.subtract)
                dve.wait_ge(turned, 1)
                nc.vector.tensor_copy(F.WT[:, 0, :], C.ps[0][:, 0:192].bitcast(BF16)[:, 0:L0_I])
                nc.vector.tensor_copy(F.WT[:, 1, :], C.ps[1][:, 0:192].bitcast(BF16)[:, 0:L0_I])
                for t, (i0, n) in enumerate(L0_IT):
                    nc.vector.tensor_copy(F.WD[0:n, t, :], C.ps[2][0:n, 64 * t:64 * t + 64].bitcast(BF16))

            @block.tensor
            def _(pe):
                pe.wait_ge(own, WEIGHTS_DONE)
                for a in range(2):
                    for t, (i0, n) in enumerate(L0_IT):
                        nc.tensor.transpose(C.ps[a][:, 0:192].bitcast(BF16)[:, i0:i0 + n], wi[0:n, a, t, :], C.identb[0:n, 0:n])
                for t, (i0, n) in enumerate(L0_IT):
                    last = nc.tensor.transpose(C.ps[2][0:n, 64 * t:64 * t + 64].bitcast(BF16), wdi[:, i0:i0 + n], C.identb[:, :])
                last.then_inc(turned, 1)
    run_stage(nc, ["loaded", "spread", "sig_ready", "turned", "own"], body)


def l0_ffn_up(nc, C, F):
    def body(g_ready, u_ready, sig_ready, h_ready, own):
        with ExitStack() as s:
            sb = sbuf(nc, s)
            sg = sb("sg", [P, 2, CH])
            gs = sb("gs", [P, 2, CH])
            block = s.enter_context(nc.Block())
            jobs = [(q, t) for q in range(2) for t in range(3)]

            @block.tensor
            def _(pe):
                with pe.Fori(0, NCH // 2) as i:
                    for j, (q, t) in enumerate(jobs):
                        i0, n = L0_IT[t]
                        if j >= 2:
                            pe.wait_ge(h_ready, i * 6 + (j - 1))
                        x = F.XQ[:, bass.ds(i * (2 * CH) + q * CH, CH)]
                        nc.tensor.matmul(C.ps[j % 2][0:n, :], F.WT[:, 0, i0:i0 + n], x, start=True, stop=True).then_inc(g_ready, 1)
                        nc.tensor.matmul(C.ps[2 + j % 2][0:n, :], F.WT[:, 1, i0:i0 + n], x, start=True, stop=True).then_inc(u_ready, 1)
                    pe.wait_ge(h_ready, i * 6 + 6)

            @block.scalar
            def _(act):
                with act.Fori(0, NCH // 2) as i:
                    for j, (q, t) in enumerate(jobs):
                        n = L0_IT[t][1]
                        act.wait_ge(g_ready, i * 6 + (j + 1))
                        nc.scalar.activation(sg[0:n, j % 2, :], C.ps[j % 2][0:n, :], ACT.Sigmoid, scale=F.sw[0:n, 0, t:t + 1]).then_inc(sig_ready, 1)

            @block.vector
            def _(dve):
                with dve.Fori(0, NCH // 2) as i:
                    for j, (q, t) in enumerate(jobs):
                        n = L0_IT[t][1]
                        dve.wait_ge(sig_ready, i * 6 + (j + 1))
                        st = Steps(dve, own, i * 6 + j)
                        st.then(nc.vector.scalar_tensor_tensor(gs[0:n, j % 2, :], C.ps[j % 2][0:n, :], F.sw[0:n, 0, t:t + 1], sg[0:n, j % 2, :], ALU.mult, ALU.mult))
                        dve.wait_ge(u_ready, i * 6 + (j + 1))
                        nc.vector.scalar_tensor_tensor(F.HB[0:n, t, bass.ds(i * (2 * CH) + q * CH, CH)], C.ps[2 + j % 2][0:n, :], F.sw[0:n, 1, t:t + 1], gs[0:n, j % 2, :], ALU.mult, ALU.mult).then_inc(h_ready, 1)
    run_stage(nc, ["g_ready", "u_ready", "sig_ready", "h_ready", "own"], body)


def l0_ffn_down(nc, C, F):
    def body(spread, quantised, y_ready, added, own):
        with ExitStack() as s:
            sb = sbuf(nc, s)
            mx, am, mt, rem = sb("mx", [P, 1]), sb("am", [P, 1]), sb("mt", [P, 3]), sb("rem", [P, 1])
            HQ = sb("HQ", [P, 3, TOK], BF16)
            block = s.enter_context(nc.Block())

            @block.gpsimd
            def _(pool):
                pool.wait_ge(own, 3)
                nc.gpsimd.partition_all_reduce(am[:, :], mx[:, :], P, RMAX).then_inc(spread, 1)

            @block.vector
            def _(dve):
                st = Steps(dve, own)
                st.then(nc.vector.memset(mt[:, :], 0.0))
                nc.vector.tensor_reduce(mt[:, 0:2], F.HB[:, 0:2, :], AX.X, ALU.max, apply_absolute_value=True)
                st.then(nc.vector.tensor_reduce(mt[0:96, 2:3], F.HB[0:96, 2, :], AX.X, ALU.max, apply_absolute_value=True))
                st.then(nc.vector.tensor_reduce(mx[:, :], mt[:, :], AX.X, ALU.max))
                dve.wait_ge(spread, 1)
                st.then(nc.vector.tensor_scalar(mx[:, :], am[:, :], F.clip[:, 1:2], None, ALU.mult))
                over(nc, st, mx[:, :], am[:, :], rem[:, :], 127.0)
                st.then(nc.vector.reciprocal(mx[:, :], am[:, :]))
                st.then(nc.vector.tensor_scalar(F.swd[:, :], F.swd[:, :], am[:, :], None, ALU.mult))
                for t, (i0, n) in enumerate(L0_IT):
                    h = F.HB[0:n, t, :]
                    st.then(nc.vector.tensor_scalar(h, h, mx[0:n, :], -128.0, ALU.mult, ALU.max))
                    st.then(nc.vector.tensor_scalar(h, h, 127.0, MAGIC, ALU.min, ALU.add))
                    nc.vector.tensor_scalar(HQ[0:n, t, :], h, MAGIC, None, ALU.subtract).then_inc(quantised, 1)
                for c in range(NCH):
                    dve.wait_ge(y_ready, c + 1)
                    x = C.XT[:, c * CH:(c + 1) * CH]
                    nc.vector.scalar_tensor_tensor(x, C.ps[c][:, :], F.swd[:, :], x, ALU.mult, ALU.add).then_inc(added, 1)

            @block.tensor
            def _(pe):
                for t, (i0, n) in enumerate(L0_IT):
                    pe.wait_ge(quantised, t + 1)
                    for c in range(NCH):
                        mm = nc.tensor.matmul(C.ps[c][:, :], F.WD[0:n, t, :], HQ[0:n, t, c * CH:(c + 1) * CH], start=(t == 0), stop=(t == 2))
                        if t == 2:
                            mm.then_inc(y_ready, 1)
    run_stage(nc, ["spread", "quantised", "y_ready", "added", "own"], body)


def l0_ffn(nc, C):
    layer_norm(nc, C, C.HT)
    F = Core()
    with ExitStack() as s:
        sb = sbuf(nc, s)
        F.clip, F.sw, F.swd = sb("clip", [P, 2]), sb("sw", [P, 2, 3]), sb("swd", [P, 1])
        F.WT, F.WD = sb("WT", [P, 2, L0_I], BF16), sb("WD", [P, 3, E], BF16)
        F.XF, F.XQ = sb("XF", [P, TOK]), sb("XQ", [P, TOK], BF16)
        F.HB = sb("HB", [P, 3, TOK])
        l0_ffn_weights(nc, C, F)
        l0_ffn_up(nc, C, F)
        l0_ffn_down(nc, C, F)


NH, HD = 16, 8
NG = NH // 2
STACK = [(0, 3, 0, 0), (3, 2, 1, 0), (5, 1, 2, 0)]
ROWS = 6 * HD


def split_parts(nc, C, A, QT, KT):
    def body(hi, rest1, mid, rest2, lo, stored):
        with ExitStack() as s:
            sb = sbuf(nc, s)
            parts = sb("parts", [P, 2, 3, TOK], BF16)
            rest = sb("rest", [P, 2, TOK])
            block = s.enter_context(nc.Block())

            @block.scalar
            def _(act):
                for n, src in enumerate((QT, KT)):
                    nc.scalar.activation(parts[:, n, 0, :], src[:, :], ACT.Copy).then_inc(hi, 1)
                for n in range(2):
                    act.wait_ge(rest1, n + 1)
                    nc.scalar.activation(parts[:, n, 1, :], rest[:, n, :], ACT.Copy).then_inc(mid, 1)
                for n in range(2):
                    act.wait_ge(rest2, n + 1)
                    nc.scalar.activation(parts[:, n, 2, :], rest[:, n, :], ACT.Copy).then_inc(lo, 1)

            @block.vector
            def _(dve):
                for n, src in enumerate((QT, KT)):
                    dve.wait_ge(hi, n + 1)
                    nc.vector.tensor_tensor(rest[:, n, :], src[:, :], parts[:, n, 0, :], ALU.subtract).then_inc(rest1, 1)
                for n in range(2):
                    dve.wait_ge(mid, n + 1)
                    nc.vector.tensor_tensor(rest[:, n, :], rest[:, n, :], parts[:, n, 1, :], ALU.subtract).then_inc(rest2, 1)

            @block.sync
            def _(sp):
                for k, done in enumerate((hi, mid, lo)):
                    for n in range(2):
                        sp.wait_ge(done, n + 1)
                        sp.dma_start(C.qk_parts[n, k, :, :], parts[:, n, k, :]).then_inc(stored, 16)
                sp.wait_ge(stored, 96)
    run_stage(nc, ["hi", "rest1", "mid", "rest2", "lo", "stored"], body)


def attend(nc, C, A):
    KR = ROWS + (1 if A.key_mask is not None else 0)
    LOADS = 24 + (2 if A.key_mask is not None else 0)

    def body(stacked0, stacked1, sel_in, ones_set, v_staged, a_ready, a_max, nm_ready, nm_turned, nm_kept, b_ready, p_ready, pv_done,
             o_normed, o_turned, oT_kept, y_ready, added, own):
        stacked = (stacked0, stacked1)
        with ExitStack() as s:
            sb = sbuf(nc, s)
            QS, KS = sb("QS", [P, 2, NG, S], BF16), sb("KS", [P, 2, NG, S], BF16)
            sel = sb("selm", [P, NH, P], BF16)
            VB = sb("VB", [P, 2, 2, NH, HD + 1])
            mx = sb("mx", [P, 2, NH])
            nm = sb("nm", [P, 2, 2, 4, NH], BF16)
            nr = sb("nr", [P, 2, NH])
            NMT = sb("NMT", [P, 2, S], BF16)
            PT = sb("PT", [P, 2, 2, 2, S])
            rec = sb("rec", [P, 2, NH])
            o = sb("oatt", [P, 2, NH, HD])
            oT = sb("oT", [P, S])
            block = s.enter_context(nc.Block())
            bankA = C.ps[0:2]
            bankB = (C.ps[2:4], C.ps[4:6])
            bankO, bankT = C.ps[6], C.ps[7]
            NMP = bankA[0][:, 0:S // 2].bitcast(BF16)
            O = bankO[:, 0:288].rearrange("p (t h e) -> p t h e", t=2, h=NH)

            @block.sync
            def _(sp):
                for r in (0, 64):
                    sp.dma_start(sel[r:r + 48, :, :], C.c["max_rows"]).then_inc(sel_in, 16)
                sp.wait_ge(ones_set, 2)

                def load(t, p):
                    for s0, n, qp, kp in STACK:
                        for hh in range(2):
                            src = C.qk_parts[0, qp, :, bass.ds(t * S, S)].rearrange("(g x d) t -> x d g t", x=2, d=HD)[hh]
                            for k in range(n):
                                r = 64 * hh + HD * (s0 + k)
                                sp.dma_start(QS[r:r + HD, p, :, :], src).then_inc(stacked[p], 16)
                                srck = C.qk_parts[1, kp + k, :, bass.ds(t * S, S)].rearrange("(g x d) t -> x d g t", x=2, d=HD)[hh]
                                sp.dma_start(KS[r:r + HD, p, :, :], srck).then_inc(stacked[p], 16)
                    if A.key_mask is not None:
                        for hh in range(2):
                            sp.dma_start(KS[64 * hh + ROWS:64 * hh + ROWS + 1, p, :, :], A.key_mask(t)).then_inc(stacked[p], 16)
                for p in range(2):
                    load(p, p)
                with sp.Fori(0, B // 2 - 1) as i:
                    for p in range(2):
                        sp.wait_ge(b_ready, i * 16 + 8 * (p + 1))
                        load(i * 2 + (2 + p), p)

            @block.gpsimd
            def _(pool):
                for p in range(2):
                    nc.gpsimd.tensor_copy(VB[:, p, :, :, :].rearrange("p t h e -> p t (h e)"), A.VA[:, 2 * p:2 * p + 2, :]).then_inc(v_staged, 1)
                with pool.Fori(0, B // 2 - 1) as i:
                    for p in range(2):
                        pool.wait_ge(pv_done, i * 16 + 8 * (p + 1))
                        nc.gpsimd.tensor_copy(VB[:, p, :, :, :].rearrange("p t h e -> p t (h e)"), A.VA[:, bass.ds(i * 4 + (4 + 2 * p), 2), :]).then_inc(v_staged, 1)

            @block.tensor
            def _(pe):
                pe.wait_ge(sel_in, 32)
                NM = len(A.masks) if A.masks else 0
                with pe.Fori(0, B // 2) as i:
                    def pass_a(p, h):
                        if not (p == 0 and h < 2):
                            pe.wait_ge(a_max, i * 32 + (16 * p + h - 1))
                        r = slice(64 * (h % 2), 64 * (h % 2) + KR)
                        for t in range(2):
                            out = bankA[h % 2][:, t * S:(t + 1) * S]
                            mm = nc.tensor.matmul(out, QS[r, p, h // 2, t * P:(t + 1) * P], KS[r, p, h // 2, :], start=(t == 0), stop=(NM == 0), skip_group_check=True)
                        for k in range(NM):
                            mm = nc.tensor.matmul(bankA[h % 2][:, :], C.identb[:, :], A.masks[k][0](i * 2 + p), start=False, stop=(k == NM - 1), skip_group_check=True)
                        mm.then_inc(a_ready, 1)

                    def pass_b(p, sl):
                        if sl >= 2:
                            pe.wait_ge(p_ready, i * 16 + (8 * p + sl - 1))
                        for x in range(2):
                            h = 2 * sl + x
                            r = slice(64 * x, 64 * x + KR)
                            bank = bankB[sl % 2][x]
                            for t in range(2):
                                out = bank[:, t * S:(t + 1) * S]
                                nc.tensor.matmul(out, KS[r, p, sl, t * P:(t + 1) * P], QS[r, p, sl, :], start=(t == 0), stop=False, skip_group_check=True)
                            for k in range(NM):
                                nc.tensor.matmul(bank[:, :], C.identb[:, :], A.masks[k][1](i * 2 + p), start=False, stop=False, skip_group_check=True)
                            for t in range(2):
                                mm = nc.tensor.matmul(bank[:, t * S:(t + 1) * S], sel[64 * x:64 * x + 48, h, :], NMT[64 * x:64 * x + 48, p, :], start=False, stop=True, skip_group_check=True)
                        mm.then_inc(b_ready, 1)

                    def values(p, sl):
                        pe.wait_ge(p_ready, i * 16 + (8 * p + sl + 1))
                        for x in range(2):
                            h = 2 * sl + x
                            for t in range(2):
                                for kt in range(2):
                                    mm = nc.tensor.matmul(bankO[:, t * 144 + h * 9:t * 144 + h * 9 + 9], PT[:, sl % 2, x, kt, t * P:(t + 1) * P], VB[:, p, kt, h, :], start=(kt == 0), stop=(kt == 1), skip_group_check=True)
                        mm.then_inc(pv_done, 1)

                    def turn_max(p):
                        pe.wait_ge(nm_ready, i * 2 + (p + 1))
                        for t in range(2):
                            mm = nc.tensor.transpose(NMP[:, t * P:(t + 1) * P], nm[:, t, :, :, :].rearrange("p a k h -> p (a k h)"), C.identb[:, :])
                        mm.then_inc(nm_turned, 1)
                        pe.wait_ge(nm_kept, i * 2 + (p + 1))

                    def turn_out(p):
                        pe.wait_ge(o_normed, i * 2 + (p + 1))
                        for t in range(2):
                            mm = nc.tensor.transpose(bankT[:, t * P:(t + 1) * P], o[:, t, :, :].rearrange("p h d -> p (h d)"), C.ident[:, :])
                        mm.then_inc(o_turned, 1)

                    def project(p):
                        pe.wait_ge(oT_kept, i * 2 + (p + 1))
                        nc.tensor.matmul(bankT[:, S:2 * S], A.wo, oT[:, :], start=True, stop=True, skip_group_check=True).then_inc(y_ready, 1)

                    pe.wait_ge(stacked[0], i * (16 * LOADS) + 16 * LOADS)
                    for h in range(NH):
                        pass_a(0, h)
                    turn_max(0)
                    pe.wait_ge(stacked[1], i * (16 * LOADS) + 16 * LOADS)
                    pe.wait_ge(v_staged, i * 2 + 1)
                    for sl in range(8):
                        pass_a(1, 2 * sl)
                        pass_b(0, sl)
                        pass_a(1, 2 * sl + 1)
                        if sl >= 1:
                            values(0, sl - 1)
                    values(0, 7)
                    turn_max(1)
                    turn_out(0)
                    pe.wait_ge(v_staged, i * 2 + 2)
                    for sl in range(8):
                        pass_b(1, sl)
                        if sl == 2:
                            project(0)
                        if sl >= 1:
                            values(1, sl - 1)
                    values(1, 7)
                    turn_out(1)
                    project(1)

            @block.vector
            def _(dve):
                nc.vector.memset(QS[32:64, :, :, :], 1.0)
                nc.vector.memset(QS[96:128, :, :, :], 1.0).then_inc(ones_set, 1)
                nc.vector.memset(KS[32:64, :, :, :], 1.0)
                nc.vector.memset(KS[96:128, :, :, :], 1.0).then_inc(ones_set, 1)
                nc.vector.memset(nm[:, :, :, :, :], 0.0)
                with dve.Fori(0, B // 2) as i:
                    st = Steps(dve, own, i * 12)

                    def maxima(p):
                        for h in range(NH):
                            dve.wait_ge(a_ready, i * 32 + (16 * p + h + 1))
                            nc.vector.tensor_reduce(mx[:, :, h], bankA[h % 2][:, :].rearrange("p (t k) -> p t k", t=2), AX.X, ALU.max).then_inc(a_max, 1)
                        dve.wait_ge(a_max, i * 32 + 16 * (p + 1))
                        st.then(nc.vector.tensor_scalar(nm[:, :, 0, 0, :], mx[:, :, :], -1.0, None, ALU.mult))
                        st.then(nc.vector.scalar_tensor_tensor(nr[:, :, :], mx[:, :, :], -1.0, nm[:, :, 0, 0, :], ALU.mult, ALU.subtract))
                        st.then(nc.vector.tensor_copy(nm[:, :, 0, 1, :], nr[:, :, :]))
                        st.then(nc.vector.tensor_tensor(nr[:, :, :], nr[:, :, :], nm[:, :, 0, 1, :], ALU.subtract))
                        st.then(nc.vector.tensor_copy(nm[:, :, 0, 2, :], nr[:, :, :]))
                        nc.vector.tensor_copy(nm[:, :, 1, 0:3, :], nm[:, :, 0, 0:3, :]).then_inc(nm_ready, 1)

                    def normalise(p):
                        dve.wait_ge(pv_done, i * 16 + 8 * (p + 1))
                        st.then(nc.vector.reciprocal(rec[:, :, :], O[:, :, :, HD]))
                        nc.vector.tensor_tensor(o[:, :, :, :].rearrange("p t h d -> p (t h) d"), O[:, :, :, 0:HD].rearrange("p t h d -> p (t h) d"),
                                                rec[:, :, :].rearrange("p t h -> p (t h)").unsqueeze(2).to_broadcast([P, 2 * NH, HD]), ALU.mult).then_inc(o_normed, 1)

                    def residual(p):
                        dve.wait_ge(y_ready, i * 2 + (p + 1))
                        x = C.XT[:, bass.ds(i * (2 * S) + p * S, S)]
                        nc.vector.scalar_tensor_tensor(x, bankT[:, S:2 * S], A.bo, x, ALU.add, ALU.add).then_inc(added, 1)

                    maxima(0)
                    maxima(1)
                    normalise(0)
                    residual(0)
                    normalise(1)
                    residual(1)
                    assert st.n == 12, st.n

            @block.scalar
            def _(act):
                nc.scalar.preload_act_table_set(LN_EXP)
                with act.Fori(0, B // 2) as i:
                    def keep_max(p):
                        act.wait_ge(nm_turned, i * 2 + (p + 1))
                        nc.scalar.activation(NMT[:, p, :], NMP, ACT.Copy).then_inc(nm_kept, 1)

                    def weights(p, sl):
                        act.wait_ge(b_ready, i * 16 + (8 * p + sl + 1))
                        if sl >= 2:
                            act.wait_ge(pv_done, i * 16 + (8 * p + sl - 1))
                        for x in range(2):
                            last = nc.scalar.activation(PT[:, sl % 2, x, :, :].rearrange("p t s -> p (t s)"), bankB[sl % 2][x][:, :], ACT.Exp, scale=A.scale)
                        last.then_inc(p_ready, 1)

                    def keep_out(p):
                        act.wait_ge(o_turned, i * 2 + (p + 1))
                        nc.scalar.activation(oT[:, :], bankT[:, 0:S], ACT.Copy).then_inc(oT_kept, 1)

                    keep_max(0)
                    for sl in range(8):
                        weights(0, sl)
                    keep_max(1)
                    keep_out(0)
                    for sl in range(8):
                        weights(1, sl)
                    keep_out(1)
    run_stage(nc, ["stacked0", "stacked1", "sel_in", "ones_set", "v_staged", "a_ready", "a_max", "nm_ready", "nm_turned", "nm_kept", "b_ready", "p_ready", "pv_done",
                   "o_normed", "o_turned", "oT_kept", "y_ready", "added", "own"], body)


def l1_prepare(nc, C, A):
    def body(loaded, made, turned, kept, wo_turned):
        with ExitStack() as s:
            sb = sbuf(nc, s)
            mi = sb("mi", [P, B, 2, S], I32)
            wo_rows = sb("wo_rows", [P, E])
            block = s.enter_context(nc.Block())

            @block.sync
            def _(sp):
                sp.dma_start(mi[:, :, :, :], C.i["mask_Bx1xSxS2_ik1"].rearrange("b o (t p) k -> p (b o) t k", p=P)).then_inc(loaded, 16)
                sp.dma_start(wo_rows[:, :], C.i["L1_xattn_W_out"]).then_inc(loaded, 16)
                sp.dma_start(A.bo_t[:, :], C.i["L1_xattn_b_out"].unsqueeze(1)).then_inc(loaded, 16)

            @block.vector
            def _(dve):
                nc.vector.memset(A.VA4[:, :, :, HD:HD + 1], 1.0)
                dve.wait_ge(loaded, 48)
                for b in range(B):
                    nc.vector.tensor_scalar(A.MQ[:, b, :, :], mi[:, b, :, :], 0, -1e20, ALU.is_equal, ALU.mult).then_inc(made, 1)
                nc.vector.tensor_copy(A.VA4[:, :, :, 0:HD], C.CN[:, :, :].rearrange("p n (h d) -> p n h d", h=NH))
                for b in range(B):
                    dve.wait_ge(turned, b + 1)
                    nc.vector.tensor_copy(A.MK[:, b, :, :].rearrange("p t s -> p (t s)"), C.ps[b][:, 0:S].bitcast(BF16)).then_inc(kept, 1)
                dve.wait_ge(wo_turned, 1)
                nc.vector.tensor_copy(A.wo_t[:, :], C.ps[0][:, 256:256 + P])

            @block.tensor
            def _(pe):
                for b in range(B):
                    pe.wait_ge(made, b + 1)
                    for kt in range(2):
                        for qt in range(2):
                            mm = nc.tensor.transpose(C.ps[b][:, 0:S].bitcast(BF16)[:, kt * S + qt * P:kt * S + (qt + 1) * P], A.MQ[:, b, qt, kt * P:(kt + 1) * P], C.identb[:, :])
                    mm.then_inc(turned, 1)
                pe.wait_ge(loaded, 48)
                pe.wait_ge(kept, 1)
                nc.tensor.transpose(C.ps[0][:, 256:256 + P], wo_rows[:, :], C.ident[:, :]).then_inc(wo_turned, 1)
    run_stage(nc, ["loaded", "made", "turned", "kept", "wo_turned"], body)


def l1_xattn(nc, C):
    layer_norm(nc, C, C.HT)
    split_parts(nc, C, None, C.HT, C.CT)
    A = Core()
    with ExitStack() as s:
        sb = sbuf(nc, s)
        A.MQ, A.MK = sb("MQ", [P, B, 2, S], BF16), sb("MK", [P, B, 2, S], BF16)
        A.wo_t, A.bo_t = sb("wo_t", [P, E]), sb("bo_t", [P, 1])
        VA = sb("VA", [P, NT, NH * (HD + 1)])
        A.VA, A.VA4 = VA, VA[:, :, :].rearrange("p n (h e) -> p n h e", h=NH)
        l1_prepare(nc, C, A)
        A.wo, A.bo = A.wo_t[:, :], A.bo_t[:, :]
        A.scale = float(E) ** -0.5
        A.key_mask = None
        MQf, MKf = A.MQ[:, :, :, :].rearrange("p b t s -> p (b t s)"), A.MK[:, :, :, :].rearrange("p b t s -> p (b t s)")
        A.masks = [(lambda b: MQf[:, bass.ds(b * (2 * S), 2 * S)], lambda b: MKf[:, bass.ds(b * (2 * S), 2 * S)])]
        attend(nc, C, A)


def project_qkv(nc, C, A, V):
    def body(qk_ready, qk_kept, v_ready, v_kept):
        with nc.Block() as block:
            jobs = [(w, src, dst, c) for w, src, dst in (("q", C.HT, A.QT), ("k", C.CT, A.KT)) for c in range(NCH)]

            @block.tensor
            def _(pe):
                for j, (w, src, dst, c) in enumerate(jobs):
                    if j >= 4:
                        pe.wait_ge(qk_kept, j - 3)
                    nc.tensor.matmul(C.ps[j % 4][:, :], A.w[w], src[:, c * CH:(c + 1) * CH], start=True, stop=True).then_inc(qk_ready, 1)
                for q in range(4):
                    for t in range(4):
                        n = 4 * q + t
                        mm = nc.tensor.matmul(C.ps[4 + q][:, t * P:(t + 1) * P], C.CT[:, n * P:(n + 1) * P], A.w["v"], start=True, stop=True)
                    mm.then_inc(v_ready, 1)

            @block.vector
            def _(dve):
                nc.vector.memset(A.VA4[:, :, :, HD:HD + 1], 1.0)
                for j, (w, src, dst, c) in enumerate(jobs):
                    dve.wait_ge(qk_ready, j + 1)
                    bias, scale = A.qk_bias[w]
                    nc.vector.tensor_scalar(dst[:, c * CH:(c + 1) * CH], C.ps[j % 4][:, :], bias, scale, ALU.add, ALU.mult).then_inc(qk_kept, 1)
                for q in range(4):
                    dve.wait_ge(v_ready, q + 1)
                    for t in range(4):
                        v = C.ps[4 + q][:, t * P:(t + 1) * P].rearrange("p (h d) -> p h d", h=NH)
                        dst = A.VA4[:, 4 * q + t, :, 0:HD]
                        if A.v_bias is None:
                            nc.vector.tensor_copy(dst, v).then_inc(v_kept, 1)
                        else:
                            nc.vector.tensor_tensor(dst, v, A.v_bias[:, :].rearrange("p (h d) -> p h d", h=NH), ALU.add).then_inc(v_kept, 1)
    run_stage(nc, ["qk_ready", "qk_kept", "v_ready", "v_kept"], body)


def l2_prepare(nc, C, A):
    def body(loaded, spread, rep_ready, rep_kept, mask_made, stored, own):
        with ExitStack() as s:
            sb = sbuf(nc, s)
            w8 = sb("w8", [HD, 3, HD])
            w8r = sb("w8r", [HD, 3, NH, HD])
            rep = sb("rep", [P, 3, HD])
            blk = sb("blk", [P, P])
            mi = sb("mi2", [8, S], I32)
            mb = sb("mb2", [8, S], BF16)
            wo_rows = sb("wo_rows2", [P, E])
            block = s.enter_context(nc.Block())

            @block.sync
            def _(sp):
                for n, name in enumerate(("Wq", "Wk", "Wv")):
                    sp.dma_start(w8[:, n, :], C.i[f"L2_xattn_{name}"]).then_inc(loaded, 16)
                sp.dma_start(wo_rows[:, :], C.i["L2_xattn_Wo"]).then_inc(loaded, 16)
                sp.dma_start(A.bo_t[:, :], C.i["L2_xattn_bo"].unsqueeze(1)).then_inc(loaded, 16)
                sp.dma_start(blk[:, :], C.c["head_blocks"]).then_inc(loaded, 16)
                sp.dma_start(mi[:, :], C.i["mask_Bx1x1xS2_if1"].rearrange("b o q k -> (b o q) k")).then_inc(loaded, 16)
                sp.wait_ge(mask_made, 1)
                sp.dma_start(C.key_bias, mb[:, :]).then_inc(stored, 16)
                sp.wait_ge(stored, 16)

            @block.vector
            def _(dve):
                dve.wait_ge(loaded, 16 * 7)
                nc.vector.tensor_scalar(mb[:, :], mi[:, :], 0, -1e20, ALU.is_equal, ALU.mult).then_inc(mask_made, 1)
                for n in range(3):
                    last = nc.vector.tensor_copy(w8r[:, n, :, :], w8[:, n, :].unsqueeze(1).to_broadcast([HD, NH, HD]))
                last.then_inc(spread, 1)
                dve.wait_ge(rep_ready, 1)
                nc.vector.tensor_copy(rep[:, :, :].rearrange("p n e -> p (n e)"), C.ps[0][:, 0:24]).then_inc(rep_kept, 1)
                nc.vector.tensor_copy(A.wo_t[:, :], C.ps[0][:, P:2 * P])
                dve.wait_ge(rep_kept, 1)
                for n in range(3):
                    nc.vector.tensor_tensor(A.bd[:, n, :].rearrange("p (h e) -> p h e", h=NH), blk[:, :].rearrange("p (h e) -> p h e", h=NH), rep[:, n, :].unsqueeze(1).to_broadcast([P, NH, HD]), ALU.mult)

            @block.tensor
            def _(pe):
                pe.wait_ge(spread, 1)
                for n in range(3):
                    nc.tensor.matmul(C.ps[0][:, n * HD:(n + 1) * HD], w8r[:, n, :, :].rearrange("k h d -> k (h d)"), C.ident[0:HD, 0:HD], start=(n == 0), stop=True, skip_group_check=True)
                nc.tensor.transpose(C.ps[0][:, P:2 * P], wo_rows[:, :], C.ident[:, :]).then_inc(rep_ready, 1)
    run_stage(nc, ["loaded", "spread", "rep_ready", "rep_kept", "mask_made", "stored", "own"], body)


def l2_xattn(nc, C):
    layer_norm(nc, C, C.HT)
    A = Core()
    with ExitStack() as s:
        sb = sbuf(nc, s)
        A.bd = sb("bd", [P, 3, P])
        A.wo_t, A.bo_t = sb("wo_t", [P, E]), sb("bo_t", [P, 1])
        VA = sb("VA", [P, NT, NH * (HD + 1)])
        A.VA, A.VA4 = VA, VA[:, :, :].rearrange("p n (h e) -> p n h e", h=NH)
        l2_prepare(nc, C, A)
        A.w = {"q": A.bd[:, 0, :], "k": A.bd[:, 1, :], "v": A.bd[:, 2, :]}
        A.qk_bias = {"q": (0.0, 1.0), "k": (0.0, 1.0)}
        A.v_bias = None
        with ExitStack() as s2:
            A.QT, A.KT = sbuf(nc, s2)("QT", [P, TOK]), sbuf(nc, s2)("KT", [P, TOK])
            project_qkv(nc, C, A, None)
            split_parts(nc, C, A, A.QT, A.KT)
        A.wo, A.bo = A.wo_t[:, :], A.bo_t[:, :]
        A.scale = float(E) ** -0.5
        A.key_mask = lambda t: C.key_bias[bass.ds(t, 1), :].unsqueeze(1).to_broadcast([1, NG, S])
        A.masks = None
        attend(nc, C, A)


def l3x_prepare(nc, C, A):
    def body(loaded, made, turned, own):
        with ExitStack() as s:
            sb = sbuf(nc, s)
            mf, r = sb("mf", [P, 2, S]), sb("mr", [P, 2, S])
            block = s.enter_context(nc.Block())

            @block.sync
            def _(sp):
                sp.dma_start(mf[:, :, :], C.i["mask_1x1xSxS2_fk1"].rearrange("o b (t p) k -> p (o b t) k", p=P)).then_inc(loaded, 16)
                for n, name in enumerate("qkvo"):
                    sp.dma_start(A.wt[:, n, :], C.i[f"L3_xattn_w{name}"]).then_inc(loaded, 16)
                for n, name in enumerate("qko"):
                    sp.dma_start(A.bt[:, n:n + 1], C.i[f"L3_xattn_b{name}"].unsqueeze(1)).then_inc(loaded, 16)
                sp.dma_start(A.v_bias[:, :], C.i["L3_xattn_bv"].unsqueeze(0).to_broadcast([P, E])).then_inc(loaded, 16)

            @block.vector
            def _(dve):
                st = Steps(dve, own)
                dve.wait_ge(loaded, 16 * 9)
                st.then(nc.vector.tensor_scalar(mf[:, :, :], mf[:, :, :], -1000000000.0, None, ALU.mult))
                st.then(nc.vector.tensor_copy(A.MQ[:, 0, :, :], mf[:, :, :]))
                st.then(nc.vector.tensor_tensor(r[:, :, :], mf[:, :, :], A.MQ[:, 0, :, :], ALU.subtract))
                st.then(nc.vector.tensor_copy(A.MQ[:, 1, :, :], r[:, :, :]))
                st.then(nc.vector.tensor_tensor(r[:, :, :], r[:, :, :], A.MQ[:, 1, :, :], ALU.subtract))
                nc.vector.tensor_copy(A.MQ[:, 2, :, :], r[:, :, :]).then_inc(made, 1)
                for k in range(3):
                    dve.wait_ge(turned, k + 1)
                    nc.vector.tensor_copy(A.MK[:, k, :, :].rearrange("p t s -> p (t s)"), C.ps[k][:, 0:S].bitcast(BF16))

            @block.tensor
            def _(pe):
                pe.wait_ge(made, 1)
                for k in range(3):
                    for kt in range(2):
                        for qt in range(2):
                            mm = nc.tensor.transpose(C.ps[k][:, 0:S].bitcast(BF16)[:, kt * S + qt * P:kt * S + (qt + 1) * P], A.MQ[:, k, qt, kt * P:(kt + 1) * P], C.identb[:, :])
                    mm.then_inc(turned, 1)
    run_stage(nc, ["loaded", "made", "turned", "own"], body)


def l3_xattn(nc, C):
    layer_norm(nc, C, C.HT)
    A = Core()
    with ExitStack() as s:
        sb = sbuf(nc, s)
        A.wt, A.bt, A.v_bias = sb("w_qkvo", [P, 4, E]), sb("b_qko", [P, 3]), sb("v_bias", [P, E])
        A.MQ, A.MK = sb("MQ3", [P, 3, 2, S], BF16), sb("MK3", [P, 3, 2, S], BF16)
        VA = sb("VA", [P, NT, NH * (HD + 1)])
        A.VA, A.VA4 = VA, VA[:, :, :].rearrange("p n (h e) -> p n h e", h=NH)
        l3x_prepare(nc, C, A)
        A.w = {"q": A.wt[:, 0, :], "k": A.wt[:, 1, :], "v": A.wt[:, 2, :]}
        A.qk_bias = {"q": (A.bt[:, 0:1], float(HD) ** -0.5), "k": (A.bt[:, 1:2], 1.0)}
        with ExitStack() as s2:
            A.QT, A.KT = sbuf(nc, s2)("QT", [P, TOK]), sbuf(nc, s2)("KT", [P, TOK])
            project_qkv(nc, C, A, None)
            split_parts(nc, C, A, A.QT, A.KT)
        A.wo, A.bo = A.wt[:, 3, :], A.bt[:, 2:3]
        A.scale = 1.0
        A.key_mask = None
        A.masks = [(lambda b, k=k: A.MQ[:, k, :, :].rearrange("p t s -> p (t s)"), lambda b, k=k: A.MK[:, k, :, :].rearrange("p t s -> p (t s)")) for k in range(3)]
        attend(nc, C, A)


L1_I = 384
L1_IT = L1_I // P
BLK = 32
QM = 32767.0


def l1_ffn_weights(nc, C, F):
    def body(loaded, turned, kept, own):
        with ExitStack() as s:
            sb = sbuf(nc, s)
            w = sb("w_rows", [P, 9, E])
            t1 = sb("w_units", [P, 9, E])
            sc, inv = sb("w_scale", [P, 36]), sb("w_inv", [P, 36])
            block = s.enter_context(nc.Block())

            @block.sync
            def _(sp):
                for n, name in enumerate(("gate", "up")):
                    sp.dma_start(w[:, 3 * n:3 * n + 3, :], C.i[f"L1_ffn_w_{name}"].rearrange("(t p) h -> p t h", p=P)).then_inc(loaded, 16)
                sp.dma_start(w[:, 6:9, :], C.i["L1_ffn_w_down"].rearrange("h (t i) -> h t i", i=E)).then_inc(loaded, 16)

            @block.vector
            def _(dve):
                st = Steps(dve, own)
                dve.wait_ge(loaded, 48)
                W = lambda a: a[:, :, :].rearrange("p n (k i) -> p (n k) i", i=BLK)
                bc = lambda a: a[:, :].unsqueeze(2).to_broadcast([P, 36, BLK])
                st.then(nc.vector.tensor_reduce(sc[:, :], W(w), AX.X, ALU.max, apply_absolute_value=True))
                st.then(nc.vector.tensor_scalar(sc[:, :], sc[:, :], 1.0 / 7.0, 1e-12, ALU.mult, ALU.max))
                st.then(nc.vector.reciprocal(inv[:, :], sc[:, :]))
                st.then(nc.vector.tensor_tensor(W(t1), W(w), bc(inv), ALU.mult))
                st.then(nc.vector.tensor_scalar(t1[:, :, :], t1[:, :, :], -8.0, 7.0, ALU.max, ALU.min))
                st.then(nc.vector.tensor_scalar(t1[:, :, :], t1[:, :, :], MAGIC, MAGIC, ALU.add, ALU.subtract))
                st.then(nc.vector.tensor_tensor(W(w), W(t1), bc(sc), ALU.mult))
                for q in range(3):
                    dve.wait_ge(turned, q + 1)
                    nc.vector.tensor_copy(F.W[:, 3 * q:3 * q + 3, :].rearrange("p n h -> p (n h)"), C.ps[q][:, 0:384])

            @block.tensor
            def _(pe):
                pe.wait_ge(own, 7)
                for q in range(9):
                    mm = nc.tensor.transpose(C.ps[q // 3][:, (q % 3) * P:(q % 3 + 1) * P], w[:, q, :], C.ident[:, :])
                    if q % 3 == 2:
                        mm.then_inc(turned, 1)
    run_stage(nc, ["loaded", "turned", "kept", "own"], body)


def l1_ffn_body(nc, C, F):
    N3 = 3 * TOK
    def body(xmax, spread, x_ready, gu_ready, gu_kept, sig_in, sig_out, o_int, y_ready, added, own):
        with ExitStack() as s:
            sb = sbuf(nc, s)
            U, G, SG = sb("U", [P, 3, TOK]), sb("G", [P, 3, TOK]), sb("SG", [P, 3, TOK])
            m = sb("m_part", [P, 8])
            am = sb("m_all", [P, 8])
            sc = sb("sc16", [P, 8])
            iv = sb("iv16", [P, 8])
            block = s.enter_context(nc.Block())
            X, UP, GT, G2, OO = range(5)
            flat = lambda a: a[:, :, :].rearrange("p t n -> p (t n)")

            @block.gpsimd
            def _(pool):
                for k in range(5):
                    pool.wait_ge(xmax, k + 1)
                    nc.gpsimd.partition_all_reduce(am[:, k:k + 1], m[:, k:k + 1], P, RMAX).then_inc(spread, 1)

            @block.vector
            def _(dve):
                st = Steps(dve, own)

                def scale_of(k):
                    dve.wait_ge(spread, k + 1)
                    st.then(nc.vector.tensor_scalar(sc[:, k:k + 1], am[:, k:k + 1], 1.0 / QM, 1e-12, ALU.mult, ALU.max))
                    st.then(nc.vector.reciprocal(iv[:, k:k + 1], sc[:, k:k + 1]))

                def to_int(a, k, last=None):
                    st.then(nc.vector.tensor_scalar(a, a, iv[:, k:k + 1], -QM - 1.0, ALU.mult, ALU.max))
                    st.then(nc.vector.tensor_scalar(a, a, QM, MAGIC, ALU.min, ALU.add))

                nc.vector.tensor_reduce(m[:, X:X + 1], C.HT[:, :], AX.X, ALU.max, apply_absolute_value=True).then_inc(xmax, 1)
                scale_of(X)
                to_int(C.HT[:, :], X)
                nc.vector.tensor_scalar(C.HT[:, :], C.HT[:, :], MAGIC, sc[:, X:X + 1], ALU.subtract, ALU.mult).then_inc(x_ready, 1)
                for c in range(NCH):
                    for t in range(3):
                        j = c * 3 + t
                        dve.wait_ge(gu_ready, j + 1)
                        nc.vector.tensor_copy(U[:, t, c * CH:(c + 1) * CH], C.ps[2 * (j % 3) + 1][:, :]).then_inc(gu_kept, 1)
                dve.wait_ge(gu_kept, 12)
                nc.vector.tensor_reduce(m[:, UP:UP + 1], flat(U), AX.X, ALU.max, apply_absolute_value=True).then_inc(xmax, 1)
                dve.wait_ge(sig_in, 12)
                nc.vector.tensor_reduce(m[:, GT:GT + 1], flat(G), AX.X, ALU.max, apply_absolute_value=True).then_inc(xmax, 1)
                scale_of(GT)
                to_int(flat(G), GT)
                nc.vector.tensor_scalar(flat(G), flat(G), MAGIC, sc[:, GT:GT + 1], ALU.subtract, ALU.mult).then_inc(x_ready, 1)
                scale_of(UP)
                to_int(flat(U), UP)
                st.then(nc.vector.tensor_scalar(flat(U), flat(U), MAGIC, sc[:, UP:UP + 1], ALU.subtract, ALU.mult))
                dve.wait_ge(sig_out, 3)
                st.then(nc.vector.tensor_scalar(flat(SG), flat(SG), 65536.0, 0.0, ALU.mult, ALU.max))
                st.then(nc.vector.tensor_scalar(flat(SG), flat(SG), 65535.0, MAGIC, ALU.min, ALU.add))
                st.then(nc.vector.tensor_scalar(flat(SG), flat(SG), MAGIC, 1.0 / 65536.0, ALU.subtract, ALU.mult))
                st.then(nc.vector.tensor_tensor(flat(G), flat(G), flat(SG), ALU.mult))
                nc.vector.tensor_reduce(m[:, G2:G2 + 1], flat(G), AX.X, ALU.max, apply_absolute_value=True).then_inc(xmax, 1)
                scale_of(G2)
                to_int(flat(G), G2)
                st.then(nc.vector.tensor_scalar(flat(G), flat(G), MAGIC, sc[:, G2:G2 + 1], ALU.subtract, ALU.mult))
                st.then(nc.vector.tensor_tensor(flat(G), flat(G), flat(U), ALU.mult))
                nc.vector.tensor_reduce(m[:, OO:OO + 1], flat(G), AX.X, ALU.max, apply_absolute_value=True).then_inc(xmax, 1)
                scale_of(OO)
                for t in range(3):
                    to_int(G[:, t, :], OO)
                    nc.vector.tensor_scalar(G[:, t, :], G[:, t, :], MAGIC, sc[:, OO:OO + 1], ALU.subtract, ALU.mult).then_inc(o_int, 1)
                for c in range(NCH):
                    dve.wait_ge(y_ready, c + 1)
                    x = C.XT[:, c * CH:(c + 1) * CH]
                    nc.vector.tensor_tensor(x, x, C.ps[c][:, :], ALU.add).then_inc(added, 1)

            @block.scalar
            def _(act):
                for c in range(NCH):
                    for t in range(3):
                        j = c * 3 + t
                        act.wait_ge(gu_ready, j + 1)
                        nc.scalar.activation(G[:, t, c * CH:(c + 1) * CH], C.ps[2 * (j % 3)][:, :], ACT.Copy).then_inc(sig_in, 1)
                act.wait_ge(x_ready, 2)
                for t in range(3):
                    nc.scalar.activation(SG[:, t, :], G[:, t, :], ACT.Sigmoid).then_inc(sig_out, 1)

            @block.tensor
            def _(pe):
                pe.wait_ge(x_ready, 1)
                for c in range(NCH):
                    for t in range(3):
                        j = c * 3 + t
                        if j >= 3:
                            pe.wait_ge(gu_kept, j - 2)
                            pe.wait_ge(sig_in, j - 2)
                        x = C.HT[:, c * CH:(c + 1) * CH]
                        nc.tensor.matmul(C.ps[2 * (j % 3)][:, :], F.W[:, t, :], x, start=True, stop=True)
                        nc.tensor.matmul(C.ps[2 * (j % 3) + 1][:, :], F.W[:, 3 + t, :], x, start=True, stop=True).then_inc(gu_ready, 1)
                pe.wait_ge(gu_kept, 12)
                pe.wait_ge(sig_in, 12)
                for t in range(3):
                    pe.wait_ge(o_int, t + 1)
                    for c in range(NCH):
                        mm = nc.tensor.matmul(C.ps[c][:, :], F.W[:, 6 + t, :], G[:, t, c * CH:(c + 1) * CH], start=(t == 0), stop=(t == 2))
                        if t == 2:
                            mm.then_inc(y_ready, 1)
    run_stage(nc, ["xmax", "spread", "x_ready", "gu_ready", "gu_kept", "sig_in", "sig_out", "o_int", "y_ready", "added", "own"], body)


def l1_ffn(nc, C):
    layer_norm(nc, C, C.HT)
    F = Core()
    with nc.sbuf_tensor("l1_w", [P, 9, E], F32) as F.W:
        l1_ffn_weights(nc, C, F)
        l1_ffn_body(nc, C, F)


LDEPTH, LH, LD, WIN = 6, 16, 64, 32
INNER = LH * LD
FI = int(E * 4 * 2 / 3)
FIT = [(0, 128), (128, 128), (256, FI - 256)]
KW = WIN + P
SH = 20
FRONT_ROUNDS = 10
HH = LH // 2


def local_attention(nc, C, L, layer):
    def body(loaded, tables, xs_ready, f_full, f_free, t1_ready, swapped, t2_ready, n2_summed, n2_ready, root_ready, rot_ready, s_ready, e_ready, x_ready, t_ready, pt_kept, o_ready,
             o_kept, w_full, w_free, v_moved, own_b, own_f, own_a, own_t):
        with ExitStack() as s:
            sb = sbuf(nc, s)
            scl = sb("scl", [P, 2, LD])
            scw = sb("scw", [P, 2, LD])
            base = sb("base", [P, 2, 2, 2, LD])
            TA = sb("TA", [P, 2, 2, LD])
            TB = sb("TB", [P, 2, 2, LD])
            win = sb("win", [P, 2, 2, KW], BF16)
            lnb = sb("lnb", [P, 1])
            xs = sb("xs", [P, S])
            qk = sb("qk", [P, 2, LH, LD])
            sq = sb("sqk", [P, 2, LH, LD])
            t1 = sb("t1", [P, 2, LH, LD])
            t2 = sb("t2", [P, 2, LH, LD])
            n2, ry, ry2, rt = (sb(n, [P, 2, 2, HH]) for n in ("n2", "ry", "ry2", "rt"))
            qT = sb("qTl", [P, 2, 8, P])
            kT = sb("kTl", [P, 2, 8, KW])
            VV = sb("VV", [P, 2, LH, LD + 1])
            VP = sb("VP", [WIN, LH, LD + 1])
            mx = sb("mxl", [P, 2, 2, 2])
            e = sb("el", [P, 2, 2, 2, KW])
            pO, pP = sb("pO", [P, 2, 4, P]), sb("pP", [WIN, 2, 4, P])
            rec = sb("recl", [P, 4])
            ob = sb("ob", [P, LH, LD])
            oT = sb("oTl", [P, 8, P])
            block = s.enter_context(nc.Block())
            SC = (C.psum[:, 2:4, :], C.psum[:, 4:6, :])
            bankO, bankW = C.ps[6], C.ps[7]
            Wqkv, Wo = L.Wqkv, L.Wo

            @block.sync
            def _(sp):
                wq = C.i["L2_ffn_Wqkv"][bass.ds(layer, 1), :, :].rearrange("o p n -> p (o n)")
                for k in range(3):
                    sp.dma_start(Wqkv[:, k * INNER:(k + 1) * INNER], wq[:, k * INNER:(k + 1) * INNER]).then_inc(loaded, 16)
                sp.dma_start(Wo[:, :, :], C.i["L2_ffn_Wo"][bass.ds(layer, 1), :, :].rearrange("o (g p) n -> p (o g) n", p=P)).then_inc(loaded, 16)
                sp.dma_start(base[:, :, :, :, :], C.c["rotary"]).then_inc(loaded, 16)
                sp.dma_start(win[:, :, :, :], C.c["window"]).then_inc(loaded, 16)
                H2 = LD // 2
                for n, name in enumerate("qk"):
                    v = C.i[f"L2_ffn_{name}_scale"][bass.ds(layer, 1), :]
                    sp.dma_start(scl[:, n, :], v.to_broadcast([P, LD])).then_inc(loaded, 16)
                    sp.dma_start(scw[:, n, 0:H2], v[:, H2:LD].to_broadcast([P, H2])).then_inc(loaded, 16)
                    sp.dma_start(scw[:, n, H2:LD], v[:, 0:H2].to_broadcast([P, H2])).then_inc(loaded, 16)

            @block.tensor
            def _(pe):
                pe.wait_ge(loaded, 16 * 12)

                def front(u, r, first, batches):
                    J, p = u
                    if not (first and r < 2):
                        pe.wait_ge(f_free, J * FRONT_ROUNDS + (r - 1))
                    if r == 0 and p == 0:
                        pe.wait_ge(xs_ready, batches)
                    F = C.ps[r % 2]
                    if r < 6:
                        kind, half = (r % 2, r // 2) if r < 4 else (2, r - 4)
                        w = kind * INNER + half * CH
                        mm = nc.tensor.matmul(F[:, :], xs[:, p * P:(p + 1) * P], Wqkv[:, w:w + CH], start=True, stop=True)
                    else:
                        kind, half = r % 2, (r - 6) // 2
                        if kind == 0:
                            pe.wait_ge(rot_ready, J * 2 + (half + 1))
                        for g in range(4):
                            h = HH * half + 2 * g
                            mm = nc.tensor.transpose(F[:, g * P:(g + 1) * P], t1[:, kind, h:h + 2, :].rearrange("p h d -> p (h d)"), C.ident[:, :])
                    mm.then_inc(f_full, 1)

                def scores(u, c, moved):
                    J, p = u
                    if c == 0:
                        pe.wait_ge(f_free, J * FRONT_ROUNDS + 8)
                        if p == 1:
                            pe.wait_ge(v_moved, moved)
                    if c == 2:
                        pe.wait_ge(f_free, J * FRONT_ROUNDS + 10)
                    if c >= 2:
                        pe.wait_ge(pt_kept, J * 4 + (c - 1))
                    for hh in range(2):
                        r = slice(64 * hh, 64 * hh + 64)
                        for x in range(2):
                            nc.tensor.matmul(SC[c % 2][:, hh, x * KW:(x + 1) * KW], qT[r, p, 2 * c + x, :], kT[r, p, 2 * c + x, :], start=(x == 0), stop=False, skip_group_check=True)
                    for hh in range(2):
                        mm = nc.tensor.matmul(SC[c % 2][:, hh, 0:2 * KW], C.identb[:, :], win[:, p, :, :].rearrange("p x k -> p (x k)"), start=False, stop=True, skip_group_check=True)
                    mm.then_inc(s_ready, 1)

                def turn_p(u, c):
                    J, p = u
                    pe.wait_ge(x_ready, J * 4 + (c + 1))
                    for hh in range(2):
                        for x in range(2):
                            k = 2 * x + hh
                            mm = nc.tensor.transpose(SC[c % 2][:, 0, k * P:(k + 1) * P], e[:, c % 2, hh, x, WIN:KW], C.ident[:, :])
                            if p == 1:
                                mm = nc.tensor.transpose(SC[c % 2][0:WIN, 1, k * P:(k + 1) * P], e[:, c % 2, hh, x, 0:WIN], C.ident[:, :])
                    mm.then_inc(t_ready, 1)

                def values(u, c, first):
                    J, p = u
                    pe.wait_ge(pt_kept, J * 4 + (c + 1))
                    if not (first and c == 0):
                        pe.wait_ge(o_kept, J * 4 + c)
                    for k in range(4):
                        h = 4 * c + k
                        out = bankO[:, k * (LD + 1):(k + 1) * (LD + 1)]
                        mm = nc.tensor.matmul(out, pO[:, c % 2, k, :], VV[:, p, h, :], start=True, stop=(p == 0), skip_group_check=True)
                        if p == 1:
                            mm = nc.tensor.matmul(out, pP[:, c % 2, k, :], VP[:, h, :], start=False, stop=True, skip_group_check=True)
                    mm.then_inc(o_ready, 1)

                def turn_o(u, half, first):
                    J, p = u
                    pe.wait_ge(o_kept, J * 4 + 2 * half + 2)
                    if not (first and half == 0):
                        pe.wait_ge(w_free, J * 3 + half)
                    for g in range(4):
                        mm = nc.tensor.transpose(bankW[:, g * P:(g + 1) * P], ob[:, 8 * half + 2 * g:8 * half + 2 * g + 2, :].rearrange("p h d -> p (h d)"), C.ident[:, :])
                    mm.then_inc(w_full, 1)

                def project(J):
                    pe.wait_ge(w_free, J * 3 + 2)
                    for g in range(8):
                        mm = nc.tensor.matmul(bankW[:, 0:P], Wo[:, g, :], oT[:, g, :], start=(g == 0), stop=(g == 7))
                    mm.then_inc(w_full, 1)

                def steps(bk, fr, batches, moved, first=False, before=True):
                    if bk is None:
                        for r in range(8):
                            front(fr, r, first, batches)
                        return
                    f = (lambda r: front(fr, r, False, batches)) if fr is not None else (lambda r: None)
                    scores(bk, 0, moved)
                    scores(bk, 1, moved)
                    front(bk, 8, False, batches)
                    front(bk, 9, False, batches)
                    f(0)
                    f(1)
                    turn_p(bk, 0)
                    if before:
                        project(bk[0] - 1)
                    turn_p(bk, 1)
                    values(bk, 0, not before)
                    scores(bk, 2, moved)
                    f(2)
                    f(3)
                    values(bk, 1, False)
                    scores(bk, 3, moved)
                    turn_p(bk, 2)
                    turn_o(bk, 0, not before)
                    f(4)
                    f(5)
                    values(bk, 2, False)
                    f(6)
                    turn_p(bk, 3)
                    f(7)
                    values(bk, 3, False)
                    turn_o(bk, 1, False)

                steps(None, (0, 0), 1, None, first=True)
                steps((0, 0), (1, 1), 1, None, before=False)
                steps((1, 1), (2, 0), 2, 1)
                with pe.Fori(1, B - 1) as b:
                    steps((b * 2, 0), (b * 2 + 1, 1), b + 1, None)
                    steps((b * 2 + 1, 1), (b * 2 + 2, 0), b + 2, b + 1)
                steps((2 * B - 2, 0), (2 * B - 1, 1), B, None)
                steps((2 * B - 1, 1), None, None, B)
                project(2 * B - 1)

            @block.vector
            def _(dve):
                nc.vector.memset(xs[64:P, 0:1], 0.0)
                nc.vector.memset(kT[:, 0, :, 0:WIN], 0.0)
                nc.vector.memset(VV[:, :, :, LD:LD + 1], 1.0)
                nc.vector.memset(lnb[:, :], 0.5 * SH * float(np.log(2.0))).then_inc(own_t, 1)
                dve.wait_ge(loaded, 16 * 12)
                for p in range(2):
                    nc.vector.tensor_tensor(TA[:, p, :, :], base[:, 0, p, :, :], scl[:, :, :], ALU.mult)
                    last = nc.vector.tensor_tensor(TB[:, p, :, :], base[:, 1, p, :, :], scw[:, :, :], ALU.mult)
                last.then_inc(tables, 1)

                def shift(b, first):
                    if not first:
                        dve.wait_ge(f_full, (b * 2 - 1) * FRONT_ROUNDS + 6)
                    nc.vector.tensor_copy(xs[0:64, :], C.XT[0:64, bass.ds(b * S, S)])
                    nc.vector.tensor_copy(xs[64:P, 1:S], C.XT[64:P, bass.ds(b * S, S - 1)]).then_inc(xs_ready, 1)

                def front_a(u, half):
                    J, p = u
                    H = slice(HH * half, HH * half + HH)
                    dve.wait_ge(f_free, J * FRONT_ROUNDS + (2 * half + 2))
                    nc.vector.tensor_reduce(n2[:, half, :, :], sq[:, :, H, :], AX.X, ALU.add).then_inc(n2_summed, 1)
                    nc.vector.tensor_tensor(t1[:, :, H, :], qk[:, :, H, :], TA[:, p, :, :].unsqueeze(2).to_broadcast([P, 2, HH, LD]), ALU.mult).then_inc(t1_ready, 1)
                    dve.wait_ge(n2_summed, J * 2 + (half + 1))
                    nc.vector.tensor_scalar(n2[:, half, :, :], n2[:, half, :, :], 1e-24, None, ALU.max).then_inc(n2_ready, 1)

                def front_scale(u, half, st):
                    J, p = u
                    H = slice(HH * half, HH * half + HH)
                    x = rt[:, half, :, :]
                    dve.wait_ge(root_ready, J * 2 + (half + 1))
                    dve.wait_ge(n2_ready, J * 2 + (half + 1))
                    st.then(nc.vector.tensor_tensor(x, n2[:, half, :, :], ry2[:, half, :, :], ALU.mult))
                    st.then(nc.vector.tensor_scalar(x, x, -0.5, 1.5, ALU.mult, ALU.add))
                    st.then(nc.vector.tensor_tensor(x, x, ry[:, half, :, :], ALU.mult))
                    dve.wait_ge(t2_ready, J * 2 + (half + 1))
                    nc.vector.tensor_tensor(t1[:, :, H, :], t1[:, :, H, :], x.unsqueeze(3).to_broadcast([P, 2, HH, LD]), ALU.mult).then_inc(rot_ready, 1)

                def centre(u, c, st):
                    J, p = u
                    dve.wait_ge(s_ready, J * 4 + (c + 1))
                    v = SC[c % 2][:, :, 0:2 * KW].rearrange("p a (x k) -> p a x k", x=2)
                    st.then(nc.vector.tensor_reduce(mx[:, c % 2, :, :], v, AX.X, ALU.max))
                    if c >= 2:
                        dve.wait_ge(t_ready, J * 4 + (c - 1))
                    for hh in range(2):
                        last = nc.vector.tensor_tensor(e[:, c % 2, hh, :, :], v[:, hh, :, :], mx[:, c % 2, hh, :].unsqueeze(2).to_broadcast([P, 2, KW]), ALU.subtract)
                    last.then_inc(e_ready, 1)

                def normalise(u, c, st):
                    J, p = u
                    dve.wait_ge(o_ready, J * 4 + (c + 1))
                    v = bankO[:, 0:4 * (LD + 1)].rearrange("p (k d) -> p k d", k=4)
                    st.then(nc.vector.reciprocal(rec[:, :], v[:, :, LD]))
                    nc.vector.tensor_tensor(ob[:, 4 * c:4 * c + 4, :], v[:, :, 0:LD], rec[:, :].unsqueeze(2).to_broadcast([P, 4, LD]), ALU.mult).then_inc(o_kept, 1)

                def residual(J):
                    dve.wait_ge(w_full, J * 3 + 3)
                    x = C.XT[:, bass.ds(J * P, P)] if not isinstance(J, int) else C.XT[:, J * P:(J + 1) * P]
                    nc.vector.tensor_tensor(x, x, bankW[:, 0:P], ALU.add).then_inc(w_free, 1)

                def steps(bk, fr, batch=None, first=False, prev=True):
                    if batch is not None:
                        shift(batch, first)
                    if fr is not None:
                        st = Steps(dve, own_f, fr[0] * 6)
                    if bk is None:
                        for half in range(2):
                            front_a(fr, half)
                        for half in range(2):
                            front_scale(fr, half, st)
                        return
                    sb_ = Steps(dve, own_b, bk[0] * 8)
                    centre(bk, 0, sb_)
                    centre(bk, 1, sb_)
                    if fr is not None:
                        front_a(fr, 0)
                    if prev:
                        residual(bk[0] - 1)
                    normalise(bk, 0, sb_)
                    centre(bk, 2, sb_)
                    normalise(bk, 1, sb_)
                    if fr is not None:
                        front_scale(fr, 0, st)
                    centre(bk, 3, sb_)
                    if fr is not None:
                        front_a(fr, 1)
                    normalise(bk, 2, sb_)
                    normalise(bk, 3, sb_)
                    if fr is not None:
                        front_scale(fr, 1, st)
                    assert sb_.n == 8

                dve.wait_ge(tables, 1)
                steps(None, (0, 0), 0, True)
                steps((0, 0), (1, 1), prev=False)
                steps((1, 1), (2, 0), 1)
                with dve.Fori(1, B - 1) as b:
                    steps((b * 2, 0), (b * 2 + 1, 1))
                    steps((b * 2 + 1, 1), (b * 2 + 2, 0), b + 1)
                steps((2 * B - 2, 0), (2 * B - 1, 1))
                steps((2 * B - 1, 1), None)
                residual(2 * B - 1)

            @block.gpsimd
            def _(pool):
                pool.wait_ge(tables, 1)

                def swap(u):
                    J, p = u
                    H2 = LD // 2
                    for half in range(2):
                        H = slice(HH * half, HH * half + HH)
                        pool.wait_ge(f_free, J * FRONT_ROUNDS + (2 * half + 2))
                        for d in range(2):
                            nc.gpsimd.tensor_tensor(t2[:, :, H, d * H2:(d + 1) * H2], qk[:, :, H, (1 - d) * H2:(2 - d) * H2],
                                                    TB[:, p, :, d * H2:(d + 1) * H2].unsqueeze(2).to_broadcast([P, 2, HH, H2]), ALU.mult).then_inc(swapped, 1)
                        pool.wait_ge(swapped, J * 4 + (2 * half + 2))
                        pool.wait_ge(t1_ready, J * 2 + (half + 1))
                        nc.gpsimd.tensor_tensor(t1[:, :, H, :], t1[:, :, H, :], t2[:, :, H, :], ALU.add).then_inc(t2_ready, 1)

                with pool.Fori(0, B) as b:
                    swap((b * 2, 0))
                    swap((b * 2 + 1, 1))

            @block.scalar
            def _(act):
                nc.scalar.preload_act_table_set(LN_EXP)
                act.wait_ge(own_t, 1)

                def keep_front(u, r, first):
                    J, p = u
                    act.wait_ge(f_full, J * FRONT_ROUNDS + (r + 1))
                    F = C.ps[r % 2]
                    heads = F.rearrange("p (h d) -> p h d", h=HH)
                    if r < 4:
                        kind, half = r % 2, r // 2
                        if kind == 0 and not first:
                            act.wait_ge(t2_ready, J * 2 + (half - 1))
                            act.wait_ge(rot_ready, J * 2 + (half - 1))
                        H = slice(HH * half, HH * half + HH)
                        nc.scalar.activation(qk[:, kind, H, :], heads, ACT.Copy)
                        nc.scalar.activation(sq[:, kind, H, :], heads, ACT.Square).then_inc(f_free, 1)
                    elif r < 6:
                        H = slice(HH * (r - 4), HH * (r - 4) + HH)
                        nc.scalar.activation(VV[:, p, H, 0:LD], heads, ACT.Copy).then_inc(f_free, 1)
                        if r == 5 and p == 1:
                            nc.scalar.activation(VP[:, :, :], VV[P - WIN:P, 0, :, :], ACT.Copy)
                            nc.scalar.activation(kT[:, 1, :, 0:WIN], kT[:, 0, :, P:KW], ACT.Copy).then_inc(v_moved, 1)
                    else:
                        kind, half = r % 2, (r - 6) // 2
                        G = slice(4 * half, 4 * half + 4)
                        dst = qT[:, p, G, :] if kind == 0 else kT[:, p, G, WIN:KW]
                        nc.scalar.activation(dst, F.rearrange("p (g q) -> p g q", g=4), ACT.Copy).then_inc(f_free, 1)

                def root(u, half):
                    J, p = u
                    act.wait_ge(n2_ready, J * 2 + (half + 1))
                    st = Steps(act, own_a, J * 4 + 2 * half)
                    st.then(nc.scalar.activation(ry2[:, half, :, :], n2[:, half, :, :], ACT.Ln, scale=float(2.0 ** SH)))
                    st.then(nc.scalar.activation(ry[:, half, :, :], ry2[:, half, :, :], ACT.Exp, scale=-0.5, bias=lnb[:, :]))
                    nc.scalar.activation(ry2[:, half, :, :], ry[:, half, :, :], ACT.Square).then_inc(root_ready, 1)

                def weights(u, c):
                    J, p = u
                    act.wait_ge(e_ready, J * 4 + (c + 1))
                    v = e[:, c % 2, :, :, :].rearrange("p a x k -> p (a x k)")
                    nc.scalar.activation(v, v, ACT.Exp, scale=8.0).then_inc(x_ready, 1)

                def keep_p(u, c):
                    J, p = u
                    act.wait_ge(t_ready, J * 4 + (c + 1))
                    if c >= 2:
                        act.wait_ge(o_ready, J * 4 + (c - 1))
                    if p == 1:
                        nc.scalar.activation(pP[:, c % 2, :, :].rearrange("p k q -> p (k q)"), SC[c % 2][0:WIN, 1, :], ACT.Copy)
                    nc.scalar.activation(pO[:, c % 2, :, :].rearrange("p k q -> p (k q)"), SC[c % 2][:, 0, :], ACT.Copy).then_inc(pt_kept, 1)

                def keep_o(u, half):
                    J, p = u
                    act.wait_ge(w_full, J * 3 + (half + 1))
                    nc.scalar.activation(oT[:, 4 * half:4 * half + 4, :].rearrange("p g q -> p (g q)"), bankW, ACT.Copy).then_inc(w_free, 1)

                def steps(bk, fr, first=False):
                    if bk is None:
                        for r in range(6):
                            keep_front(fr, r, first)
                        for half in range(2):
                            root(fr, half)
                        for r in range(6, 8):
                            keep_front(fr, r, first)
                        return
                    f = (lambda r: keep_front(fr, r, False)) if fr is not None else (lambda r: None)
                    weights(bk, 0)
                    keep_front(bk, 8, False)
                    keep_front(bk, 9, False)
                    weights(bk, 1)
                    f(0)
                    f(1)
                    keep_p(bk, 0)
                    keep_p(bk, 1)
                    if fr is not None:
                        root(fr, 0)
                    f(2)
                    weights(bk, 2)
                    f(3)
                    keep_p(bk, 2)
                    keep_o(bk, 0)
                    f(4)
                    weights(bk, 3)
                    f(5)
                    f(6)
                    keep_p(bk, 3)
                    f(7)
                    if fr is not None:
                        root(fr, 1)
                    keep_o(bk, 1)

                steps(None, (0, 0), True)
                with act.Fori(0, B - 1) as b:
                    steps((b * 2, 0), (b * 2 + 1, 1))
                    steps((b * 2 + 1, 1), (b * 2 + 2, 0))
                steps((2 * B - 2, 0), (2 * B - 1, 1))
                steps((2 * B - 1, 1), None)
    run_stage(nc, ["loaded", "tables", "xs_ready", "f_full", "f_free", "t1_ready", "swapped", "t2_ready", "n2_summed", "n2_ready", "root_ready", "rot_ready", "s_ready", "e_ready", "x_ready", "t_ready",
                   "pt_kept", "o_ready", "o_kept", "w_full", "w_free", "v_moved", "own_b", "own_f", "own_a", "own_t"], body)


def geglu_prepare(nc, C, L, layer):
    def body(loaded):
        with nc.Block() as block:
            @block.sync
            def _(sp):
                one = lambda name: C.i[f"L2_ffn_{name}"][bass.ds(layer, 1)]
                sp.dma_start(L.W1[:, :], one("W1").rearrange("o p n -> p (o n)")).then_inc(loaded, 16)
                for t, (i0, n) in enumerate(FIT):
                    sp.dma_start(L.W2[0:n, t, :], one("W2")[:, i0:i0 + n, :].rearrange("o p n -> p (o n)")).then_inc(loaded, 16)
                    for a in range(2):
                        sp.dma_start(L.b1[0:n, a, t:t + 1], one("b1")[:, a * FI + i0:a * FI + i0 + n].rearrange("o p -> p o")).then_inc(loaded, 16)
                for k, name in enumerate(("b2", "ln_g", "ln_b")):
                    sp.dma_start(L.cols[:, k:k + 1], one(name).rearrange("o p -> p o")).then_inc(loaded, 16)
                sp.wait_ge(loaded, 16 * 13)

            @block.vector
            def _(dve):
                v = lambda t: t[64:P, :].rearrange("p (b s) -> p b s", b=B)
                nc.vector.memset(v(L.XS)[:, :, 0:1], 0.0)
                nc.vector.tensor_copy(L.XS[0:64, :], C.XT[0:64, :])
                nc.vector.tensor_copy(v(L.XS)[:, :, 1:S], v(C.XT)[:, :, 0:S - 1])
    run_stage(nc, ["loaded"], body)


def geglu(nc, C, L):
    def body(a_ready, g_ready, gelu_ready, h_ready, y_ready, added):
        with ExitStack() as s:
            sb = sbuf(nc, s)
            ge = sb("ge", [P, 2, CH])
            hb = sb("hbg", [P, 2, 3, CH])
            block = s.enter_context(nc.Block())
            jobs = [(q, t) for q in range(2) for t in range(3)]

            @block.tensor
            def _(pe):
                with pe.Fori(0, NCH // 2) as i:
                    for j, (q, t) in enumerate(jobs):
                        i0, n = FIT[t]
                        if j >= 2:
                            pe.wait_ge(h_ready, i * 6 + (j - 1))
                        x = C.HT[:, bass.ds(i * (2 * CH) + q * CH, CH)]
                        nc.tensor.matmul(C.ps[j % 2][0:n, :], L.W1[:, FI + i0:FI + i0 + n], x, start=True, stop=True).then_inc(g_ready, 1)
                        nc.tensor.matmul(C.ps[2 + j % 2][0:n, :], L.W1[:, i0:i0 + n], x, start=True, stop=True).then_inc(a_ready, 1)
                    for q in range(2):
                        for t, (i0, n) in enumerate(FIT):
                            pe.wait_ge(h_ready, i * 6 + (3 * q + t + 1))
                            mm = nc.tensor.matmul(C.ps[4 + q][:, :], L.W2[0:n, t, :], hb[0:n, q, t, :], start=(t == 0), stop=(t == 2))
                        mm.then_inc(y_ready, 1)
                    pe.wait_ge(added, i * 2 + 2)

            @block.scalar
            def _(act):
                with act.Fori(0, NCH // 2) as i:
                    for j, (q, t) in enumerate(jobs):
                        n = FIT[t][1]
                        act.wait_ge(g_ready, i * 6 + (j + 1))
                        nc.scalar.activation(ge[0:n, j % 2, :], C.ps[j % 2][0:n, :], ACT.Gelu, bias=L.b1[0:n, 1, t:t + 1]).then_inc(gelu_ready, 1)

            @block.vector
            def _(dve):
                with dve.Fori(0, NCH // 2) as i:
                    for j, (q, t) in enumerate(jobs):
                        n = FIT[t][1]
                        dve.wait_ge(gelu_ready, i * 6 + (j + 1))
                        dve.wait_ge(a_ready, i * 6 + (j + 1))
                        nc.vector.scalar_tensor_tensor(hb[0:n, q, t, :], C.ps[2 + j % 2][0:n, :], L.b1[0:n, 0, t:t + 1], ge[0:n, j % 2, :], ALU.add, ALU.mult).then_inc(h_ready, 1)
                    for q in range(2):
                        dve.wait_ge(y_ready, i * 2 + (q + 1))
                        x = C.XT[:, bass.ds(i * (2 * CH) + q * CH, CH)]
                        nc.vector.scalar_tensor_tensor(x, C.ps[4 + q][:, :], L.cols[:, 0:1], x, ALU.add, ALU.add).then_inc(added, 1)
    run_stage(nc, ["a_ready", "g_ready", "gelu_ready", "h_ready", "y_ready", "added"], body)


def l2_ffn(nc, C):
    L = Core()
    with ExitStack() as s:
        sb = sbuf(nc, s)
        L.Wqkv, L.Wo = sb("Wqkv", [P, 3 * INNER]), sb("Wo", [P, 8, P])
        L.W1, L.W2, L.b1, L.cols = sb("W1", [P, 2 * FI]), sb("W2", [P, 3, P]), sb("b1", [P, 2, 3]), sb("cols", [P, 3])
        L.XS = sb("XS", [P, TOK])
        L.X0 = sb("X0", [P, TOK])
        keep_input(nc, C, L.X0)
        layer_norm(nc, C, C.XT, src=L.X0)
        with nc.Fori(0, LDEPTH) as layer:
            local_attention(nc, C, L, layer)
            geglu_prepare(nc, C, L, layer)
            layer_norm(nc, C, C.HT, gain=L.cols[:, 1:2], shift=L.cols[:, 2:3], src=L.XS)
            geglu(nc, C, L)
        add_input(nc, C, L.X0)


def keep_input(nc, C, X0, columns=()):
    def body(kept, loaded):
        with nc.Block() as block:
            @block.sync
            def _(sp):
                for dst, src in columns:
                    sp.dma_start(dst, src.unsqueeze(1)).then_inc(loaded, 16)
                if columns:
                    sp.wait_ge(loaded, 16 * len(columns))

            @block.vector
            def _(dve):
                nc.vector.tensor_copy(X0[:, :], C.XT[:, :]).then_inc(kept, 1)
    run_stage(nc, ["kept", "loaded"], body)


def add_input(nc, C, X0):
    def body(added):
        with nc.Block() as block:
            @block.vector
            def _(dve):
                nc.vector.tensor_tensor(C.XT[:, :], C.XT[:, :], X0[:, :], ALU.add).then_inc(added, 1)
    run_stage(nc, ["added"], body)


def rotary_tables():
    half = np.arange(0, LD, 2, dtype=np.float32)
    inv_freq = (1.0 / 10000.0 ** (half.astype(np.float64) / LD)).astype(np.float32)
    t = np.arange(S, dtype=np.float32)
    f = t[:, None] * inv_freq[None, :]
    f = np.concatenate([f, f], -1).astype(np.float64)
    bs = (half.astype(np.float64) + 0.4 * LD) / (1.4 * LD)
    sc = bs[None, :] ** ((t.astype(np.float64) - S // 2) / (WIN // 2))[:, None]
    sc = np.concatenate([sc, sc], -1)
    sign = np.where(np.arange(LD) < LD // 2, -1.0, 1.0)[None, :]
    out = np.zeros((P, 2, 2, 2, LD), np.float32)
    for tile in range(2):
        r = slice(tile * P, (tile + 1) * P)
        for a, m in enumerate((sc, 1.0 / sc)):
            out[:, 0, tile, a, :] = (np.cos(f) * m)[r]
            out[:, 1, tile, a, :] = (np.sin(f) * sign * m)[r]
    return out


def window_mask():
    q, k = np.arange(P)[:, None], np.arange(KW)[None, :] - WIN
    out = np.zeros((P, 2, 2, KW), np.float32)
    for tile in range(2):
        seen = (k <= q) & (q <= k + WIN) & ((k >= 0) | (tile == 1))
        out[:, tile, :, :] = np.where(seen, 0.0, NEG)[:, None, :]
    return out


NEXP = 4
DFF = 4 * E
FT = DFF // P


def l3f_qkv(nc, C, A):
    def body(loaded, prepared, conv_ready, qk_ready, qk_kept, v_ready, v_kept, own):
        with ExitStack() as s:
            sb = sbuf(nc, s)
            cw, ta = sb("cw", [P, 3]), sb("ta", [P, 2, CH])
            aw = sb("aw", [P, 3, E])
            asw = sb("asw", [P, 2, E])
            rope = sb("rope", [P, 2, S])
            CV = sb("CV", [P, TOK])
            block = s.enter_context(nc.Block())
            jobs = [(n, c) for c in range(NCH) for n in range(2)]

            @block.sync
            def _(sp):
                sp.dma_start(cw[:, :], C.i["L3_ffn_conv_w"].rearrange("c o k -> c (o k)")).then_inc(loaded, 16)
                sp.dma_start(aw[:, :, :], C.i["L3_ffn_attn_w"].rearrange("c (n e) -> c n e", n=3)).then_inc(loaded, 16)
                sp.dma_start(rope[:, :, :], C.c["rope8"]).then_inc(loaded, 16)
                sp.dma_start(A.wo, C.i["L3_ffn_proj_w"]).then_inc(loaded, 16)
                sp.dma_start(A.MQ[:, :, :], C.c["causal_q"]).then_inc(loaded, 16)
                sp.dma_start(A.MK[:, :, :], C.c["causal_k"]).then_inc(loaded, 16)

            @block.vector
            def _(dve):
                st = Steps(dve, own)
                nc.vector.memset(A.bo, 0.0)
                nc.vector.memset(A.VA4[:, :, :, HD:HD + 1], 1.0)
                dve.wait_ge(loaded, 96)
                H2 = HD // 2
                for n in range(2):
                    w = aw[:, n, :].rearrange("p (h d) -> p h d", h=NH)
                    o = asw[:, n, :].rearrange("p (h d) -> p h d", h=NH)
                    nc.vector.tensor_scalar(o[:, :, 0:H2], w[:, :, H2:HD], -1.0, None, ALU.mult)
                    last = nc.vector.tensor_copy(o[:, :, H2:HD], w[:, :, 0:H2])
                last.then_inc(prepared, 1)
                st.then(nc.vector.tensor_scalar(CV[:, :], C.HT[:, :], cw[:, 2:3], None, ALU.mult))
                for k in (1, 2):
                    for b in range(B):
                        o = CV[:, b * S + k:(b + 1) * S]
                        last = nc.vector.scalar_tensor_tensor(o, C.HT[:, b * S:(b + 1) * S - k], cw[:, 2 - k:3 - k], o, ALU.mult, ALU.add)
                    if k == 1:
                        st.then(last)
                last.then_inc(conv_ready, 1)
                for j, (n, c) in enumerate(jobs):
                    dve.wait_ge(qk_ready, j + 1)
                    bs = lambda a: a.rearrange("p (b s) -> p b s", s=S)
                    tab = lambda k: rope[:, k, :].unsqueeze(1).to_broadcast([P, 2, S])
                    dst = (A.QT, A.KT)[n][:, c * CH:(c + 1) * CH]
                    nc.vector.tensor_tensor(bs(dst), bs(C.ps[2 * n][:, :]), tab(0), ALU.mult)
                    st.then(nc.vector.tensor_tensor(bs(ta[:, n, :]), bs(C.ps[2 * n + 1][:, :]), tab(1), ALU.mult))
                    nc.vector.tensor_tensor(dst, dst, ta[:, n, :], ALU.add).then_inc(qk_kept, 1)
                for q in range(4):
                    dve.wait_ge(v_ready, q + 1)
                    nc.vector.tensor_copy(A.VA4[:, 4 * q:4 * q + 4, :, 0:HD], C.ps[4 + q][:, :].rearrange("p (t h d) -> p t h d", t=4, h=NH)).then_inc(v_kept, 1)

            @block.tensor
            def _(pe):
                pe.wait_ge(loaded, 96)
                pe.wait_ge(prepared, 1)
                pe.wait_ge(conv_ready, 1)
                for j, (n, c) in enumerate(jobs):
                    if j >= 2:
                        pe.wait_ge(qk_kept, j - 1)
                    x = CV[:, c * CH:(c + 1) * CH]
                    nc.tensor.matmul(C.ps[2 * n][:, :], aw[:, n, :], x, start=True, stop=True)
                    nc.tensor.matmul(C.ps[2 * n + 1][:, :], asw[:, n, :], x, start=True, stop=True).then_inc(qk_ready, 1)
                for q in range(4):
                    for t in range(4):
                        n = 4 * q + t
                        mm = nc.tensor.matmul(C.ps[4 + q][:, t * P:(t + 1) * P], CV[:, n * P:(n + 1) * P], aw[:, 2, :], start=True, stop=True)
                    mm.then_inc(v_ready, 1)
    run_stage(nc, ["loaded", "prepared", "conv_ready", "qk_ready", "qk_kept", "v_ready", "v_kept", "own"], body)


def moe_prepare(nc, C, M):
    def body(loaded, routed, own):
        with ExitStack() as s:
            sb = sbuf(nc, s)
            rw = sb("rw", [P, NEXP])
            lg, eq = sb("lg", [P, NT, NEXP]), sb("eq", [P, NT, NEXP])
            mx, free = sb("mxr", [P, NT]), sb("free", [P, NT])
            block = s.enter_context(nc.Block())

            @block.sync
            def _(sp):
                sp.dma_start(rw[:, :], C.i["L3_ffn_router_w"]).then_inc(loaded, 16)
                for e in range(NEXP):
                    sp.dma_start(M.WV[:, e, :], C.i["L3_ffn_expert_wv"][e]).then_inc(loaded, 16)
                    sp.dma_start(M.WP[:, e, :, :], C.i["L3_ffn_expert_proj"][e].rearrange("(t p) n -> p t n", p=P)).then_inc(loaded, 16)
                sp.wait_ge(loaded, 16 * 9)

            @block.tensor
            def _(pe):
                pe.wait_ge(loaded, 16 * 9)
                for t in range(NT):
                    mm = nc.tensor.matmul(C.ps[0][:, t * NEXP:(t + 1) * NEXP], C.HT[:, t * P:(t + 1) * P], rw[:, :], start=(t == 0), stop=True, skip_group_check=True)
                mm.then_inc(routed, 1)

            @block.vector
            def _(dve):
                st = Steps(dve, own)
                dve.wait_ge(routed, 1)
                st.then(nc.vector.tensor_copy(lg[:, :, :].rearrange("p t e -> p (t e)"), C.ps[0][:, 0:NT * NEXP]))
                st.then(nc.vector.tensor_reduce(mx[:, :], lg[:, :, :], AX.X, ALU.max))
                st.then(nc.vector.tensor_tensor(eq[:, :, :], lg[:, :, :], mx[:, :].unsqueeze(2).to_broadcast([P, NT, NEXP]), ALU.is_equal))
                st.then(nc.vector.tensor_scalar(free[:, :], eq[:, :, 0], -1.0, 1.0, ALU.mult, ALU.add))
                nc.vector.tensor_copy(M.pick[:, :, 0], eq[:, :, 0])
                for e in range(1, NEXP):
                    st.then(nc.vector.tensor_tensor(M.pick[:, :, e], eq[:, :, e], free[:, :], ALU.mult))
                    st.then(nc.vector.tensor_tensor(free[:, :], free[:, :], M.pick[:, :, e], ALU.subtract))
    run_stage(nc, ["loaded", "routed", "own"], body)


def moe_experts(nc, C, M):
    NJ = NEXP * FT
    def body(g_ready, v_ready, silu_ready, h_ready, y_ready, y_kept, turned, added, own):
        with ExitStack() as s:
            sb = sbuf(nc, s)
            sg = sb("sgm", [P, 2, CH])
            hb = sb("hbm", [P, 2, FT, CH])
            acc = sb("accm", [P, 4, E])
            pick = sb("pickc", [P, 4, NEXP])
            block = s.enter_context(nc.Block())
            jobs = [(e, t) for e in range(NEXP) for t in range(FT)]

            @block.tensor
            def _(pe):
                with pe.Fori(0, NCH) as i:
                    def down(e):
                        pe.wait_ge(h_ready, i * NJ + FT * (e + 1))
                        if e >= 2:
                            pe.wait_ge(y_kept, i * NEXP + (e - 1))
                        for k in range(4):
                            for t in range(FT):
                                mm = nc.tensor.matmul(C.ps[4 + e % 2][:, k * P:(k + 1) * P], hb[:, e % 2, t, k * P:(k + 1) * P], M.WP[:, e, t, :], start=(t == 0), stop=(t == FT - 1), skip_group_check=True)
                        mm.then_inc(y_ready, 1)
                    x = C.HT[:, bass.ds(i * CH, CH)]
                    for j, (e, t) in enumerate(jobs):
                        if j >= 2:
                            pe.wait_ge(h_ready, i * NJ + (j - 1))
                        nc.tensor.matmul(C.ps[j % 2][:, :], M.WV[:, e, t * P:(t + 1) * P], x, start=True, stop=True).then_inc(g_ready, 1)
                        nc.tensor.matmul(C.ps[2 + j % 2][:, :], M.WV[:, e, DFF + t * P:DFF + (t + 1) * P], x, start=True, stop=True).then_inc(v_ready, 1)
                        if t == 1 and e >= 1:
                            down(e - 1)
                    down(NEXP - 1)
                    pe.wait_ge(y_kept, i * NEXP + NEXP)
                    for k in range(4):
                        mm = nc.tensor.transpose(C.ps[6][:, k * P:(k + 1) * P], acc[:, k, :], C.ident[:, :])
                    mm.then_inc(turned, 1)

            @block.scalar
            def _(act):
                with act.Fori(0, NCH) as i:
                    for j, (e, t) in enumerate(jobs):
                        act.wait_ge(g_ready, i * NJ + (j + 1))
                        nc.scalar.activation(sg[:, j % 2, :], C.ps[j % 2][:, :], ACT.Silu).then_inc(silu_ready, 1)

            @block.vector
            def _(dve):
                with dve.Fori(0, NCH) as i:
                    st = Steps(dve, own, i)

                    def keep(e):
                        dve.wait_ge(y_ready, i * NEXP + (e + 1))
                        for k in range(4):
                            y = C.ps[4 + e % 2][:, k * P:(k + 1) * P]
                            if e == 0:
                                last = nc.vector.tensor_scalar(acc[:, k, :], y, pick[:, k, e:e + 1], None, ALU.mult)
                            else:
                                last = nc.vector.scalar_tensor_tensor(acc[:, k, :], y, pick[:, k, e:e + 1], acc[:, k, :], ALU.mult, ALU.add)
                        last.then_inc(y_kept, 1)
                        dve.wait_ge(y_kept, i * NEXP + (e + 1))

                    st.then(nc.vector.tensor_copy(pick[:, :, :], M.pick[:, bass.ds(i * 4, 4), :]))
                    for j, (e, t) in enumerate(jobs):
                        dve.wait_ge(silu_ready, i * NJ + (j + 1))
                        dve.wait_ge(v_ready, i * NJ + (j + 1))
                        nc.vector.tensor_tensor(hb[:, e % 2, t, :], C.ps[2 + j % 2][:, :], sg[:, j % 2, :], ALU.mult).then_inc(h_ready, 1)
                        if t == 2 and e >= 1:
                            keep(e - 1)
                    keep(NEXP - 1)
                    dve.wait_ge(turned, i + 1)
                    xx = C.XT[:, bass.ds(i * CH, CH)]
                    nc.vector.tensor_tensor(xx, xx, C.ps[6][:, :], ALU.add).then_inc(added, 1)
    run_stage(nc, ["g_ready", "v_ready", "silu_ready", "h_ready", "y_ready", "y_kept", "turned", "added", "own"], body)


def l3_ffn(nc, C):
    with ExitStack() as s0:
        X0 = sbuf(nc, s0)("X0", [P, TOK])
        cols = sbuf(nc, s0)("ln_cols", [P, 4])
        keep_input(nc, C, X0, [(cols[:, k:k + 1], C.i[f"L3_ffn_{n}"]) for k, n in enumerate(("ln1_w", "ln1_b", "ln2_w", "ln2_b"))])
        layer_norm(nc, C, C.XT, src=X0)
        layer_norm(nc, C, C.HT, gain=cols[:, 0:1], shift=cols[:, 1:2])
        A = Core()
        with ExitStack() as s:
            sb = sbuf(nc, s)
            wo_t, bo_t = sb("wo_t", [P, E]), sb("bo_t", [P, 1])
            A.wo, A.bo = wo_t[:, :], bo_t[:, :]
            A.MQ, A.MK = sb("MQc", [P, 2, S], BF16), sb("MKc", [P, 2, S], BF16)
            VA = sb("VA", [P, NT, NH * (HD + 1)])
            A.VA, A.VA4 = VA, VA[:, :, :].rearrange("p n (h e) -> p n h e", h=NH)
            with ExitStack() as s2:
                A.QT, A.KT = sbuf(nc, s2)("QT", [P, TOK]), sbuf(nc, s2)("KT", [P, TOK])
                l3f_qkv(nc, C, A)
                split_parts(nc, C, A, A.QT, A.KT)
            A.scale = float(HD) ** -0.5
            A.key_mask = None
            flat = lambda m: m[:, :, :].rearrange("p t s -> p (t s)")
            A.masks = [(lambda b: flat(A.MQ), lambda b: flat(A.MK))]
            attend(nc, C, A)
        layer_norm(nc, C, C.HT, gain=cols[:, 2:3], shift=cols[:, 3:4])
        with ExitStack() as s:
            sb = sbuf(nc, s)
            M = Core()
            M.WV, M.WP, M.pick = sb("WV", [P, NEXP, 2 * DFF]), sb("WP", [P, NEXP, FT, E]), sb("pick", [P, NT, NEXP])
            moe_prepare(nc, C, M)
            moe_experts(nc, C, M)
        add_input(nc, C, X0)


def rope_rows():
    inv_freq = (1.0 / 10000.0 ** (np.arange(0, HD, 2, dtype=np.float64) / HD)).astype(np.float32)
    f = np.arange(S, dtype=np.float32)[:, None] * inv_freq[None, :]
    f = np.tile(np.concatenate([f, f], -1).astype(np.float64).T, (NH, 1))
    return np.ascontiguousarray(np.stack([np.cos(f), np.sin(f)], 1).astype(np.float32))


def causal_masks():
    hidden = np.where(np.arange(S)[None, :] > np.arange(S)[:, None], NEG, 0.0)
    rows = lambda m: np.ascontiguousarray(m.reshape(2, P, S).transpose(1, 0, 2))
    return rows(hidden), rows(hidden.T)


def program(nc, ins, consts, out, stages):
    C = Core()
    C.i, C.c, C.out = ins, consts, out
    with ExitStack() as ctx:
        def sb(name, shape, dt=F32):
            return ctx.enter_context(nc.sbuf_tensor(name, shape, dt))
        C.psum = ctx.enter_context(nc.psum_tensor("psum", [P, 8, 512], F32))
        C.ps = [C.psum[:, n, :] for n in range(8)]
        C.ident = sb("ident", [P, P])
        C.identb = sb("identb", [P, P], BF16)
        C.mean_w = sb("mean_w", [P, P])
        C.eps = sb("eps", [P, 1])
        C.one = sb("one", [P, 1])
        C.XT = sb("XT", [P, TOK])
        C.CT = sb("CT", [P, TOK])
        C.CN = sb("CN", [P, NT, E])
        C.HT = sb("HT", [P, TOK])
        C.qk_parts = nc.dram_tensor("qk_parts", (2, 3, P, TOK), BF16, kind="Internal").ap()
        C.key_bias = nc.dram_tensor("key_bias", (B, S), BF16, kind="Internal").ap()
        load_inputs(nc, C)
        for stage in stages:
            stage(nc, C)
        store_output(nc, C, C.XT)


STAGES = [l0_xattn, l0_ffn, l1_xattn, l1_ffn, l2_xattn, l2_ffn, l3_xattn, l3_ffn]


def constants():
    ident = np.eye(P, dtype=np.float32)
    bf16 = mybir.dt.np(BF16)
    key, query = np.arange(P)[:, None], np.arange(P)[None, :]
    return {
        "ident": ident, "identb": ident.astype(bf16),
        "causal_kq": np.where(key > query, NEG, 0.0).astype(bf16),
        "rotary": rotary_tables(), "window": window_mask().astype(bf16),
        "rope8": rope_rows(), "causal_q": causal_masks()[0].astype(bf16), "causal_k": causal_masks()[1].astype(bf16),
        "head_blocks": np.kron(np.eye(NH), np.ones((HD, HD))).astype(np.float32),
        "max_rows": np.ascontiguousarray(np.repeat(np.tile(np.eye(NH), (3, 1))[:, :, None], P, 2).astype(bf16)),
        "head_rows": np.ascontiguousarray(np.repeat(np.eye(L0_NH, dtype=np.float32)[:, :, None], P, 2)),
    }


def build(nc, inputs, stages):
    arrays, ins, consts = {}, {}, {}
    for group, values in ((ins, inputs), (consts, constants())):
        for name, a in values.items():
            a = np.ascontiguousarray(a)
            arrays[f"in_{name}_dram"] = a
            group[name] = nc.dram_tensor(f"in_{name}_dram", a.shape, mybir.dt.from_np(a.dtype), kind="ExternalInput").ap()
    out = nc.dram_tensor("out_0_dram", (B, S, E), F32, kind="ExternalOutput").ap()
    program(nc, ins, consts, out, [STAGES[n] for n in stages])
    return arrays, out


def kernel(**inputs):
    import concourse.bacc as bacc
    from concourse.bass_utils import run_bass_kernel_spmd

    nc = bacc.Bacc("TRN2", target_bir_lowering=False, num_devices=1)
    arrays, _ = build(nc, {name: np.asarray(a) for name, a in inputs.items()}, range(len(STAGES)))
    r = run_bass_kernel_spmd(nc, [arrays], core_ids=[0])
    return np.asarray(r.results[0]["out_0_dram"])
```

```python
from contextlib import ExitStack

import numpy as np

import concourse.bass as bass
from concourse import mybir

ALU = mybir.AluOpType
ACT = mybir.ActivationFunctionType
F32 = mybir.dt.float32
BF16 = mybir.dt.bfloat16
I32 = mybir.dt.int32
AX = mybir.AxisListType

P = 128
B, S, E = 8, 256, 128
TOK = B * S
NT = TOK // P
CH = 512
NCH = TOK // CH
LN_EPS = 1e-5


class Steps:

    def __init__(self, eng, sem, base=0):
        self.eng, self.sem, self.base, self.n = eng, sem, base, 0

    def then(self, ins):
        self.n += 1
        ins.then_inc(self.sem, 1)
        self.eng.wait_ge(self.sem, self.base + self.n)


class Core:
    pass


def sbuf(nc, stack):
    return lambda name, shape, dt=F32: stack.enter_context(nc.sbuf_tensor(f"{name}_{nc.next_id()}", shape, dt))


def run_stage(nc, names, body):
    with ExitStack() as ctx:
        handles = [ctx.enter_context(nc.semaphore(f"{n}_{nc.next_id()}")) for n in names]
        body(*handles)
        nums = sorted(h.num for h in handles)
        first = nums[0]
        for n, after in zip(nums, nums[1:] + [None]):
            if after != n + 1:
                nc.gpsimd.sem_clear(range(first, n + 1))
                first = after
        nc.all_engine_barrier()


def load_inputs(nc, C):
    def body(loaded, turned, kept):
        with nc.sbuf_tensor("x_rows", [P, NT, E], F32) as x_rows, nc.Block() as block:
            @block.sync
            def _(sp):
                sp.dma_start(C.ident[:, :], C.c["ident"]).then_inc(loaded, 16)
                sp.dma_start(C.identb[:, :], C.c["identb"]).then_inc(loaded, 16)
                sp.dma_start(x_rows[:, :, :], C.i["x"].rearrange("b (h p) d -> p (b h) d", p=P)).then_inc(loaded, 16)
                sp.dma_start(C.CN[:, :, :], C.i["ctx_1024"].rearrange("b (h p) d -> p (b h) d", p=P)).then_inc(loaded, 16)

            @block.tensor
            def _(pe):
                pe.wait_ge(loaded, 64)
                for n, src in enumerate((x_rows, C.CN)):
                    for t in range(NT):
                        last = nc.tensor.transpose(C.ps[n * 4 + t // 4][:, (t % 4) * P:(t % 4 + 1) * P], src[:, t, :], C.ident[:, :])
                        if t % 4 == 3:
                            last.then_inc(turned, 1)

            @block.vector
            def _(dve):
                nc.vector.memset(C.mean_w[:, :], 1.0 / E)
                nc.vector.memset(C.eps[:, :], LN_EPS)
                nc.vector.memset(C.one[:, :], 1.0)
                for q in range(8):
                    dve.wait_ge(turned, q + 1)
                    dst = C.XT if q < 4 else C.CT
                    nc.vector.tensor_copy(dst[:, (q % 4) * CH:(q % 4 + 1) * CH], C.ps[q][:, :]).then_inc(kept, 1)
    run_stage(nc, ["loaded", "turned", "kept"], body)


def layer_norm(nc, C, HT, gain=None, shift=None, src=None):
    src = C.XT if src is None else src

    def body(mean_ready, centred, squared, var_ready, logs, y_ready, root_ready, scaled, off_one, halved, corrected, added, normed):
        with ExitStack() as s:
            sb = sbuf(nc, s)
            xc, sq, y, y2, ln, tt = (sb(n, [P, NCH, CH]) for n in ("xc", "sq", "y", "y2", "ln", "tt"))
            block = s.enter_context(nc.Block())
            cols = lambda c: slice(c * CH, (c + 1) * CH)
            pairs = [(c, c + 1) for c in range(0, NCH, 2)]

            @block.tensor
            def _(pe):
                for c in range(NCH):
                    nc.tensor.matmul(C.ps[c][:, :], C.mean_w[:, :], src[:, cols(c)], start=True, stop=True).then_inc(mean_ready, 1)
                for c in range(NCH):
                    pe.wait_ge(squared, c + 1)
                    nc.tensor.matmul(C.ps[NCH + c][:, :], C.mean_w[:, :], sq[:, c, :], start=True, stop=True).then_inc(var_ready, 1)

            @block.vector
            def _(dve):
                for c in range(NCH):
                    dve.wait_ge(mean_ready, c + 1)
                    nc.vector.tensor_tensor(xc[:, c, :], src[:, cols(c)], C.ps[c][:, :], ALU.subtract).then_inc(centred, 1)
                for pair in pairs:
                    for c in pair:
                        dve.wait_ge(root_ready, c + 1)
                        nc.vector.scalar_tensor_tensor(tt[:, c, :], C.ps[NCH + c][:, :], LN_EPS, y2[:, c, :], ALU.add, ALU.mult).then_inc(off_one, 1)
                    for c in pair:
                        dve.wait_ge(off_one, c + 1)
                        nc.vector.tensor_scalar(tt[:, c, :], tt[:, c, :], -0.5, 0.5, ALU.mult, ALU.add).then_inc(halved, 1)
                    for c in pair:
                        dve.wait_ge(scaled, c + 1)
                        dve.wait_ge(halved, c + 1)
                        nc.vector.tensor_tensor(tt[:, c, :], xc[:, c, :], tt[:, c, :], ALU.mult).then_inc(corrected, 1)
                    for c in pair:
                        dve.wait_ge(corrected, c + 1)
                        if gain is None:
                            nc.vector.tensor_tensor(HT[:, cols(c)], xc[:, c, :], tt[:, c, :], ALU.add).then_inc(normed, 1)
                        else:
                            nc.vector.tensor_tensor(xc[:, c, :], xc[:, c, :], tt[:, c, :], ALU.add).then_inc(added, 1)
                    if gain is not None:
                        for c in pair:
                            dve.wait_ge(added, c + 1)
                            nc.vector.tensor_scalar(HT[:, cols(c)], xc[:, c, :], gain, shift, ALU.mult, ALU.add).then_inc(normed, 1)

            @block.gpsimd
            def _(pool):
                for c in range(NCH):
                    pool.wait_ge(y_ready, c + 1)
                    nc.gpsimd.tensor_tensor(xc[:, c, :], xc[:, c, :], y[:, c, :], ALU.mult).then_inc(scaled, 1)

            @block.scalar
            def _(act):
                nc.scalar.preload_act_table_set(LN_EXP)
                for c in range(NCH):
                    act.wait_ge(centred, c + 1)
                    nc.scalar.activation(sq[:, c, :], xc[:, c, :], ACT.Square).then_inc(squared, 1)
                for pair in pairs:
                    for c in pair:
                        act.wait_ge(var_ready, c + 1)
                        nc.scalar.activation(ln[:, c, :], C.ps[NCH + c][:, :], ACT.Ln, bias=C.eps[:, :]).then_inc(logs, 1)
                    for c in pair:
                        act.wait_ge(logs, c + 1)
                        nc.scalar.activation(y[:, c, :], ln[:, c, :], ACT.Exp, scale=-0.5).then_inc(y_ready, 1)
                    for c in pair:
                        act.wait_ge(y_ready, c + 1)
                        nc.scalar.activation(y2[:, c, :], y[:, c, :], ACT.Square).then_inc(root_ready, 1)
    run_stage(nc, ["mean_ready", "centred", "squared", "var_ready", "logs", "y_ready", "root_ready", "scaled", "off_one", "halved", "corrected", "added", "normed"], body)


def store_output(nc, C, src):
    def body(turned, kept, stored):
        with nc.sbuf_tensor("y_rows", [P, NT, E], F32) as y_rows, nc.Block() as block:
            @block.tensor
            def _(pe):
                for t in range(NT):
                    last = nc.tensor.transpose(C.ps[t // 4][:, (t % 4) * P:(t % 4 + 1) * P], src[:, t * P:(t + 1) * P], C.ident[:, :])
                    if t % 4 == 3:
                        last.then_inc(turned, 1)

            @block.vector
            def _(dve):
                for q in range(4):
                    dve.wait_ge(turned, q + 1)
                    nc.vector.tensor_copy(y_rows[:, 4 * q:4 * q + 4, :], C.ps[q][:, :].rearrange("p (t d) -> p t d", t=4)).then_inc(kept, 1)

            @block.sync
            def _(sp):
                rows = C.out.rearrange("b (h p) d -> p (b h) d", p=P)
                for q in range(4):
                    sp.wait_ge(kept, q + 1)
                    sp.dma_start(rows[:, 4 * q:4 * q + 4, :], y_rows[:, 4 * q:4 * q + 4, :]).then_inc(stored, 16)
                sp.wait_ge(stored, 64)
    run_stage(nc, ["turned", "kept", "stored"], body)


L0_NH = 4
L0_HD = E // L0_NH
NEG = -1e30
MAGIC = 12582912.0
LOG2E = float(1.0 / np.log(2.0))
LN2_HI = 0.693145751953125
LN2_LO = float(np.log(2.0) - LN2_HI)
EXP1 = 2.0 ** 23


def split_exponent(nc, st, x, n, r):
    st.then(nc.vector.tensor_scalar(n, x, LOG2E, MAGIC, ALU.mult, ALU.add))
    st.then(nc.vector.tensor_scalar(n, n, MAGIC, None, ALU.subtract))
    st.then(nc.vector.scalar_tensor_tensor(r, n, -LN2_HI, x, ALU.mult, ALU.add))
    st.then(nc.vector.scalar_tensor_tensor(r, n, -LN2_LO, r, ALU.mult, ALU.add))


def eighth_power(nc, st, e):
    st.then(nc.vector.tensor_tensor(e, e, e, ALU.mult))
    st.then(nc.vector.tensor_tensor(e, e, e, ALU.mult))
    st.then(nc.vector.tensor_tensor(e, e, e, ALU.mult))

LN_EXP = "natural_log_exp_and_others"


def mlstm_gates(nc, C, G):
    def body(loaded, projected, u_split, exp_ready, own, w_ready, softplus_ready, lf_ready, lf_turned, cs_ready, cs_turned, M_ready, M_turned, m_ready, floor_ready):
        with ExitStack() as s:
            sb = sbuf(nc, s)
            gk = sb("gk", [P, 3, 2 * L0_NH])
            gb = sb("gb", [P, 2 * L0_NH])
            gate = sb("gate", [P, NT, 2 * L0_NH])
            ig, u, z, w, lw, lf, cs, m, n, r, ez = (sb(k, [P, NT, L0_NH]) for k in ("ig", "u", "z", "w", "lw", "log_f", "csum", "m", "n", "r", "ez"))
            a_col = sb("a_col", [P, NT * L0_NH])
            n2, r2, n3, r3 = (sb(k, [P, NT * L0_NH]) for k in ("n_a", "r_a", "n_M", "r_M"))
            pow2 = sb("pow2", [P, NT * L0_NH], I32)
            q_a = sb("q_a", [P, NT * L0_NH])
            ones = sb("ones", [L0_NH, TOK])
            rows_cs, rows_a = sb("rows_cs", [L0_NH, TOK]), sb("rows_a", [L0_NH, TOK])
            rows_M = sb("rows_M", [L0_NH, TOK])
            block = s.enter_context(nc.Block())
            flat = lambda t: t[:, :, :].rearrange("p t h -> p (t h)")
            bankG, bankC, bankM = C.ps[0], C.ps[1], C.ps[6]
            bankR = C.psum[0:L0_NH, 2:6, :].rearrange("p k c -> p (k c)")
            GV = bankG[:, 0:NT * 2 * L0_NH].rearrange("p (t g) -> p t g", t=NT)

            @block.sync
            def _(sp):
                for k, g in enumerate(("i", "f")):
                    h = slice(k * L0_NH, (k + 1) * L0_NH)
                    sp.dma_start(gk[:, :, h], C.i[f"L0_xattn_{g}gate_kernel"].rearrange("(c p) h -> p c h", p=P)).then_inc(loaded, 16)
                    sp.dma_start(gb[:, h], C.i[f"L0_xattn_{g}gate_bias"].unsqueeze(0).to_broadcast([P, L0_NH])).then_inc(loaded, 16)

            @block.tensor
            def _(pe):
                pe.wait_ge(loaded, 64)
                for t in range(NT):
                    for k, src in enumerate((C.HT, C.CT, C.CT)):
                        last = nc.tensor.matmul(GV[:, t, :], src[:, t * P:(t + 1) * P], gk[:, k, :], start=(k == 0), stop=(k == 2))
                last.then_inc(projected, 1)
                pe.wait_ge(lf_ready, 1)
                for t in range(NT):
                    last = nc.tensor.transpose(bankR[:, t * P:(t + 1) * P], lf[:, t, :], C.ident[:, :])
                last.then_inc(lf_turned, 1)
                pe.wait_ge(cs_ready, 1)
                for t in range(NT):
                    nc.tensor.transpose(bankR[:, t * P:(t + 1) * P], ig[:, t, :], C.ident[:, :])
                    last = nc.tensor.transpose(bankC[:, t * L0_NH:(t + 1) * L0_NH], rows_cs[:, t * P:(t + 1) * P], C.ident[0:L0_NH, 0:L0_NH])
                last.then_inc(cs_turned, 1)
                pe.wait_ge(M_ready, 1)
                for t in range(NT):
                    last = nc.tensor.transpose(bankM[:, t * L0_NH:(t + 1) * L0_NH], rows_M[:, t * P:(t + 1) * P], C.ident[0:L0_NH, 0:L0_NH])
                last.then_inc(M_turned, 1)

            @block.scalar
            def _(act):
                nc.scalar.preload_act_table_set(LN_EXP)
                act.wait_ge(u_split, 1)
                nc.scalar.activation(flat(ez), flat(r), ACT.Exp, scale=0.125).then_inc(exp_ready, 1)
                act.wait_ge(w_ready, 1)
                nc.scalar.activation(flat(lw), flat(w), ACT.Ln).then_inc(softplus_ready, 1)
                act.wait_ge(m_ready, 1)
                nc.scalar.activation(G.em_col[:, :], flat(m), ACT.Exp, scale=-1.0)
                nc.scalar.activation(G.key_factor[:, :], r2[:, :], ACT.Exp, scale=0.125)
                nc.scalar.activation(G.query_factor[:, :], r3[:, :], ACT.Exp, scale=-0.125).then_inc(floor_ready, 1)

            @block.vector
            def _(dve):
                st = Steps(dve, own)
                nc.vector.memset(ones[:, :], 1.0)
                dve.wait_ge(projected, 1)
                nc.vector.tensor_tensor(ig[:, :, :], GV[:, :, 0:L0_NH], gb[:, 0:L0_NH].unsqueeze(1).to_broadcast([P, NT, L0_NH]), ALU.add)
                st.then(nc.vector.tensor_tensor(gate[:, :, :], GV, gb[:, :].unsqueeze(1).to_broadcast([P, NT, 2 * L0_NH]), ALU.add))
                f = gate[:, :, L0_NH:2 * L0_NH]
                st.then(nc.vector.tensor_scalar(u[:, :, :], f, -1.0, None, ALU.mult))
                st.then(nc.vector.tensor_tensor(u[:, :, :], u[:, :, :], f, ALU.min))
                st.then(nc.vector.tensor_scalar(u[:, :, :], u[:, :, :], -80.0, None, ALU.max))
                split_exponent(nc, st, flat(u), flat(n), flat(r))
                nc.vector.tensor_scalar(pow2[:, :], flat(n), 127.0, EXP1, ALU.add, ALU.mult).then_inc(u_split, 1)
                dve.wait_ge(exp_ready, 1)
                dve.wait_ge(u_split, 1)
                eighth_power(nc, st, flat(ez))
                st.then(nc.vector.tensor_tensor(flat(z), flat(ez), pow2[:, :].bitcast(F32), ALU.mult))
                nc.vector.tensor_scalar(flat(w), flat(z), 1.0, None, ALU.add).then_inc(w_ready, 1)
                dve.wait_ge(w_ready, 1)
                st.then(nc.vector.scalar_tensor_tensor(flat(z), flat(w), 1.0, flat(z), ALU.subtract, ALU.subtract))
                st.then(nc.vector.reciprocal(flat(r), flat(w)))
                st.then(nc.vector.tensor_tensor(flat(z), flat(z), flat(r), ALU.mult))
                dve.wait_ge(softplus_ready, 1)
                st.then(nc.vector.tensor_tensor(flat(z), flat(lw), flat(z), ALU.subtract))
                nc.vector.scalar_tensor_tensor(lf[:, :, :], f, 0.0, z[:, :, :], ALU.min, ALU.subtract).then_inc(lf_ready, 1)
                dve.wait_ge(lf_turned, 1)
                st.then(nc.vector.tensor_copy(rows_a[:, :], bankR))
                for b in range(B):
                    c = slice(b * S, (b + 1) * S)
                    last = nc.vector.tensor_tensor_scan(rows_cs[:, c], ones[:, c], rows_a[:, c], 0.0, ALU.mult, ALU.add)
                last.then_inc(cs_ready, 1)
                dve.wait_ge(cs_turned, 1)
                nc.vector.tensor_tensor(rows_a[:, :], bankR, rows_cs[:, :], ALU.subtract)
                st.then(nc.vector.tensor_copy(flat(cs), bankC[:, 0:NT * L0_NH]))
                st.then(nc.vector.tensor_tensor(a_col[:, :], flat(ig), flat(cs), ALU.subtract))
                st.then(nc.vector.tensor_scalar(n2[:, :], a_col[:, :], LOG2E, MAGIC, ALU.mult, ALU.add))
                st.then(nc.vector.tensor_scalar(n2[:, :], n2[:, :], MAGIC, None, ALU.subtract))
                st.then(nc.vector.scalar_tensor_tensor(q_a[:, :], n2[:, :], LN2_HI, flat(cs), ALU.mult, ALU.add))
                st.then(nc.vector.tensor_tensor(r2[:, :], flat(ig), q_a[:, :], ALU.subtract))
                st.then(nc.vector.scalar_tensor_tensor(r2[:, :], n2[:, :], -LN2_LO, r2[:, :], ALU.mult, ALU.add))
                nc.vector.tensor_scalar(G.key_exponent[:, :], n2[:, :], 127.0, EXP1, ALU.add, ALU.mult)
                for b in range(B):
                    c = slice(b * S, (b + 1) * S)
                    last = nc.vector.tensor_tensor_scan(rows_M[:, c], rows_a[:, c], rows_a[:, c], -3e38, ALU.max, ALU.max)
                last.then_inc(M_ready, 1)
                dve.wait_ge(M_ready, 1)
                st.then(nc.vector.tensor_scalar(G.query_exponent[:, :], rows_M[:, :], LOG2E, MAGIC, ALU.mult, ALU.add))
                st.then(nc.vector.tensor_scalar(G.query_exponent[:, :], G.query_exponent[:, :], MAGIC, -EXP1, ALU.subtract, ALU.mult))
                dve.wait_ge(M_turned, 1)
                st.then(nc.vector.tensor_copy(z[:, :, :].rearrange("p t h -> p (t h)"), bankM[:, 0:NT * L0_NH]))
                split_exponent(nc, st, flat(z), n3[:, :], r3[:, :])
                nc.vector.tensor_tensor(flat(m), flat(cs), flat(z), ALU.add).then_inc(m_ready, 1)
                dve.wait_ge(floor_ready, 1)
                eighth_power(nc, st, G.key_factor[:, :])
                eighth_power(nc, st, G.query_factor[:, :])
    run_stage(nc, ["loaded", "projected", "u_split", "exp_ready", "own", "w_ready", "softplus_ready", "lf_ready", "lf_turned", "cs_ready", "cs_turned", "M_ready", "M_turned", "m_ready",
                   "floor_ready"], body)


def mlstm_heads(nc, C, G):
    NH, HD = L0_NH, L0_HD
    DS = 12
    def body(loaded, staged, d_ready, s_ready, d_made, c_ready, pv_ready, ln_ready, root_ready, o_ready, o_turned, added, own, act_own):
        with ExitStack() as s:
            sb = sbuf(nc, s)
            maskb = sb("maskb", [P, P], BF16)
            sel = sb("sel", [NH, NH, P])
            rms = sb("rms", [P, 1])
            ab = sb("ab", [P, 2, 8])
            qs, ks = sb("qs", [P, 2, S]), sb("ks", [P, 2, S])
            ms = sb("ms", [NH, 2, S])
            VA = sb("VA", [P, 2, 2, NH, HD + 1])
            dm = sb("dm", [P, NH, 384], I32)
            cT = sb("cT", [P, NH, 384])
            nrm, ssq, v0, y, y2, t2 = (sb(n, [P, 8]) for n in ("nrm", "ssq", "v0", "y8", "y28", "t28"))
            o, osq = sb("o", [P, 2, NH, HD]), sb("osq", [P, 2, NH, HD])
            block = s.enter_context(nc.Block())
            bankD, bankS, bankO, bankT = C.ps[0:2], C.ps[2:4], C.ps[4], C.ps[5]

            @block.sync
            def _(sp):
                sp.dma_start(maskb[:, :], C.c["causal_kq"]).then_inc(loaded, 16)
                sp.dma_start(sel[:, :, :], C.c["head_rows"]).then_inc(loaded, 16)
                for h in range(NH):
                    sp.dma_start(rms[h * HD:(h + 1) * HD, :], C.i["L0_xattn_rms_scale"].unsqueeze(1)).then_inc(loaded, 16)

            @block.tensor
            def _(pe):
                pe.wait_ge(loaded, 16 * 6)

                def scores(n, p, h):
                    g = slice(32 * h, 32 * h + 32)
                    if not (isinstance(n, int) and n == 0 and h < 2):
                        pe.wait_ge(d_made, n * NH + (h - 1))
                    D = bankD[h % 2]
                    nc.tensor.matmul(D[:, 0:S], sel[:, h, :], ms[:, p, :], start=True, stop=False, skip_group_check=True)
                    nc.tensor.matmul(D[:, S:S + P], sel[:, h, :], ms[:, p, P:S], start=False, stop=False, skip_group_check=True)
                    nc.tensor.matmul(D[:, 0:P], C.identb[:, :], maskb[:, :], start=False, stop=False, skip_group_check=True)
                    nc.tensor.matmul(D[:, S:S + P], C.identb[:, :], maskb[:, :], start=False, stop=True, skip_group_check=True).then_inc(d_ready, 1)
                    if not (isinstance(n, int) and n == 0 and h < 2):
                        pe.wait_ge(c_ready, n * NH + (h - 1))
                    Z = bankS[h % 2]
                    nc.tensor.matmul(Z[:, 0:S], ks[g, p, 0:P], qs[g, p, :], start=True, stop=True, skip_group_check=True)
                    nc.tensor.matmul(Z[:, S:S + P], ks[g, p, P:S], qs[g, p, P:S], start=True, stop=True, skip_group_check=True).then_inc(s_ready, 1)

                def values(n, p, h):
                    pe.wait_ge(c_ready, n * NH + (h + 1))
                    nc.tensor.matmul(bankO[:, h * 33:(h + 1) * 33], cT[:, h, 0:P], VA[:, p, 0, h, :], start=True, stop=True, skip_group_check=True)
                    nc.tensor.matmul(bankO[:, (4 + h) * 33:(5 + h) * 33], cT[:, h, P:2 * P], VA[:, p, 0, h, :], start=True, stop=False, skip_group_check=True)
                    return nc.tensor.matmul(bankO[:, (4 + h) * 33:(5 + h) * 33], cT[:, h, 2 * P:3 * P], VA[:, p, 1, h, :], start=False, stop=True, skip_group_check=True)

                def batch(n, p, after):
                    for h in range(NH):
                        if h + 2 < NH:
                            last = values(n, p, h)
                            scores(n, p, h + 2)
                        else:
                            last = values(n, p, h)
                    last.then_inc(pv_ready, 1)
                    if after is not None:
                        pe.wait_ge(staged, after * 4 + 4)
                        scores(after, 1 - p, 0)
                        scores(after, 1 - p, 1)
                    pe.wait_ge(o_ready, n + 1)
                    for t in range(2):
                        last = nc.tensor.transpose(bankT[:, t * P:(t + 1) * P], o[:, t, :, :].rearrange("p h d -> p (h d)"), C.ident[:, :])
                    last.then_inc(o_turned, 1)

                pe.wait_ge(staged, 4)
                scores(0, 0, 0)
                scores(0, 0, 1)
                with pe.Fori(0, B // 2 - 1) as i:
                    batch(i * 2, 0, i * 2 + 1)
                    batch(i * 2 + 1, 1, i * 2 + 2)
                batch(B - 2, 0, B - 1)
                batch(B - 1, 1, None)

            @block.scalar
            def _(act):
                nc.scalar.preload_act_table_set(LN_EXP)
                with act.Fori(0, B) as b:
                    act.wait_ge(ln_ready, b + 1)
                    st = Steps(act, act_own, b * 2)
                    st.then(nc.scalar.activation(y2[:, :], v0[:, :], ACT.Ln))
                    st.then(nc.scalar.activation(y[:, :], y2[:, :], ACT.Exp, scale=-0.5))
                    nc.scalar.activation(y2[:, :], y[:, :], ACT.Square).then_inc(root_ready, 1)

            @block.vector
            def _(dve):
                dve.wait_ge(loaded, 16 * 6)
                st0 = Steps(dve, own)
                st0.then(nc.vector.tensor_scalar(rms[:, :], rms[:, :], 1.0, None, ALU.add))
                def stage(n, p):
                    nc.vector.tensor_copy(ms[:, p, :], G.query_exponent[:, bass.ds(n * S, S)]).then_inc(staged, 1)
                    nc.vector.tensor_copy(qs[:, p, :], C.HT[:, bass.ds(n * S, S)]).then_inc(staged, 1)
                    nc.vector.tensor_scalar(ks[:, p, :], C.CT[:, bass.ds(n * S, S)], float(HD) ** -0.5, None, ALU.mult).then_inc(staged, 1)
                    nc.vector.tensor_copy(ab[:, p, :], G.key_exponent[:, bass.ds(n * 8, 8)])
                    kf = G.key_factor[:, bass.ds(n * 8, 8)]
                    nc.vector.tensor_copy(VA[:, p, :, :, HD].rearrange("p t h -> p (t h)"), kf)
                    nc.vector.tensor_tensor(VA[:, p, :, :, 0:HD].rearrange("p t h d -> p (t h) d"), C.CN[:, bass.ds(n * 2, 2), :].rearrange("p t (h d) -> p (t h) d", h=NH), kf.unsqueeze(2).to_broadcast([P, 8, HD]), ALU.mult).then_inc(staged, 1)

                def heads(n, p):
                    for h in range(NH):
                        dve.wait_ge(d_ready, n * NH + (h + 1))
                        nc.vector.tensor_scalar(dm[:, h, 0:S], bankD[h % 2][:, 0:S], ab[:, p, h:h + 1], 0.0, ALU.add, ALU.max)
                        nc.vector.tensor_scalar(dm[:, h, S:S + P], bankD[h % 2][:, S:S + P], ab[:, p, 4 + h:5 + h], 0.0, ALU.add, ALU.max).then_inc(d_made, 1)
                        dve.wait_ge(d_made, n * NH + (h + 1))
                        dve.wait_ge(s_ready, n * NH + (h + 1))
                        nc.vector.tensor_tensor(cT[:, h, :], bankS[h % 2][:, 0:384], dm[:, h, :].bitcast(F32), ALU.mult).then_inc(c_ready, 1)

                def finish(n):
                    dve.wait_ge(pv_ready, n + 1)
                    st = Steps(dve, own, n * DS + 1)
                    O = bankO[:, 0:8 * 33].rearrange("p (t h e) -> p t h e", t=2, h=NH)
                    qf = G.query_factor[:, bass.ds(n * 8, 8)]
                    st.then(nc.vector.tensor_tensor(nrm[:, :].rearrange("p (t h) -> p t h", t=2), O[:, :, :, HD], qf.rearrange("p (t h) -> p t h", t=2), ALU.mult))
                    st.then(nc.vector.tensor_tensor(nrm[:, :], nrm[:, :], G.em_col[:, bass.ds(n * 8, 8)], ALU.max))
                    st.then(nc.vector.tensor_scalar(nrm[:, :], nrm[:, :], 1e-6, None, ALU.add))
                    st.then(nc.vector.reciprocal(nrm[:, :], nrm[:, :]))
                    st.then(nc.vector.tensor_tensor(nrm[:, :], nrm[:, :], qf, ALU.mult))
                    st.then(nc.vector.tensor_tensor(o[:, :, :, :].rearrange("p t h d -> p (t h) d"), O[:, :, :, 0:HD].rearrange("p t h d -> p (t h) d"), nrm[:, :].unsqueeze(2).to_broadcast([P, 8, HD]), ALU.mult))
                    st.then(nc.vector.tensor_tensor(osq[:, :, :, :], o[:, :, :, :], o[:, :, :, :], ALU.mult))
                    st.then(nc.vector.tensor_reduce(ssq[:, :], osq[:, :, :, :].rearrange("p t h d -> p (t h) d"), AX.X, ALU.add))
                    nc.vector.tensor_scalar(v0[:, :], ssq[:, :], 1.0 / HD, 1e-6, ALU.mult, ALU.add).then_inc(ln_ready, 1)
                    dve.wait_ge(root_ready, n + 1)
                    dve.wait_ge(ln_ready, n + 1)
                    st.then(nc.vector.tensor_tensor(t2[:, :], v0[:, :], y2[:, :], ALU.mult))
                    st.then(nc.vector.tensor_scalar(t2[:, :], t2[:, :], -0.5, 0.5, ALU.mult, ALU.add))
                    st.then(nc.vector.tensor_tensor(t2[:, :], t2[:, :], y[:, :], ALU.mult))
                    st.then(nc.vector.tensor_tensor(t2[:, :], t2[:, :], y[:, :], ALU.add))
                    nc.vector.tensor_tensor(o[:, :, :, :].rearrange("p t h d -> p (t h) d"), o[:, :, :, :].rearrange("p t h d -> p (t h) d"), t2[:, :].unsqueeze(2).to_broadcast([P, 8, HD]), ALU.mult).then_inc(o_ready, 1)
                    dve.wait_ge(o_turned, n + 1)
                    xs = C.XT[:, bass.ds(n * S, S)]
                    nc.vector.scalar_tensor_tensor(xs, bankT[:, 0:S], rms[:, :], xs, ALU.mult, ALU.add).then_inc(added, 1)
                    assert st.n == DS, st.n

                def batch(n, p, after):
                    heads(n, p)
                    if after is not None:
                        stage(after, 1 - p)
                    finish(n)

                stage(0, 0)
                with dve.Fori(0, B // 2 - 1) as i:
                    batch(i * 2, 0, i * 2 + 1)
                    batch(i * 2 + 1, 1, i * 2 + 2)
                batch(B - 2, 0, B - 1)
                batch(B - 1, 1, None)
    run_stage(nc, ["loaded", "staged", "d_ready", "s_ready", "d_made", "c_ready", "pv_ready", "ln_ready", "root_ready", "o_ready", "o_turned", "added", "own", "act_own"], body)


def l0_xattn(nc, C):
    layer_norm(nc, C, C.HT)
    G = Core()
    with ExitStack() as s:
        sb = sbuf(nc, s)
        G.query_exponent = sb("query_exponent", [L0_NH, TOK])
        G.em_col, G.key_factor, G.query_factor, G.key_exponent = (sb(n, [P, NT * L0_NH]) for n in ("em_col", "key_factor", "query_factor", "key_exponent"))
        mlstm_gates(nc, C, G)
        mlstm_heads(nc, C, G)




def over(nc, st, x, t, d, k):
    st.then(nc.vector.tensor_scalar(t, x, 1.0 / k, None, ALU.mult))
    st.then(nc.vector.scalar_tensor_tensor(d, t, -(k + 1.0), x, ALU.mult, ALU.add))
    st.then(nc.vector.tensor_tensor(d, d, t, ALU.add))
    st.then(nc.vector.scalar_tensor_tensor(t, d, 1.0 / k, t, ALU.mult, ALU.add))

RMAX = bass.bass_isa.ReduceOp.max
L0_I = 352
L0_IT = [(0, 128), (128, 128), (256, 96)]


def l0_ffn_weights(nc, C, F):
    WEIGHTS_DONE = 26

    def body(loaded, spread, sig_ready, turned, own):
        with ExitStack() as s:
            sb = sbuf(nc, s)
            wr = sb("wr", [P, 2, 3, E])
            wd = sb("wd", [P, L0_I])
            wi = sb("wi", [P, 2, 3, E], BF16)
            wdi = sb("wdi", [P, L0_I], BF16)
            tmp = sb("tmp", [P, 2, 3, E])
            nclip, nn, rc, ez = (sb(k, [P, 2]) for k in ("neg_clip", "n_clip", "r_clip", "exp_clip"))
            pow2 = sb("pow2_clip", [P, 2], I32)
            rem, t127 = sb("rem", [P, 8]), sb("t127", [P, 8])
            inv, invd, mx, am = sb("inv", [P, 2, 3]), sb("invd", [P, 1]), sb("mx", [P, 1]), sb("am", [P, 1])
            block = s.enter_context(nc.Block())

            @block.sync
            def _(sp):
                for n, name in enumerate(("gate", "up")):
                    w = C.i[f"L0_ffn_w_{name}"]
                    sp.dma_start(wr[:, n, 0:2, :], w[0:256, :].rearrange("(t p) h -> p t h", p=P)).then_inc(loaded, 16)
                    sp.dma_start(wr[0:96, n, 2, :], w[256:L0_I, :]).then_inc(loaded, 16)
                    sp.dma_start(wr[96:P, n, 2, :], w[0:32, :]).then_inc(loaded, 16)
                sp.dma_start(wd[:, :], C.i["L0_ffn_w_down"]).then_inc(loaded, 16)
                for n, name in enumerate(("x", "down")):
                    sp.dma_start(F.clip[:, n:n + 1], C.i[f"L0_ffn_clip_{name}"].unsqueeze(0).to_broadcast([P, 1])).then_inc(loaded, 16)

            @block.scalar
            def _(act):
                act.wait_ge(own, 5)
                nc.scalar.activation(ez[:, :], rc[:, :], ACT.Exp, scale=0.125).then_inc(sig_ready, 1)

            @block.gpsimd
            def _(pool):
                pool.wait_ge(own, 6)
                nc.gpsimd.partition_all_reduce(am[:, :], mx[:, :], P, RMAX).then_inc(spread, 1)

            @block.vector
            def _(dve):
                st = Steps(dve, own)
                dve.wait_ge(loaded, 16 * 9)
                st.then(nc.vector.tensor_scalar(nclip[:, :], F.clip[:, :], -1.0, 80.0, ALU.mult, ALU.min))
                split_exponent(nc, st, nclip[:, :], nn[:, :], rc[:, :])
                st.then(nc.vector.tensor_reduce(mx[:, :], C.HT[:, :], AX.X, ALU.max, apply_absolute_value=True))
                st.then(nc.vector.tensor_reduce(F.sw[:, :, :], wr[:, :, :, :], AX.X, ALU.max, apply_absolute_value=True))
                st.then(nc.vector.tensor_reduce(F.swd[:, :], wd[:, :], AX.X, ALU.max, apply_absolute_value=True))
                sw6 = F.sw[:, :, :].rearrange("p a t -> p (a t)")
                over(nc, st, sw6, t127[:, 0:6], rem[:, 0:6], 127.0)
                st.then(nc.vector.tensor_copy(sw6, t127[:, 0:6]))
                over(nc, st, F.swd[:, :], t127[:, 7:8], rem[:, 7:8], 127.0)
                st.then(nc.vector.tensor_copy(F.swd[:, :], t127[:, 7:8]))
                st.then(nc.vector.reciprocal(inv[:, :, :], F.sw[:, :, :]))
                st.then(nc.vector.reciprocal(invd[:, :], F.swd[:, :]))
                W = lambda t: t[:, :, :, :].rearrange("p a t h -> p (a t) h")
                st.then(nc.vector.tensor_tensor(W(tmp), W(wr), inv[:, :, :].rearrange("p a t -> p (a t)").unsqueeze(2).to_broadcast([P, 6, E]), ALU.mult))
                st.then(nc.vector.tensor_scalar(W(tmp), W(tmp), -128.0, 127.0, ALU.max, ALU.min))
                st.then(nc.vector.tensor_scalar(W(wi), W(tmp), MAGIC, MAGIC, ALU.add, ALU.subtract))
                st.then(nc.vector.tensor_scalar(wd[:, :], wd[:, :], invd[:, :], -128.0, ALU.mult, ALU.max))
                st.then(nc.vector.tensor_scalar(wd[:, :], wd[:, :], 127.0, MAGIC, ALU.min, ALU.add))
                st.then(nc.vector.tensor_scalar(wdi[:, :], wd[:, :], MAGIC, None, ALU.subtract))
                assert st.n == WEIGHTS_DONE
                dve.wait_ge(sig_ready, 1)
                dve.wait_ge(spread, 1)
                eighth_power(nc, st, ez[:, :])
                st.then(nc.vector.tensor_scalar(nn[:, :], nn[:, :], -126.0, 127.0, ALU.max, ALU.add))
                st.then(nc.vector.tensor_scalar(pow2[:, :], nn[:, :], EXP1, None, ALU.mult))
                st.then(nc.vector.tensor_tensor(ez[:, :], ez[:, :], pow2[:, :].bitcast(F32), ALU.mult))
                st.then(nc.vector.tensor_scalar(ez[:, :], ez[:, :], 1.0, None, ALU.add))
                st.then(nc.vector.reciprocal(F.clip[:, :], ez[:, :]))
                st.then(nc.vector.tensor_scalar(mx[:, :], am[:, :], F.clip[:, 0:1], None, ALU.mult))
                over(nc, st, mx[:, :], am[:, :], rem[:, 6:7], 127.0)
                st.then(nc.vector.reciprocal(mx[:, :], am[:, :]))
                st.then(nc.vector.tensor_scalar(F.sw[:, :, :], F.sw[:, :, :], am[:, :], None, ALU.mult))
                st.then(nc.vector.tensor_scalar(F.XF[:, :], C.HT[:, :], mx[:, :], -128.0, ALU.mult, ALU.max))
                st.then(nc.vector.tensor_scalar(F.XF[:, :], F.XF[:, :], 127.0, MAGIC, ALU.min, ALU.add))
                nc.vector.tensor_scalar(F.XQ[:, :], F.XF[:, :], MAGIC, None, ALU.subtract)
                dve.wait_ge(turned, 1)
                nc.vector.tensor_copy(F.WT[:, 0, :], C.ps[0][:, 0:192].bitcast(BF16)[:, 0:L0_I])
                nc.vector.tensor_copy(F.WT[:, 1, :], C.ps[1][:, 0:192].bitcast(BF16)[:, 0:L0_I])
                for t, (i0, n) in enumerate(L0_IT):
                    nc.vector.tensor_copy(F.WD[0:n, t, :], C.ps[2][0:n, 64 * t:64 * t + 64].bitcast(BF16))

            @block.tensor
            def _(pe):
                pe.wait_ge(own, WEIGHTS_DONE)
                for a in range(2):
                    for t, (i0, n) in enumerate(L0_IT):
                        nc.tensor.transpose(C.ps[a][:, 0:192].bitcast(BF16)[:, i0:i0 + n], wi[0:n, a, t, :], C.identb[0:n, 0:n])
                for t, (i0, n) in enumerate(L0_IT):
                    last = nc.tensor.transpose(C.ps[2][0:n, 64 * t:64 * t + 64].bitcast(BF16), wdi[:, i0:i0 + n], C.identb[:, :])
                last.then_inc(turned, 1)
    run_stage(nc, ["loaded", "spread", "sig_ready", "turned", "own"], body)


def l0_ffn_up(nc, C, F):
    def body(g_ready, u_ready, sig_ready, h_ready, own):
        with ExitStack() as s:
            sb = sbuf(nc, s)
            sg = sb("sg", [P, 2, CH])
            gs = sb("gs", [P, 2, CH])
            block = s.enter_context(nc.Block())
            jobs = [(q, t) for q in range(2) for t in range(3)]

            @block.tensor
            def _(pe):
                with pe.Fori(0, NCH // 2) as i:
                    for j, (q, t) in enumerate(jobs):
                        i0, n = L0_IT[t]
                        if j >= 2:
                            pe.wait_ge(h_ready, i * 6 + (j - 1))
                        x = F.XQ[:, bass.ds(i * (2 * CH) + q * CH, CH)]
                        nc.tensor.matmul(C.ps[j % 2][0:n, :], F.WT[:, 0, i0:i0 + n], x, start=True, stop=True).then_inc(g_ready, 1)
                        nc.tensor.matmul(C.ps[2 + j % 2][0:n, :], F.WT[:, 1, i0:i0 + n], x, start=True, stop=True).then_inc(u_ready, 1)
                    pe.wait_ge(h_ready, i * 6 + 6)

            @block.scalar
            def _(act):
                with act.Fori(0, NCH // 2) as i:
                    for j, (q, t) in enumerate(jobs):
                        n = L0_IT[t][1]
                        act.wait_ge(g_ready, i * 6 + (j + 1))
                        nc.scalar.activation(sg[0:n, j % 2, :], C.ps[j % 2][0:n, :], ACT.Sigmoid, scale=F.sw[0:n, 0, t:t + 1]).then_inc(sig_ready, 1)

            @block.vector
            def _(dve):
                with dve.Fori(0, NCH // 2) as i:
                    for j, (q, t) in enumerate(jobs):
                        n = L0_IT[t][1]
                        dve.wait_ge(sig_ready, i * 6 + (j + 1))
                        st = Steps(dve, own, i * 6 + j)
                        st.then(nc.vector.scalar_tensor_tensor(gs[0:n, j % 2, :], C.ps[j % 2][0:n, :], F.sw[0:n, 0, t:t + 1], sg[0:n, j % 2, :], ALU.mult, ALU.mult))
                        dve.wait_ge(u_ready, i * 6 + (j + 1))
                        nc.vector.scalar_tensor_tensor(F.HB[0:n, t, bass.ds(i * (2 * CH) + q * CH, CH)], C.ps[2 + j % 2][0:n, :], F.sw[0:n, 1, t:t + 1], gs[0:n, j % 2, :], ALU.mult, ALU.mult).then_inc(h_ready, 1)
    run_stage(nc, ["g_ready", "u_ready", "sig_ready", "h_ready", "own"], body)


def l0_ffn_down(nc, C, F):
    def body(spread, quantised, y_ready, added, own):
        with ExitStack() as s:
            sb = sbuf(nc, s)
            mx, am, mt, rem = sb("mx", [P, 1]), sb("am", [P, 1]), sb("mt", [P, 3]), sb("rem", [P, 1])
            HQ = sb("HQ", [P, 3, TOK], BF16)
            block = s.enter_context(nc.Block())

            @block.gpsimd
            def _(pool):
                pool.wait_ge(own, 3)
                nc.gpsimd.partition_all_reduce(am[:, :], mx[:, :], P, RMAX).then_inc(spread, 1)

            @block.vector
            def _(dve):
                st = Steps(dve, own)
                st.then(nc.vector.memset(mt[:, :], 0.0))
                nc.vector.tensor_reduce(mt[:, 0:2], F.HB[:, 0:2, :], AX.X, ALU.max, apply_absolute_value=True)
                st.then(nc.vector.tensor_reduce(mt[0:96, 2:3], F.HB[0:96, 2, :], AX.X, ALU.max, apply_absolute_value=True))
                st.then(nc.vector.tensor_reduce(mx[:, :], mt[:, :], AX.X, ALU.max))
                dve.wait_ge(spread, 1)
                st.then(nc.vector.tensor_scalar(mx[:, :], am[:, :], F.clip[:, 1:2], None, ALU.mult))
                over(nc, st, mx[:, :], am[:, :], rem[:, :], 127.0)
                st.then(nc.vector.reciprocal(mx[:, :], am[:, :]))
                st.then(nc.vector.tensor_scalar(F.swd[:, :], F.swd[:, :], am[:, :], None, ALU.mult))
                for t, (i0, n) in enumerate(L0_IT):
                    h = F.HB[0:n, t, :]
                    st.then(nc.vector.tensor_scalar(h, h, mx[0:n, :], -128.0, ALU.mult, ALU.max))
                    st.then(nc.vector.tensor_scalar(h, h, 127.0, MAGIC, ALU.min, ALU.add))
                    nc.vector.tensor_scalar(HQ[0:n, t, :], h, MAGIC, None, ALU.subtract).then_inc(quantised, 1)
                for c in range(NCH):
                    dve.wait_ge(y_ready, c + 1)
                    x = C.XT[:, c * CH:(c + 1) * CH]
                    nc.vector.scalar_tensor_tensor(x, C.ps[c][:, :], F.swd[:, :], x, ALU.mult, ALU.add).then_inc(added, 1)

            @block.tensor
            def _(pe):
                for t, (i0, n) in enumerate(L0_IT):
                    pe.wait_ge(quantised, t + 1)
                    for c in range(NCH):
                        mm = nc.tensor.matmul(C.ps[c][:, :], F.WD[0:n, t, :], HQ[0:n, t, c * CH:(c + 1) * CH], start=(t == 0), stop=(t == 2))
                        if t == 2:
                            mm.then_inc(y_ready, 1)
    run_stage(nc, ["spread", "quantised", "y_ready", "added", "own"], body)


def l0_ffn(nc, C):
    layer_norm(nc, C, C.HT)
    F = Core()
    with ExitStack() as s:
        sb = sbuf(nc, s)
        F.clip, F.sw, F.swd = sb("clip", [P, 2]), sb("sw", [P, 2, 3]), sb("swd", [P, 1])
        F.WT, F.WD = sb("WT", [P, 2, L0_I], BF16), sb("WD", [P, 3, E], BF16)
        F.XF, F.XQ = sb("XF", [P, TOK]), sb("XQ", [P, TOK], BF16)
        F.HB = sb("HB", [P, 3, TOK])
        l0_ffn_weights(nc, C, F)
        l0_ffn_up(nc, C, F)
        l0_ffn_down(nc, C, F)


NH, HD = 16, 8
NG = NH // 2
STACK = [(0, 3, 0, 0), (3, 2, 1, 0), (5, 1, 2, 0)]
ROWS = 6 * HD


TWO_BF16_ONES = float(np.array([0x3F803F80], np.uint32).view(np.float32)[0])


def split_parts(nc, C, QT, KT):
    def body(hi, rest1, mid, rest2, lo, stored):
        with ExitStack() as s:
            sb = sbuf(nc, s)
            parts = sb("parts", [P, 2, 3, TOK], BF16)
            rest = sb("rest", [P, 2, TOK])
            block = s.enter_context(nc.Block())

            @block.scalar
            def _(act):
                for n, src in enumerate((QT, KT)):
                    nc.scalar.activation(parts[:, n, 0, :], src[:, :], ACT.Copy).then_inc(hi, 1)
                for n in range(2):
                    act.wait_ge(rest1, n + 1)
                    nc.scalar.activation(parts[:, n, 1, :], rest[:, n, :], ACT.Copy).then_inc(mid, 1)
                for n in range(2):
                    act.wait_ge(rest2, n + 1)
                    nc.scalar.activation(parts[:, n, 2, :], rest[:, n, :], ACT.Copy).then_inc(lo, 1)

            @block.vector
            def _(dve):
                for n, src in enumerate((QT, KT)):
                    dve.wait_ge(hi, n + 1)
                    nc.vector.tensor_tensor(rest[:, n, :], src[:, :], parts[:, n, 0, :], ALU.subtract).then_inc(rest1, 1)
                for n in range(2):
                    dve.wait_ge(mid, n + 1)
                    nc.vector.tensor_tensor(rest[:, n, :], rest[:, n, :], parts[:, n, 1, :], ALU.subtract).then_inc(rest2, 1)

            @block.sync
            def _(sp):
                for k, done in enumerate((hi, mid, lo)):
                    for n in range(2):
                        sp.wait_ge(done, n + 1)
                        sp.dma_start(C.qk_parts[n, k, :, :], parts[:, n, k, :]).then_inc(stored, 16)
                sp.wait_ge(stored, 96)
    run_stage(nc, ["hi", "rest1", "mid", "rest2", "lo", "stored"], body)


def attend(nc, C, A):
    KR = ROWS + (1 if A.key_mask is not None else 0)
    LOADS = 4 * sum(n for _, n, _, _ in STACK) + (2 if A.key_mask is not None else 0)
    VW = 32
    HG = NG // 2

    def body(stacked00, stacked01, stacked10, stacked11, consts_in, ones_set, v_staged, a_ready, a_max, nm_ready, nm_turned, nm_kept, b_ready, p_ready, pv_done,
             o_kept, o_placed, o_normed, inverted, y_ready, added, own):
        stacked = ((stacked00, stacked01), (stacked10, stacked11))
        with ExitStack() as s:
            sb = sbuf(nc, s)
            QS, KS = sb("QS", [P, 2, NG, S], BF16), sb("KS", [P, 2, NG, S], BF16)
            sel = sb("selm", [P, NH, P], BF16)
            place = sb("place", [P, 4, 2, P])
            VB = sb("VB", [P, 2, 2, NH, VW])
            mx = sb("mx", [P, 2, NH])
            nm = sb("nm", [P, 2, 2, 4, NH], BF16)
            nr = sb("nr", [P, 2, NH])
            NMT = sb("NMT", [P, 2, S], BF16)
            PT = sb("PT", [P, 2, 2, 2, S])
            OH = sb("o_heads", [P, 2, 2, S])
            rec = sb("rec", [P, S])
            oT = sb("oT", [P, S])
            block = s.enter_context(nc.Block())
            bankA = C.ps[0:2]
            bankB = (C.psum[:, 2:4, :], C.psum[:, 4:6, :])
            bankO, bankT = C.ps[6], C.ps[7]
            NMP = bankA[0][:, 0:S // 2].bitcast(BF16)

            @block.sync
            def _(sp):
                for r in (0, 64):
                    sp.dma_start(sel[r:r + 48, :, :], C.c["max_rows"]).then_inc(consts_in, 16)
                sp.dma_start(place[:, :, :, :], C.c["head_places"]).then_inc(consts_in, 16)
                sp.wait_ge(ones_set, 1)

                def load(t, p, half):
                    done = stacked[p][half]
                    G = slice(half * HG, half * HG + HG)
                    for s0, n, qp, kp in STACK:
                        for hh in range(2):
                            rows = slice(64 * hh + HD * s0, 64 * hh + HD * (s0 + n))
                            parts = lambda w: C.qk_parts[w, :, :, bass.ds(t * S, S)].rearrange("k (g x d) t -> x k d g t", x=2, d=HD)[hh][:, :, G, :]
                            for k in range(n):
                                sp.dma_start(QS[rows.start + HD * k:rows.start + HD * (k + 1), p, G, :], parts(0)[qp]).then_inc(done, 16)
                                sp.dma_start(KS[rows.start + HD * k:rows.start + HD * (k + 1), p, G, :], parts(1)[kp + k]).then_inc(done, 16)
                    if A.key_mask is not None:
                        for hh in range(2):
                            sp.dma_start(KS[64 * hh + ROWS:64 * hh + ROWS + 1, p, G, :], A.key_mask(t)).then_inc(done, 16)
                for p in range(2):
                    for half in range(2):
                        load(p, p, half)
                with sp.Fori(0, B // 2 - 1) as i:
                    for p in range(2):
                        for half in range(2):
                            sp.wait_ge(b_ready, i * 16 + (8 * p + 4 * half + 4))
                            load(i * 2 + (2 + p), p, half)

            @block.gpsimd
            def _(pool):
                def stage(n, p):
                    for t in range(2):
                        nc.gpsimd.tensor_copy(VB[:, p, t, :, 0:HD + 1], A.VA[:, bass.ds(n * 2 + t, 1), :].rearrange("p o (h e) -> p (o h) e", h=NH)).then_inc(v_staged, 1)
                pool.wait_ge(ones_set, 2)
                for p in range(2):
                    stage(p, p)
                with pool.Fori(0, B // 2 - 1) as i:
                    for p in range(2):
                        pool.wait_ge(pv_done, i * 16 + 8 * (p + 1))
                        stage(i * 2 + (2 + p), p)

            @block.tensor
            def _(pe):
                pe.wait_ge(consts_in, 48)
                NM = len(A.masks) if A.masks else 0

                def pass_a(n, p, g):
                    if g % HG == 0:
                        pe.wait_ge(stacked[p][g // HG], loads_due(n, p))
                    if not (isinstance(n, int) and n == 0 and g == 0):
                        pe.wait_ge(a_max, n * NH + 2 * g)
                    for t in range(2):
                        for x in range(2):
                            r = slice(64 * x, 64 * x + KR)
                            mm = nc.tensor.matmul(bankA[x][:, t * S:(t + 1) * S], QS[r, p, g, t * P:(t + 1) * P], KS[r, p, g, :], start=(t == 0), stop=(NM == 0), skip_group_check=True)
                            if NM == 0 and t == 1:
                                mm.then_inc(a_ready, 1)
                    for x in range(2):
                        for k in range(NM):
                            mm = nc.tensor.matmul(bankA[x][:, :], C.identb[:, :], A.masks[k][0](n), start=False, stop=(k == NM - 1), skip_group_check=True)
                        if NM:
                            mm.then_inc(a_ready, 1)

                def loads_due(n, p):
                    return (n - p) * (8 * LOADS) + 16 * LOADS

                def pass_b(n, p, sl):
                    if not (isinstance(n, int) and n == 0 and sl < 2):
                        pe.wait_ge(p_ready, n * 8 + (sl - 1))
                    bank = bankB[sl % 2]
                    for t in range(2):
                        for x in range(2):
                            r = slice(64 * x, 64 * x + KR)
                            nc.tensor.matmul(bank[:, x, t * S:(t + 1) * S], KS[r, p, sl, t * P:(t + 1) * P], QS[r, p, sl, :], start=(t == 0), stop=False, skip_group_check=True)
                    for x in range(2):
                        for k in range(NM):
                            nc.tensor.matmul(bank[:, x, :], C.identb[:, :], A.masks[k][1](n), start=False, stop=False, skip_group_check=True)
                    for t in range(2):
                        for x in range(2):
                            r = slice(64 * x, 64 * x + 48)
                            mm = nc.tensor.matmul(bank[:, x, t * S:(t + 1) * S], sel[r, 2 * sl + x, :], NMT[r, p, :], start=False, stop=True, skip_group_check=True)
                    mm.then_inc(b_ready, 1)

                def values(n, p, sl):
                    pe.wait_ge(p_ready, n * 8 + (sl + 1))
                    if sl == 0:
                        pe.wait_ge(v_staged, n * 2 + 2)
                    if sl % 4 == 0 and not (isinstance(n, int) and n == 0 and sl == 0):
                        pe.wait_ge(o_kept, n * 2 + sl // 4)
                    for kt in range(2):
                        for x in range(2):
                            h = 2 * sl + x
                            out = bankO[VW * (h % 4):VW * (h % 4 + 1), (h // 4 % 2) * S:(h // 4 % 2 + 1) * S]
                            mm = nc.tensor.matmul(out, VB[:, p, kt, h, :], PT[:, sl % 2, x, kt, :], start=(kt == 0), stop=(kt == 1), skip_group_check=True)
                    mm.then_inc(pv_done, 1)

                def turn_max(n):
                    pe.wait_ge(nm_ready, n + 1)
                    for t in range(2):
                        mm = nc.tensor.transpose(NMP[:, t * P:(t + 1) * P], nm[:, t, :, :, :].rearrange("p a k h -> p (a k h)"), C.identb[:, :])
                    mm.then_inc(nm_turned, 1)

                def place_out(n, half):
                    pe.wait_ge(o_kept, n * 2 + (half + 1))
                    if half == 0 and not (isinstance(n, int) and n == 0):
                        pe.wait_ge(added, n)
                    for k in range(2):
                        for g in range(2):
                            mm = nc.tensor.matmul(bankT[:, k * S:(k + 1) * S], place[:, 2 * half + g, k, :], OH[:, half, g, :], start=(half == k == g == 0), stop=(half == g == 1), skip_group_check=True)
                    if half == 1:
                        mm.then_inc(o_placed, 1)

                def project(n):
                    pe.wait_ge(o_normed, n + 1)
                    nc.tensor.matmul(bankT[:, 0:S], A.wo, oT[:, :], start=True, stop=True, skip_group_check=True).then_inc(y_ready, 1)

                def batch(n, p, after, before):
                    pe.wait_ge(nm_kept, n + 1)
                    for sl in range(8):
                        pass_b(n, p, sl)
                        if after is not None:
                            pass_a(after, 1 - p, sl)
                        if sl == 5 and before:
                            project(n - 1)
                        if sl >= 1:
                            values(n, p, sl - 1)
                    values(n, p, 7)
                    place_out(n, 0)
                    if after is not None:
                        turn_max(after)
                    place_out(n, 1)

                for g in range(NG):
                    pass_a(0, 0, g)
                turn_max(0)
                batch(0, 0, 1, False)
                batch(1, 1, 2, True)
                with pe.Fori(1, B // 2 - 1) as i:
                    batch(i * 2, 0, i * 2 + 1, True)
                    batch(i * 2 + 1, 1, i * 2 + 2, True)
                batch(B - 2, 0, B - 1, True)
                batch(B - 1, 1, None, True)
                project(B - 1)

            @block.vector
            def _(dve):
                pairs = lambda a: a.rearrange("p a g n -> p (a g n)").bitcast(F32)
                nc.vector.memset(pairs(QS[32:64, :, :, :]), TWO_BF16_ONES)
                nc.vector.memset(pairs(QS[96:128, :, :, :]), TWO_BF16_ONES)
                nc.vector.memset(pairs(KS[32:64, :, :, :]), TWO_BF16_ONES)
                nc.vector.memset(pairs(KS[96:128, :, :, :]), TWO_BF16_ONES).then_inc(ones_set, 1)
                nc.vector.memset(VB[:, :, :, :, :], 0.0).then_inc(ones_set, 1)
                nc.vector.memset(nm[:, :, :, :, :], 0.0)

                def maximum(n, h):
                    dve.wait_ge(a_ready, n * NH + (h + 1))
                    nc.vector.tensor_reduce(mx[:, :, h], bankA[h % 2][:, :].rearrange("p (t k) -> p t k", t=2), AX.X, ALU.max).then_inc(a_max, 1)

                def split_max(n):
                    dve.wait_ge(a_max, n * NH + NH)
                    st = Steps(dve, own, n * 5)
                    st.then(nc.vector.tensor_scalar(nm[:, :, 0, 0, :], mx[:, :, :], -1.0, None, ALU.mult))
                    st.then(nc.vector.scalar_tensor_tensor(nr[:, :, :], mx[:, :, :], -1.0, nm[:, :, 0, 0, :], ALU.mult, ALU.subtract))
                    st.then(nc.vector.tensor_copy(nm[:, :, 0, 1, :], nr[:, :, :]))
                    st.then(nc.vector.tensor_tensor(nr[:, :, :], nr[:, :, :], nm[:, :, 0, 1, :], ALU.subtract))
                    st.then(nc.vector.tensor_copy(nm[:, :, 0, 2, :], nr[:, :, :]))
                    nc.vector.tensor_copy(nm[:, :, 1, 0:3, :], nm[:, :, 0, 0:3, :]).then_inc(nm_ready, 1)

                def invert(n, half):
                    dve.wait_ge(o_placed, n + 1)
                    nc.vector.reciprocal(rec[:, half * P:(half + 1) * P], bankT[:, S + half * P:S + (half + 1) * P]).then_inc(inverted, 1)

                def normalise(n):
                    dve.wait_ge(inverted, n * 2 + 2)
                    nc.vector.tensor_tensor(oT[:, :], bankT[:, 0:S], rec[:, :], ALU.mult).then_inc(o_normed, 1)

                def residual(n):
                    dve.wait_ge(y_ready, n + 1)
                    x = C.XT[:, bass.ds(n * S, S)]
                    nc.vector.scalar_tensor_tensor(x, bankT[:, 0:S], A.bo, x, ALU.add, ALU.add).then_inc(added, 1)

                def batch(n, after, before):
                    for sl in range(8):
                        if after is not None:
                            maximum(after, 2 * sl)
                            maximum(after, 2 * sl + 1)
                        if sl in (1, 2) and before:
                            invert(n - 1, sl - 1)
                        if sl == 3 and before:
                            normalise(n - 1)
                        if sl == 6 and before:
                            residual(n - 1)
                    if after is not None:
                        split_max(after)

                for h in range(NH):
                    maximum(0, h)
                split_max(0)
                batch(0, 1, False)
                batch(1, 2, True)
                with dve.Fori(1, B // 2 - 1) as i:
                    batch(i * 2, i * 2 + 1, True)
                    batch(i * 2 + 1, i * 2 + 2, True)
                batch(B - 2, B - 1, True)
                batch(B - 1, None, True)
                invert(B - 1, 0)
                invert(B - 1, 1)
                normalise(B - 1)
                residual(B - 1)

            @block.scalar
            def _(act):
                nc.scalar.preload_act_table_set(LN_EXP)

                def keep_max(n, p):
                    act.wait_ge(nm_turned, n + 1)
                    nc.scalar.activation(NMT[:, p, :], NMP, ACT.Copy).then_inc(nm_kept, 1)

                def weights(n, sl):
                    act.wait_ge(b_ready, n * 8 + (sl + 1))
                    if not (isinstance(n, int) and n == 0 and sl < 2):
                        act.wait_ge(pv_done, n * 8 + (sl - 1))
                    nc.scalar.activation(PT[:, sl % 2, :, :, :].rearrange("p x t s -> p x (t s)"), bankB[sl % 2], ACT.Exp, scale=A.scale).then_inc(p_ready, 1)

                def keep_out(n, half):
                    act.wait_ge(pv_done, n * 8 + (4 * half + 4))
                    if half == 0 and not (isinstance(n, int) and n == 0):
                        act.wait_ge(o_placed, n)
                    nc.scalar.activation(OH[:, half, :, :].rearrange("p g s -> p (g s)"), bankO[:, :], ACT.Copy).then_inc(o_kept, 1)

                def batch(n, p, after):
                    for sl in range(8):
                        weights(n, sl)
                        if sl == 4:
                            keep_out(n, 0)
                    keep_out(n, 1)
                    if after is not None:
                        keep_max(after, 1 - p)

                keep_max(0, 0)
                batch(0, 0, 1)
                batch(1, 1, 2)
                with act.Fori(1, B // 2 - 1) as i:
                    batch(i * 2, 0, i * 2 + 1)
                    batch(i * 2 + 1, 1, i * 2 + 2)
                batch(B - 2, 0, B - 1)
                batch(B - 1, 1, None)
    run_stage(nc, ["stacked00", "stacked01", "stacked10", "stacked11", "consts_in", "ones_set", "v_staged", "a_ready", "a_max", "nm_ready", "nm_turned", "nm_kept", "b_ready", "p_ready",
                   "pv_done", "o_kept", "o_placed", "o_normed", "inverted", "y_ready", "added", "own"], body)


def l1_prepare(nc, C, A):
    def body(loaded, made, turned, kept, wo_turned):
        with ExitStack() as s:
            sb = sbuf(nc, s)
            mi = sb("mi", [P, B, 2, S], I32)
            wo_rows = sb("wo_rows", [P, E])
            block = s.enter_context(nc.Block())

            @block.sync
            def _(sp):
                sp.dma_start(mi[:, :, :, :], C.i["mask_Bx1xSxS2_ik1"].rearrange("b o (t p) k -> p (b o) t k", p=P)).then_inc(loaded, 16)
                sp.dma_start(wo_rows[:, :], C.i["L1_xattn_W_out"]).then_inc(loaded, 16)
                sp.dma_start(A.bo_t[:, :], C.i["L1_xattn_b_out"].unsqueeze(1)).then_inc(loaded, 16)

            @block.vector
            def _(dve):
                nc.vector.memset(A.VA4[:, :, :, HD:HD + 1], 1.0)
                dve.wait_ge(loaded, 48)
                for b in range(B):
                    nc.vector.tensor_scalar(A.MQ[:, b, :, :], mi[:, b, :, :], 0, -1e20, ALU.is_equal, ALU.mult).then_inc(made, 1)
                nc.vector.tensor_copy(A.VA4[:, :, :, 0:HD], C.CN[:, :, :].rearrange("p n (h d) -> p n h d", h=NH))
                for b in range(B):
                    dve.wait_ge(turned, b + 1)
                    nc.vector.tensor_copy(A.MK[:, b, :, :].rearrange("p t s -> p (t s)"), C.ps[b][:, 0:S].bitcast(BF16)).then_inc(kept, 1)
                dve.wait_ge(wo_turned, 1)
                nc.vector.tensor_copy(A.wo_t[:, :], C.ps[0][:, 256:256 + P])

            @block.tensor
            def _(pe):
                for b in range(B):
                    pe.wait_ge(made, b + 1)
                    for kt in range(2):
                        for qt in range(2):
                            mm = nc.tensor.transpose(C.ps[b][:, 0:S].bitcast(BF16)[:, kt * S + qt * P:kt * S + (qt + 1) * P], A.MQ[:, b, qt, kt * P:(kt + 1) * P], C.identb[:, :])
                    mm.then_inc(turned, 1)
                pe.wait_ge(loaded, 48)
                pe.wait_ge(kept, 1)
                nc.tensor.transpose(C.ps[0][:, 256:256 + P], wo_rows[:, :], C.ident[:, :]).then_inc(wo_turned, 1)
    run_stage(nc, ["loaded", "made", "turned", "kept", "wo_turned"], body)


def l1_xattn(nc, C):
    layer_norm(nc, C, C.HT)
    split_parts(nc, C, C.HT, C.CT)
    A = Core()
    with ExitStack() as s:
        sb = sbuf(nc, s)
        A.MQ, A.MK = sb("MQ", [P, B, 2, S], BF16), sb("MK", [P, B, 2, S], BF16)
        A.wo_t, A.bo_t = sb("wo_t", [P, E]), sb("bo_t", [P, 1])
        VA = sb("VA", [P, NT, NH * (HD + 1)])
        A.VA, A.VA4 = VA, VA[:, :, :].rearrange("p n (h e) -> p n h e", h=NH)
        l1_prepare(nc, C, A)
        A.wo, A.bo = A.wo_t[:, :], A.bo_t[:, :]
        A.scale = float(E) ** -0.5
        A.key_mask = None
        MQf, MKf = A.MQ[:, :, :, :].rearrange("p b t s -> p (b t s)"), A.MK[:, :, :, :].rearrange("p b t s -> p (b t s)")
        A.masks = [(lambda b: MQf[:, bass.ds(b * (2 * S), 2 * S)], lambda b: MKf[:, bass.ds(b * (2 * S), 2 * S)])]
        attend(nc, C, A)


def project_qkv(nc, C, A):
    def body(qk_ready, qk_kept, v_ready, v_kept):
        with nc.Block() as block:
            jobs = [(w, src, dst, c) for w, src, dst in (("q", C.HT, A.QT), ("k", C.CT, A.KT)) for c in range(NCH)]

            @block.tensor
            def _(pe):
                for j, (w, src, dst, c) in enumerate(jobs):
                    if j >= 4:
                        pe.wait_ge(qk_kept, j - 3)
                    nc.tensor.matmul(C.ps[j % 4][:, :], A.w[w], src[:, c * CH:(c + 1) * CH], start=True, stop=True).then_inc(qk_ready, 1)
                for q in range(4):
                    for t in range(4):
                        n = 4 * q + t
                        mm = nc.tensor.matmul(C.ps[4 + q][:, t * P:(t + 1) * P], C.CT[:, n * P:(n + 1) * P], A.w["v"], start=True, stop=True)
                    mm.then_inc(v_ready, 1)

            @block.vector
            def _(dve):
                nc.vector.memset(A.VA4[:, :, :, HD:HD + 1], 1.0)
                for j, (w, src, dst, c) in enumerate(jobs):
                    dve.wait_ge(qk_ready, j + 1)
                    bias, scale = A.qk_bias[w]
                    nc.vector.tensor_scalar(dst[:, c * CH:(c + 1) * CH], C.ps[j % 4][:, :], bias, scale, ALU.add, ALU.mult).then_inc(qk_kept, 1)
                for q in range(4):
                    dve.wait_ge(v_ready, q + 1)
                    for t in range(4):
                        v = C.ps[4 + q][:, t * P:(t + 1) * P].rearrange("p (h d) -> p h d", h=NH)
                        dst = A.VA4[:, 4 * q + t, :, 0:HD]
                        if A.v_bias is None:
                            nc.vector.tensor_copy(dst, v).then_inc(v_kept, 1)
                        else:
                            nc.vector.tensor_tensor(dst, v, A.v_bias[:, :].rearrange("p (h d) -> p h d", h=NH), ALU.add).then_inc(v_kept, 1)
    run_stage(nc, ["qk_ready", "qk_kept", "v_ready", "v_kept"], body)


def l2_prepare(nc, C, A):
    def body(loaded, spread, rep_ready, rep_kept, mask_made, stored, own):
        with ExitStack() as s:
            sb = sbuf(nc, s)
            w8 = sb("w8", [HD, 3, HD])
            w8r = sb("w8r", [HD, 3, NH, HD])
            rep = sb("rep", [P, 3, HD])
            blk = sb("blk", [P, P])
            mi = sb("mi2", [8, S], I32)
            mb = sb("mb2", [8, S], BF16)
            wo_rows = sb("wo_rows2", [P, E])
            block = s.enter_context(nc.Block())

            @block.sync
            def _(sp):
                for n, name in enumerate(("Wq", "Wk", "Wv")):
                    sp.dma_start(w8[:, n, :], C.i[f"L2_xattn_{name}"]).then_inc(loaded, 16)
                sp.dma_start(wo_rows[:, :], C.i["L2_xattn_Wo"]).then_inc(loaded, 16)
                sp.dma_start(A.bo_t[:, :], C.i["L2_xattn_bo"].unsqueeze(1)).then_inc(loaded, 16)
                sp.dma_start(blk[:, :], C.c["head_blocks"]).then_inc(loaded, 16)
                sp.dma_start(mi[:, :], C.i["mask_Bx1x1xS2_if1"].rearrange("b o q k -> (b o q) k")).then_inc(loaded, 16)
                sp.wait_ge(mask_made, 1)
                sp.dma_start(C.key_bias, mb[:, :]).then_inc(stored, 16)
                sp.wait_ge(stored, 16)

            @block.vector
            def _(dve):
                dve.wait_ge(loaded, 16 * 7)
                nc.vector.tensor_scalar(mb[:, :], mi[:, :], 0, -1e20, ALU.is_equal, ALU.mult).then_inc(mask_made, 1)
                for n in range(3):
                    last = nc.vector.tensor_copy(w8r[:, n, :, :], w8[:, n, :].unsqueeze(1).to_broadcast([HD, NH, HD]))
                last.then_inc(spread, 1)
                dve.wait_ge(rep_ready, 1)
                nc.vector.tensor_copy(rep[:, :, :].rearrange("p n e -> p (n e)"), C.ps[0][:, 0:24]).then_inc(rep_kept, 1)
                nc.vector.tensor_copy(A.wo_t[:, :], C.ps[0][:, P:2 * P])
                dve.wait_ge(rep_kept, 1)
                for n in range(3):
                    nc.vector.tensor_tensor(A.bd[:, n, :].rearrange("p (h e) -> p h e", h=NH), blk[:, :].rearrange("p (h e) -> p h e", h=NH), rep[:, n, :].unsqueeze(1).to_broadcast([P, NH, HD]), ALU.mult)

            @block.tensor
            def _(pe):
                pe.wait_ge(spread, 1)
                for n in range(3):
                    nc.tensor.matmul(C.ps[0][:, n * HD:(n + 1) * HD], w8r[:, n, :, :].rearrange("k h d -> k (h d)"), C.ident[0:HD, 0:HD], start=(n == 0), stop=True, skip_group_check=True)
                nc.tensor.transpose(C.ps[0][:, P:2 * P], wo_rows[:, :], C.ident[:, :]).then_inc(rep_ready, 1)
    run_stage(nc, ["loaded", "spread", "rep_ready", "rep_kept", "mask_made", "stored", "own"], body)


def l2_xattn(nc, C):
    layer_norm(nc, C, C.HT)
    A = Core()
    with ExitStack() as s:
        sb = sbuf(nc, s)
        A.bd = sb("bd", [P, 3, P])
        A.wo_t, A.bo_t = sb("wo_t", [P, E]), sb("bo_t", [P, 1])
        VA = sb("VA", [P, NT, NH * (HD + 1)])
        A.VA, A.VA4 = VA, VA[:, :, :].rearrange("p n (h e) -> p n h e", h=NH)
        l2_prepare(nc, C, A)
        A.w = {"q": A.bd[:, 0, :], "k": A.bd[:, 1, :], "v": A.bd[:, 2, :]}
        A.qk_bias = {"q": (0.0, 1.0), "k": (0.0, 1.0)}
        A.v_bias = None
        with ExitStack() as s2:
            A.QT, A.KT = sbuf(nc, s2)("QT", [P, TOK]), sbuf(nc, s2)("KT", [P, TOK])
            project_qkv(nc, C, A)
            split_parts(nc, C, A.QT, A.KT)
        A.wo, A.bo = A.wo_t[:, :], A.bo_t[:, :]
        A.scale = float(E) ** -0.5
        A.key_mask = lambda t: C.key_bias[bass.ds(t, 1), :].unsqueeze(1).to_broadcast([1, NG // 2, S])
        A.masks = None
        attend(nc, C, A)


def l3x_prepare(nc, C, A):
    def body(loaded, made, turned, own):
        with ExitStack() as s:
            sb = sbuf(nc, s)
            mf, r = sb("mf", [P, 2, S]), sb("mr", [P, 2, S])
            block = s.enter_context(nc.Block())

            @block.sync
            def _(sp):
                sp.dma_start(mf[:, :, :], C.i["mask_1x1xSxS2_fk1"].rearrange("o b (t p) k -> p (o b t) k", p=P)).then_inc(loaded, 16)
                for n, name in enumerate("qkvo"):
                    sp.dma_start(A.wt[:, n, :], C.i[f"L3_xattn_w{name}"]).then_inc(loaded, 16)
                for n, name in enumerate("qko"):
                    sp.dma_start(A.bt[:, n:n + 1], C.i[f"L3_xattn_b{name}"].unsqueeze(1)).then_inc(loaded, 16)
                sp.dma_start(A.v_bias[:, :], C.i["L3_xattn_bv"].unsqueeze(0).to_broadcast([P, E])).then_inc(loaded, 16)

            @block.vector
            def _(dve):
                st = Steps(dve, own)
                dve.wait_ge(loaded, 16 * 9)
                st.then(nc.vector.tensor_scalar(mf[:, :, :], mf[:, :, :], -1000000000.0, None, ALU.mult))
                st.then(nc.vector.tensor_copy(A.MQ[:, 0, :, :], mf[:, :, :]))
                st.then(nc.vector.tensor_tensor(r[:, :, :], mf[:, :, :], A.MQ[:, 0, :, :], ALU.subtract))
                st.then(nc.vector.tensor_copy(A.MQ[:, 1, :, :], r[:, :, :]))
                st.then(nc.vector.tensor_tensor(r[:, :, :], r[:, :, :], A.MQ[:, 1, :, :], ALU.subtract))
                nc.vector.tensor_copy(A.MQ[:, 2, :, :], r[:, :, :]).then_inc(made, 1)
                for k in range(3):
                    dve.wait_ge(turned, k + 1)
                    nc.vector.tensor_copy(A.MK[:, k, :, :].rearrange("p t s -> p (t s)"), C.ps[k][:, 0:S].bitcast(BF16))

            @block.tensor
            def _(pe):
                pe.wait_ge(made, 1)
                for k in range(3):
                    for kt in range(2):
                        for qt in range(2):
                            mm = nc.tensor.transpose(C.ps[k][:, 0:S].bitcast(BF16)[:, kt * S + qt * P:kt * S + (qt + 1) * P], A.MQ[:, k, qt, kt * P:(kt + 1) * P], C.identb[:, :])
                    mm.then_inc(turned, 1)
    run_stage(nc, ["loaded", "made", "turned", "own"], body)


def l3_xattn(nc, C):
    layer_norm(nc, C, C.HT)
    A = Core()
    with ExitStack() as s:
        sb = sbuf(nc, s)
        A.wt, A.bt, A.v_bias = sb("w_qkvo", [P, 4, E]), sb("b_qko", [P, 3]), sb("v_bias", [P, E])
        A.MQ, A.MK = sb("MQ3", [P, 3, 2, S], BF16), sb("MK3", [P, 3, 2, S], BF16)
        VA = sb("VA", [P, NT, NH * (HD + 1)])
        A.VA, A.VA4 = VA, VA[:, :, :].rearrange("p n (h e) -> p n h e", h=NH)
        l3x_prepare(nc, C, A)
        A.w = {"q": A.wt[:, 0, :], "k": A.wt[:, 1, :], "v": A.wt[:, 2, :]}
        A.qk_bias = {"q": (A.bt[:, 0:1], float(HD) ** -0.5), "k": (A.bt[:, 1:2], 1.0)}
        with ExitStack() as s2:
            A.QT, A.KT = sbuf(nc, s2)("QT", [P, TOK]), sbuf(nc, s2)("KT", [P, TOK])
            project_qkv(nc, C, A)
            split_parts(nc, C, A.QT, A.KT)
        A.wo, A.bo = A.wt[:, 3, :], A.bt[:, 2:3]
        A.scale = 1.0
        A.key_mask = None
        A.masks = [(lambda b, k=k: A.MQ[:, k, :, :].rearrange("p t s -> p (t s)"), lambda b, k=k: A.MK[:, k, :, :].rearrange("p t s -> p (t s)")) for k in range(3)]
        attend(nc, C, A)


L1_I = 384
L1_IT = L1_I // P
BLK = 32
QM = 32767.0


def l1_ffn_weights(nc, C, F):
    def body(loaded, turned, kept, own):
        with ExitStack() as s:
            sb = sbuf(nc, s)
            w = sb("w_rows", [P, 9, E])
            t1 = sb("w_units", [P, 9, E])
            sc, inv = sb("w_scale", [P, 36]), sb("w_inv", [P, 36])
            block = s.enter_context(nc.Block())

            @block.sync
            def _(sp):
                for n, name in enumerate(("gate", "up")):
                    sp.dma_start(w[:, 3 * n:3 * n + 3, :], C.i[f"L1_ffn_w_{name}"].rearrange("(t p) h -> p t h", p=P)).then_inc(loaded, 16)
                sp.dma_start(w[:, 6:9, :], C.i["L1_ffn_w_down"].rearrange("h (t i) -> h t i", i=E)).then_inc(loaded, 16)

            @block.vector
            def _(dve):
                st = Steps(dve, own)
                dve.wait_ge(loaded, 48)
                W = lambda a: a[:, :, :].rearrange("p n (k i) -> p (n k) i", i=BLK)
                bc = lambda a: a[:, :].unsqueeze(2).to_broadcast([P, 36, BLK])
                st.then(nc.vector.tensor_reduce(sc[:, :], W(w), AX.X, ALU.max, apply_absolute_value=True))
                st.then(nc.vector.tensor_scalar(sc[:, :], sc[:, :], 1.0 / 7.0, 1e-12, ALU.mult, ALU.max))
                st.then(nc.vector.reciprocal(inv[:, :], sc[:, :]))
                st.then(nc.vector.tensor_tensor(W(t1), W(w), bc(inv), ALU.mult))
                st.then(nc.vector.tensor_scalar(t1[:, :, :], t1[:, :, :], -8.0, 7.0, ALU.max, ALU.min))
                st.then(nc.vector.tensor_scalar(t1[:, :, :], t1[:, :, :], MAGIC, MAGIC, ALU.add, ALU.subtract))
                st.then(nc.vector.tensor_tensor(W(w), W(t1), bc(sc), ALU.mult))
                for q in range(3):
                    dve.wait_ge(turned, q + 1)
                    nc.vector.tensor_copy(F.W[:, 3 * q:3 * q + 3, :].rearrange("p n h -> p (n h)"), C.ps[q][:, 0:384])

            @block.tensor
            def _(pe):
                pe.wait_ge(own, 7)
                for q in range(9):
                    mm = nc.tensor.transpose(C.ps[q // 3][:, (q % 3) * P:(q % 3 + 1) * P], w[:, q, :], C.ident[:, :])
                    if q % 3 == 2:
                        mm.then_inc(turned, 1)
    run_stage(nc, ["loaded", "turned", "kept", "own"], body)


def l1_ffn_body(nc, C, F):
    N3 = 3 * TOK
    def body(xmax, piece_max, spread, x_ready, gu_ready, gu_kept, sig_in, sig_out, o_int, y_ready, added, own):
        with ExitStack() as s:
            sb = sbuf(nc, s)
            U, G, SG = sb("U", [P, 3, TOK]), sb("G", [P, 3, TOK]), sb("SG", [P, 3, TOK])
            m = sb("m_part", [P, 8])
            pieces = sb("m_pieces", [P, 2, 12])
            am = sb("m_all", [P, 8])
            sc = sb("sc16", [P, 8])
            iv = sb("iv16", [P, 8])
            block = s.enter_context(nc.Block())
            X, UP, GT, G2, OO = range(5)
            flat = lambda a: a[:, :, :].rearrange("p t n -> p (t n)")

            @block.gpsimd
            def _(pool):
                for k in range(5):
                    pool.wait_ge(xmax, k + 1)
                    nc.gpsimd.partition_all_reduce(am[:, k:k + 1], m[:, k:k + 1], P, RMAX).then_inc(spread, 1)

            @block.vector
            def _(dve):
                st = Steps(dve, own)

                def scale_of(k):
                    dve.wait_ge(spread, k + 1)
                    st.then(nc.vector.tensor_scalar(sc[:, k:k + 1], am[:, k:k + 1], 1.0 / QM, 1e-12, ALU.mult, ALU.max))
                    st.then(nc.vector.reciprocal(iv[:, k:k + 1], sc[:, k:k + 1]))

                def to_int(a, k, last=None):
                    st.then(nc.vector.tensor_scalar(a, a, iv[:, k:k + 1], -QM - 1.0, ALU.mult, ALU.max))
                    st.then(nc.vector.tensor_scalar(a, a, QM, MAGIC, ALU.min, ALU.add))

                nc.vector.tensor_reduce(m[:, X:X + 1], C.HT[:, :], AX.X, ALU.max, apply_absolute_value=True).then_inc(xmax, 1)
                scale_of(X)
                to_int(C.HT[:, :], X)
                nc.vector.tensor_scalar(C.HT[:, :], C.HT[:, :], MAGIC, sc[:, X:X + 1], ALU.subtract, ALU.mult).then_inc(x_ready, 1)
                for c in range(NCH):
                    for t in range(3):
                        j = c * 3 + t
                        dve.wait_ge(gu_ready, j + 1)
                        nc.vector.tensor_copy(U[:, t, c * CH:(c + 1) * CH], C.ps[2 * (j % 3) + 1][:, :]).then_inc(gu_kept, 1)
                        dve.wait_ge(sig_in, j + 1)
                        nc.vector.tensor_reduce(pieces[:, 1, j:j + 1], G[:, t, c * CH:(c + 1) * CH], AX.X, ALU.max, apply_absolute_value=True).then_inc(piece_max, 1)
                        dve.wait_ge(gu_kept, j + 1)
                        nc.vector.tensor_reduce(pieces[:, 0, j:j + 1], U[:, t, c * CH:(c + 1) * CH], AX.X, ALU.max, apply_absolute_value=True).then_inc(piece_max, 1)
                dve.wait_ge(piece_max, 24)
                nc.vector.tensor_reduce(m[:, UP:UP + 1], pieces[:, 0, :], AX.X, ALU.max).then_inc(xmax, 1)
                nc.vector.tensor_reduce(m[:, GT:GT + 1], pieces[:, 1, :], AX.X, ALU.max).then_inc(xmax, 1)
                scale_of(GT)
                to_int(flat(G), GT)
                nc.vector.tensor_scalar(flat(G), flat(G), MAGIC, sc[:, GT:GT + 1], ALU.subtract, ALU.mult).then_inc(x_ready, 1)
                scale_of(UP)
                to_int(flat(U), UP)
                st.then(nc.vector.tensor_scalar(flat(U), flat(U), MAGIC, sc[:, UP:UP + 1], ALU.subtract, ALU.mult))
                dve.wait_ge(sig_out, 3)
                st.then(nc.vector.tensor_scalar(flat(SG), flat(SG), 65536.0, 0.0, ALU.mult, ALU.max))
                st.then(nc.vector.tensor_scalar(flat(SG), flat(SG), 65535.0, MAGIC, ALU.min, ALU.add))
                st.then(nc.vector.tensor_scalar(flat(SG), flat(SG), MAGIC, 1.0 / 65536.0, ALU.subtract, ALU.mult))
                st.then(nc.vector.tensor_tensor(flat(G), flat(G), flat(SG), ALU.mult))
                nc.vector.tensor_reduce(m[:, G2:G2 + 1], flat(G), AX.X, ALU.max, apply_absolute_value=True).then_inc(xmax, 1)
                scale_of(G2)
                to_int(flat(G), G2)
                st.then(nc.vector.tensor_scalar(flat(G), flat(G), MAGIC, sc[:, G2:G2 + 1], ALU.subtract, ALU.mult))
                st.then(nc.vector.tensor_tensor(flat(G), flat(G), flat(U), ALU.mult))
                nc.vector.tensor_reduce(m[:, OO:OO + 1], flat(G), AX.X, ALU.max, apply_absolute_value=True).then_inc(xmax, 1)
                scale_of(OO)
                for t in range(3):
                    to_int(G[:, t, :], OO)
                    nc.vector.tensor_scalar(G[:, t, :], G[:, t, :], MAGIC, sc[:, OO:OO + 1], ALU.subtract, ALU.mult).then_inc(o_int, 1)
                for c in range(NCH):
                    dve.wait_ge(y_ready, c + 1)
                    x = C.XT[:, c * CH:(c + 1) * CH]
                    nc.vector.tensor_tensor(x, x, C.ps[c][:, :], ALU.add).then_inc(added, 1)

            @block.scalar
            def _(act):
                for c in range(NCH):
                    for t in range(3):
                        j = c * 3 + t
                        act.wait_ge(gu_ready, j + 1)
                        nc.scalar.activation(G[:, t, c * CH:(c + 1) * CH], C.ps[2 * (j % 3)][:, :], ACT.Copy).then_inc(sig_in, 1)
                act.wait_ge(x_ready, 2)
                for t in range(3):
                    nc.scalar.activation(SG[:, t, :], G[:, t, :], ACT.Sigmoid).then_inc(sig_out, 1)

            @block.tensor
            def _(pe):
                pe.wait_ge(x_ready, 1)
                for c in range(NCH):
                    for t in range(3):
                        j = c * 3 + t
                        if j >= 3:
                            pe.wait_ge(gu_kept, j - 2)
                            pe.wait_ge(sig_in, j - 2)
                        x = C.HT[:, c * CH:(c + 1) * CH]
                        nc.tensor.matmul(C.ps[2 * (j % 3)][:, :], F.W[:, t, :], x, start=True, stop=True)
                        nc.tensor.matmul(C.ps[2 * (j % 3) + 1][:, :], F.W[:, 3 + t, :], x, start=True, stop=True).then_inc(gu_ready, 1)
                pe.wait_ge(gu_kept, 12)
                pe.wait_ge(sig_in, 12)
                for t in range(3):
                    pe.wait_ge(o_int, t + 1)
                    for c in range(NCH):
                        mm = nc.tensor.matmul(C.ps[c][:, :], F.W[:, 6 + t, :], G[:, t, c * CH:(c + 1) * CH], start=(t == 0), stop=(t == 2))
                        if t == 2:
                            mm.then_inc(y_ready, 1)
    run_stage(nc, ["xmax", "piece_max", "spread", "x_ready", "gu_ready", "gu_kept", "sig_in", "sig_out", "o_int", "y_ready", "added", "own"], body)


def l1_ffn(nc, C):
    layer_norm(nc, C, C.HT)
    F = Core()
    with nc.sbuf_tensor("l1_w", [P, 9, E], F32) as F.W:
        l1_ffn_weights(nc, C, F)
        l1_ffn_body(nc, C, F)


ATTENTION_LOADS = 10


def load_attention(sp, C, L, layer, loaded):
    H2 = LD // 2
    wq = C.i["L2_ffn_Wqkv"][bass.ds(layer, 1), :, :].rearrange("o p n -> p (o n)")
    for k in range(3):
        sp.dma_start(L.Wqkv[:, k * INNER:(k + 1) * INNER], wq[:, k * INNER:(k + 1) * INNER]).then_inc(loaded, 16)
    sp.dma_start(L.Wo[:, :, :], C.i["L2_ffn_Wo"][bass.ds(layer, 1), :, :].rearrange("o (g p) n -> p (o g) n", p=P)).then_inc(loaded, 16)
    for n, name in enumerate("qk"):
        v = C.i[f"L2_ffn_{name}_scale"][bass.ds(layer, 1), :]
        sp.dma_start(L.scl[:, n, :], v.to_broadcast([P, LD])).then_inc(loaded, 16)
        sp.dma_start(L.scw[:, n, 0:H2], v[:, H2:LD].to_broadcast([P, H2])).then_inc(loaded, 16)
        sp.dma_start(L.scw[:, n, H2:LD], v[:, 0:H2].to_broadcast([P, H2])).then_inc(loaded, 16)


def first_weights(nc, C, L):
    def body(loaded):
        with nc.Block() as block:
            @block.sync
            def _(sp):
                sp.dma_start(L.base[:, :, :, :, :], C.c["rotary"]).then_inc(loaded, 16)
                sp.dma_start(L.win[:, :, :, :], C.c["window"]).then_inc(loaded, 16)
                load_attention(sp, C, L, 0, loaded)
                sp.wait_ge(loaded, 16 * (2 + ATTENTION_LOADS))
    run_stage(nc, ["loaded"], body)


LDEPTH, LH, LD, WIN = 6, 16, 64, 32
INNER = LH * LD
FI = int(E * 4 * 2 / 3)
FIT = [(0, 128), (128, 128), (256, FI - 256)]
KW = WIN + P
SH = 20
FRONT_ROUNDS = 10
HH = LH // 2


def local_attention(nc, C, L, layer):
    def body(ffn_loaded, tables, xs_ready, f_full, f_free, t1_ready, swapped, t2_ready, n2_summed, n2_ready, root_ready, rot_ready, s_ready, e_ready, x_ready, t_ready, pt_kept, o_ready,
             o_kept, w_full, w_free, v_moved, own_b, own_f, own_a, own_t):
        with ExitStack() as s:
            sb = sbuf(nc, s)
            TA = sb("TA", [P, 2, 2, LD])
            TB = sb("TB", [P, 2, 2, LD])
            lnb = sb("lnb", [P, 1])
            xs = sb("xs", [P, S])
            qk = sb("qk", [P, 2, LH, LD])
            sq = sb("sqk", [P, 2, LH, LD])
            t1 = sb("t1", [P, 2, LH, LD])
            t2 = sb("t2", [P, 2, LH, LD])
            n2, ry, ry2, rt = (sb(n, [P, 2, 2, HH]) for n in ("n2", "ry", "ry2", "rt"))
            qT = sb("qTl", [P, 2, 8, P])
            kT = sb("kTl", [P, 2, 8, KW])
            VV = sb("VV", [P, 2, LH, LD + 1])
            VP = sb("VP", [WIN, LH, LD + 1])
            mx = sb("mxl", [P, 2, 2, 2])
            e = sb("el", [P, 2, 2, 2, KW])
            pO, pP = sb("pO", [P, 2, 4, P]), sb("pP", [WIN, 2, 4, WIN])
            rec = sb("recl", [P, 4])
            ob = sb("ob", [P, LH, LD])
            oT = sb("oTl", [P, 8, P])
            block = s.enter_context(nc.Block())
            SC = (C.psum[:, 2:4, :], C.psum[:, 4:6, :])
            bankO, bankW = C.ps[6], C.ps[7]
            Wqkv, Wo, scl, scw, base, win = L.Wqkv, L.Wo, L.scl, L.scw, L.base, L.win

            @block.sync
            def _(sp):
                one = lambda name: C.i[f"L2_ffn_{name}"][bass.ds(layer, 1)]
                sp.dma_start(L.W1[:, :], one("W1").rearrange("o p n -> p (o n)")).then_inc(ffn_loaded, 16)
                for t, (i0, n) in enumerate(FIT):
                    sp.dma_start(L.W2[0:n, t, :], one("W2")[:, i0:i0 + n, :].rearrange("o p n -> p (o n)")).then_inc(ffn_loaded, 16)
                    for a in range(2):
                        sp.dma_start(L.b1[0:n, a, t:t + 1], one("b1")[:, a * FI + i0:a * FI + i0 + n].rearrange("o p -> p o")).then_inc(ffn_loaded, 16)
                for k, name in enumerate(("b2", "ln_g", "ln_b")):
                    sp.dma_start(L.cols[:, k:k + 1], one(name).rearrange("o p -> p o")).then_inc(ffn_loaded, 16)
                sp.wait_ge(ffn_loaded, 16 * 13)

            @block.tensor
            def _(pe):
                def front(u, r, first, batches):
                    J, p = u
                    if not (first and r < 2):
                        pe.wait_ge(f_free, J * FRONT_ROUNDS + (r - 1))
                    if r == 0 and p == 0:
                        pe.wait_ge(xs_ready, batches)
                    F = C.ps[r % 2]
                    if r < 6:
                        kind, half = (r % 2, r // 2) if r < 4 else (2, r - 4)
                        w = kind * INNER + half * CH
                        mm = nc.tensor.matmul(F[:, :], xs[:, p * P:(p + 1) * P], Wqkv[:, w:w + CH], start=True, stop=True)
                    else:
                        kind, half = r % 2, (r - 6) // 2
                        if kind == 0:
                            pe.wait_ge(rot_ready, J * 2 + (half + 1))
                        for g in range(4):
                            h = HH * half + 2 * g
                            mm = nc.tensor.transpose(F[:, g * P:(g + 1) * P], t1[:, kind, h:h + 2, :].rearrange("p h d -> p (h d)"), C.ident[:, :])
                    mm.then_inc(f_full, 1)

                def scores(u, c, moved):
                    J, p = u
                    if c == 0:
                        pe.wait_ge(f_free, J * FRONT_ROUNDS + 8)
                        if p == 1:
                            pe.wait_ge(v_moved, moved)
                    if c == 1 and not (isinstance(J, int) and J == 0):
                        pe.wait_ge(pt_kept, J * 4)
                    if c == 2:
                        pe.wait_ge(f_free, J * FRONT_ROUNDS + 10)
                    if c >= 2:
                        pe.wait_ge(pt_kept, J * 4 + (c - 1))
                    for x in range(2):
                        for hh in range(2):
                            r = slice(64 * hh, 64 * hh + 64)
                            nc.tensor.matmul(SC[c % 2][:, hh, x * KW:(x + 1) * KW], qT[r, p, 2 * c + x, :], kT[r, p, 2 * c + x, :], start=(x == 0), stop=False, skip_group_check=True)
                    for hh in range(2):
                        mm = nc.tensor.matmul(SC[c % 2][:, hh, 0:2 * KW], C.identb[:, :], win[:, p, :, :].rearrange("p x k -> p (x k)"), start=False, stop=True, skip_group_check=True)
                    mm.then_inc(s_ready, 1)

                def turn_p(u, c):
                    J, p = u
                    pe.wait_ge(x_ready, J * 4 + (c + 1))
                    for hh in range(2):
                        for x in range(2):
                            k = 2 * x + hh
                            mm = nc.tensor.transpose(SC[c % 2][:, 0, k * P:(k + 1) * P], e[:, c % 2, hh, x, WIN:KW], C.ident[:, :])
                            if p == 1:
                                mm = nc.tensor.transpose(SC[c % 2][0:WIN, 1, k * WIN:(k + 1) * WIN], e[0:WIN, c % 2, hh, x, 0:WIN], C.ident[0:WIN, 0:WIN])
                    mm.then_inc(t_ready, 1)

                def values(u, c, first):
                    J, p = u
                    pe.wait_ge(pt_kept, J * 4 + (c + 1))
                    if not (first and c == 0):
                        pe.wait_ge(o_kept, J * 4 + c)
                    for k in range(4):
                        h = 4 * c + k
                        out = bankO[:, k * (LD + 1):(k + 1) * (LD + 1)]
                        mm = nc.tensor.matmul(out, pO[:, c % 2, k, :], VV[:, p, h, :], start=True, stop=(p == 0), skip_group_check=True)
                        if p == 1:
                            mm = nc.tensor.matmul(out[0:WIN, :], pP[:, c % 2, k, :], VP[:, h, :], start=False, stop=True, skip_group_check=True)
                    mm.then_inc(o_ready, 1)

                def turn_o(u, half, first):
                    J, p = u
                    pe.wait_ge(o_kept, J * 4 + 2 * half + 2)
                    if not (first and half == 0):
                        pe.wait_ge(w_free, J * 3 + half)
                    for g in range(4):
                        mm = nc.tensor.transpose(bankW[:, g * P:(g + 1) * P], ob[:, 8 * half + 2 * g:8 * half + 2 * g + 2, :].rearrange("p h d -> p (h d)"), C.ident[:, :])
                    mm.then_inc(w_full, 1)

                def project(J):
                    pe.wait_ge(w_free, J * 3 + 2)
                    for g in range(8):
                        mm = nc.tensor.matmul(bankW[:, 0:P], Wo[:, g, :], oT[:, g, :], start=(g == 0), stop=(g == 7))
                    mm.then_inc(w_full, 1)

                def steps(bk, fr, batches, moved, first=False, before=True):
                    if bk is None:
                        for r in range(8):
                            front(fr, r, first, batches)
                        return
                    f = (lambda r: front(fr, r, False, batches)) if fr is not None else (lambda r: None)
                    last = (bk[0] - 1, 1 - bk[1])
                    scores(bk, 0, moved)
                    if before:
                        values(last, 3, False)
                    scores(bk, 1, moved)
                    front(bk, 8, False, batches)
                    front(bk, 9, False, batches)
                    if before:
                        turn_o(last, 1, False)
                    f(0)
                    f(1)
                    turn_p(bk, 0)
                    if before:
                        project(bk[0] - 1)
                    turn_p(bk, 1)
                    values(bk, 0, not before)
                    scores(bk, 2, moved)
                    f(2)
                    f(3)
                    values(bk, 1, False)
                    scores(bk, 3, moved)
                    turn_p(bk, 2)
                    turn_o(bk, 0, not before)
                    f(4)
                    f(5)
                    values(bk, 2, False)
                    f(6)
                    turn_p(bk, 3)
                    f(7)

                steps(None, (0, 0), 1, None, first=True)
                steps((0, 0), (1, 1), 1, None, before=False)
                steps((1, 1), (2, 0), 2, 1)
                with pe.Fori(1, B - 1) as b:
                    steps((b * 2, 0), (b * 2 + 1, 1), b + 1, None)
                    steps((b * 2 + 1, 1), (b * 2 + 2, 0), b + 2, b + 1)
                steps((2 * B - 2, 0), (2 * B - 1, 1), B, None)
                steps((2 * B - 1, 1), None, None, B)
                values((2 * B - 1, 1), 3, False)
                turn_o((2 * B - 1, 1), 1, False)
                project(2 * B - 1)

            @block.vector
            def _(dve):
                nc.vector.memset(xs[64:P, 0:1], 0.0)
                nc.vector.memset(kT[:, 0, :, 0:WIN], 0.0)
                nc.vector.memset(VV[:, :, :, LD:LD + 1], 1.0)
                nc.vector.memset(lnb[:, :], 0.5 * SH * float(np.log(2.0))).then_inc(own_t, 1)
                for p in range(2):
                    nc.vector.tensor_tensor(TA[:, p, :, :], base[:, 0, p, :, :], scl[:, :, :], ALU.mult)
                    last = nc.vector.tensor_tensor(TB[:, p, :, :], base[:, 1, p, :, :], scw[:, :, :], ALU.mult)
                last.then_inc(tables, 1)

                def shift(b, first):
                    if not first:
                        dve.wait_ge(f_full, (b * 2 - 1) * FRONT_ROUNDS + 6)
                    nc.vector.tensor_copy(xs[0:64, :], C.XT[0:64, bass.ds(b * S, S)])
                    nc.vector.tensor_copy(xs[64:P, 1:S], C.XT[64:P, bass.ds(b * S, S - 1)]).then_inc(xs_ready, 1)

                def front_a(u, half):
                    J, p = u
                    H = slice(HH * half, HH * half + HH)
                    dve.wait_ge(f_free, J * FRONT_ROUNDS + (2 * half + 2))
                    nc.vector.tensor_reduce(n2[:, half, :, :], sq[:, :, H, :], AX.X, ALU.add).then_inc(n2_summed, 1)
                    nc.vector.tensor_tensor(t1[:, :, H, :], qk[:, :, H, :], TA[:, p, :, :].unsqueeze(2).to_broadcast([P, 2, HH, LD]), ALU.mult).then_inc(t1_ready, 1)
                    dve.wait_ge(n2_summed, J * 2 + (half + 1))
                    nc.vector.tensor_scalar(n2[:, half, :, :], n2[:, half, :, :], 1e-24, None, ALU.max).then_inc(n2_ready, 1)

                def front_scale(u, half, st):
                    J, p = u
                    H = slice(HH * half, HH * half + HH)
                    x = rt[:, half, :, :]
                    dve.wait_ge(root_ready, J * 2 + (half + 1))
                    dve.wait_ge(n2_ready, J * 2 + (half + 1))
                    st.then(nc.vector.tensor_tensor(x, n2[:, half, :, :], ry2[:, half, :, :], ALU.mult))
                    st.then(nc.vector.tensor_scalar(x, x, -0.5, 1.5, ALU.mult, ALU.add))
                    st.then(nc.vector.tensor_tensor(x, x, ry[:, half, :, :], ALU.mult))
                    dve.wait_ge(t2_ready, J * 2 + (half + 1))
                    nc.vector.tensor_tensor(t1[:, :, H, :], t1[:, :, H, :], x.unsqueeze(3).to_broadcast([P, 2, HH, LD]), ALU.mult).then_inc(rot_ready, 1)

                def centre(u, c, st):
                    J, p = u
                    dve.wait_ge(s_ready, J * 4 + (c + 1))
                    v = SC[c % 2][:, :, 0:2 * KW].rearrange("p a (x k) -> p a x k", x=2)
                    st.then(nc.vector.tensor_reduce(mx[:, c % 2, :, :], v, AX.X, ALU.max))
                    if c >= 2:
                        dve.wait_ge(t_ready, J * 4 + (c - 1))
                    for hh in range(2):
                        last = nc.vector.tensor_tensor(e[:, c % 2, hh, :, :], v[:, hh, :, :], mx[:, c % 2, hh, :].unsqueeze(2).to_broadcast([P, 2, KW]), ALU.subtract)
                    last.then_inc(e_ready, 1)

                def normalise(u, c, st):
                    J, p = u
                    dve.wait_ge(o_ready, J * 4 + (c + 1))
                    v = bankO[:, 0:4 * (LD + 1)].rearrange("p (k d) -> p k d", k=4)
                    st.then(nc.vector.reciprocal(rec[:, :], v[:, :, LD]))
                    nc.vector.tensor_tensor(ob[:, 4 * c:4 * c + 4, :], v[:, :, 0:LD], rec[:, :].unsqueeze(2).to_broadcast([P, 4, LD]), ALU.mult).then_inc(o_kept, 1)

                def residual(J):
                    dve.wait_ge(w_full, J * 3 + 3)
                    x = C.XT[:, bass.ds(J * P, P)] if not isinstance(J, int) else C.XT[:, J * P:(J + 1) * P]
                    nc.vector.tensor_tensor(x, x, bankW[:, 0:P], ALU.add).then_inc(w_free, 1)

                def steps(bk, fr, batch=None, first=False, prev=True):
                    if batch is not None:
                        shift(batch, first)
                    if fr is not None:
                        st = Steps(dve, own_f, fr[0] * 6)
                    if bk is None:
                        for half in range(2):
                            front_a(fr, half)
                        for half in range(2):
                            front_scale(fr, half, st)
                        return
                    sb_ = Steps(dve, own_b, bk[0] * 8 - 1 if prev else 0)
                    centre(bk, 0, sb_)
                    if prev:
                        normalise((bk[0] - 1, None), 3, sb_)
                    centre(bk, 1, sb_)
                    if fr is not None:
                        front_a(fr, 0)
                    if prev:
                        residual(bk[0] - 1)
                    normalise(bk, 0, sb_)
                    centre(bk, 2, sb_)
                    normalise(bk, 1, sb_)
                    if fr is not None:
                        front_scale(fr, 0, st)
                    centre(bk, 3, sb_)
                    if fr is not None:
                        front_a(fr, 1)
                    normalise(bk, 2, sb_)
                    if fr is not None:
                        front_scale(fr, 1, st)
                    assert sb_.n == (8 if prev else 7)

                dve.wait_ge(tables, 1)
                steps(None, (0, 0), 0, True)
                steps((0, 0), (1, 1), prev=False)
                steps((1, 1), (2, 0), 1)
                with dve.Fori(1, B - 1) as b:
                    steps((b * 2, 0), (b * 2 + 1, 1))
                    steps((b * 2 + 1, 1), (b * 2 + 2, 0), b + 1)
                steps((2 * B - 2, 0), (2 * B - 1, 1))
                steps((2 * B - 1, 1), None)
                normalise((2 * B - 1, None), 3, Steps(dve, own_b, 2 * B * 8 - 1))
                residual(2 * B - 1)

            @block.gpsimd
            def _(pool):
                pool.wait_ge(tables, 1)

                def swap(u):
                    J, p = u
                    H2 = LD // 2
                    for half in range(2):
                        H = slice(HH * half, HH * half + HH)
                        pool.wait_ge(f_free, J * FRONT_ROUNDS + (2 * half + 2))
                        for d in range(2):
                            nc.gpsimd.tensor_tensor(t2[:, :, H, d * H2:(d + 1) * H2], qk[:, :, H, (1 - d) * H2:(2 - d) * H2],
                                                    TB[:, p, :, d * H2:(d + 1) * H2].unsqueeze(2).to_broadcast([P, 2, HH, H2]), ALU.mult).then_inc(swapped, 1)
                        pool.wait_ge(swapped, J * 4 + (2 * half + 2))
                        pool.wait_ge(t1_ready, J * 2 + (half + 1))
                        nc.gpsimd.tensor_tensor(t1[:, :, H, :], t1[:, :, H, :], t2[:, :, H, :], ALU.add).then_inc(t2_ready, 1)

                with pool.Fori(0, B) as b:
                    swap((b * 2, 0))
                    swap((b * 2 + 1, 1))

            @block.scalar
            def _(act):
                nc.scalar.preload_act_table_set(LN_EXP)
                act.wait_ge(own_t, 1)

                def keep_front(u, r, first):
                    J, p = u
                    act.wait_ge(f_full, J * FRONT_ROUNDS + (r + 1))
                    F = C.ps[r % 2]
                    heads = F.rearrange("p (h d) -> p h d", h=HH)
                    if r < 4:
                        kind, half = r % 2, r // 2
                        if kind == 0 and not first:
                            act.wait_ge(t2_ready, J * 2 + (half - 1))
                            act.wait_ge(rot_ready, J * 2 + (half - 1))
                        H = slice(HH * half, HH * half + HH)
                        nc.scalar.activation(qk[:, kind, H, :], heads, ACT.Copy)
                        nc.scalar.activation(sq[:, kind, H, :], heads, ACT.Square).then_inc(f_free, 1)
                    elif r < 6:
                        H = slice(HH * (r - 4), HH * (r - 4) + HH)
                        nc.scalar.activation(VV[:, p, H, 0:LD], heads, ACT.Copy).then_inc(f_free, 1)
                        if r == 5 and p == 1:
                            nc.scalar.activation(VP[:, :, :], VV[P - WIN:P, 0, :, :], ACT.Copy)
                            nc.scalar.activation(kT[:, 1, :, 0:WIN], kT[:, 0, :, P:KW], ACT.Copy).then_inc(v_moved, 1)
                    else:
                        kind, half = r % 2, (r - 6) // 2
                        G = slice(4 * half, 4 * half + 4)
                        dst = qT[:, p, G, :] if kind == 0 else kT[:, p, G, WIN:KW]
                        nc.scalar.activation(dst, F.rearrange("p (g q) -> p g q", g=4), ACT.Copy).then_inc(f_free, 1)

                def root(u, half):
                    J, p = u
                    act.wait_ge(n2_ready, J * 2 + (half + 1))
                    st = Steps(act, own_a, J * 4 + 2 * half)
                    st.then(nc.scalar.activation(ry2[:, half, :, :], n2[:, half, :, :], ACT.Ln, scale=float(2.0 ** SH)))
                    st.then(nc.scalar.activation(ry[:, half, :, :], ry2[:, half, :, :], ACT.Exp, scale=-0.5, bias=lnb[:, :]))
                    nc.scalar.activation(ry2[:, half, :, :], ry[:, half, :, :], ACT.Square).then_inc(root_ready, 1)

                def weights(u, c):
                    J, p = u
                    act.wait_ge(e_ready, J * 4 + (c + 1))
                    v = e[:, c % 2, :, :, :].rearrange("p a x k -> p (a x k)")
                    nc.scalar.activation(v, v, ACT.Exp, scale=8.0).then_inc(x_ready, 1)

                def keep_p(u, c):
                    J, p = u
                    act.wait_ge(t_ready, J * 4 + (c + 1))
                    if c >= 2:
                        act.wait_ge(o_ready, J * 4 + (c - 1))
                    if c == 1 and not (isinstance(J, int) and J == 0):
                        act.wait_ge(o_ready, J * 4)
                    if p == 1:
                        nc.scalar.activation(pP[:, c % 2, :, :].rearrange("p k q -> p (k q)"), SC[c % 2][0:WIN, 1, 0:4 * WIN], ACT.Copy)
                    nc.scalar.activation(pO[:, c % 2, :, :].rearrange("p k q -> p (k q)"), SC[c % 2][:, 0, :], ACT.Copy).then_inc(pt_kept, 1)

                def keep_o(u, half):
                    J, p = u
                    act.wait_ge(w_full, J * 3 + (half + 1))
                    nc.scalar.activation(oT[:, 4 * half:4 * half + 4, :].rearrange("p g q -> p (g q)"), bankW, ACT.Copy).then_inc(w_free, 1)

                def steps(bk, fr, first=False, before=True):
                    if bk is None:
                        for r in range(6):
                            keep_front(fr, r, first)
                        for half in range(2):
                            root(fr, half)
                        for r in range(6, 8):
                            keep_front(fr, r, first)
                        return
                    f = (lambda r: keep_front(fr, r, False)) if fr is not None else (lambda r: None)
                    weights(bk, 0)
                    keep_front(bk, 8, False)
                    keep_front(bk, 9, False)
                    weights(bk, 1)
                    if before:
                        keep_o((bk[0] - 1, None), 1)
                    f(0)
                    f(1)
                    keep_p(bk, 0)
                    keep_p(bk, 1)
                    if fr is not None:
                        root(fr, 0)
                    f(2)
                    weights(bk, 2)
                    f(3)
                    keep_p(bk, 2)
                    keep_o(bk, 0)
                    f(4)
                    weights(bk, 3)
                    f(5)
                    f(6)
                    keep_p(bk, 3)
                    f(7)
                    if fr is not None:
                        root(fr, 1)

                steps(None, (0, 0), True)
                steps((0, 0), (1, 1), before=False)
                steps((1, 1), (2, 0))
                with act.Fori(1, B - 1) as b:
                    steps((b * 2, 0), (b * 2 + 1, 1))
                    steps((b * 2 + 1, 1), (b * 2 + 2, 0))
                steps((2 * B - 2, 0), (2 * B - 1, 1))
                steps((2 * B - 1, 1), None)
                keep_o((2 * B - 1, None), 1)
    run_stage(nc, ["ffn_loaded", "tables", "xs_ready", "f_full", "f_free", "t1_ready", "swapped", "t2_ready", "n2_summed", "n2_ready", "root_ready", "rot_ready", "s_ready", "e_ready", "x_ready", "t_ready",
                   "pt_kept", "o_ready", "o_kept", "w_full", "w_free", "v_moved", "own_b", "own_f", "own_a", "own_t"], body)


def shift_tokens(nc, C, L):
    def body(shifted):
        with nc.Block() as block:
            @block.vector
            def _(dve):
                v = lambda t: t[64:P, :].rearrange("p (b s) -> p b s", b=B)
                nc.vector.memset(v(L.XS)[:, :, 0:1], 0.0)
                nc.vector.tensor_copy(L.XS[0:64, :], C.XT[0:64, :])
                nc.vector.tensor_copy(v(L.XS)[:, :, 1:S], v(C.XT)[:, :, 0:S - 1]).then_inc(shifted, 1)
    run_stage(nc, ["shifted"], body)


def geglu(nc, C, L, layer_after):
    def body(loaded, a_ready, g_ready, gelu_ready, h_ready, y_ready, added):
        with ExitStack() as s:
            sb = sbuf(nc, s)
            ge = sb("ge", [P, 2, CH])
            hb = sb("hbg", [P, 2, 3, CH])
            block = s.enter_context(nc.Block())
            jobs = [(q, t) for q in range(2) for t in range(3)]

            @block.sync
            def _(sp):
                if layer_after is not None:
                    load_attention(sp, C, L, layer_after, loaded)
                    sp.wait_ge(loaded, 16 * ATTENTION_LOADS)

            @block.tensor
            def _(pe):
                with pe.Fori(0, NCH // 2) as i:
                    for j, (q, t) in enumerate(jobs):
                        i0, n = FIT[t]
                        if j >= 2:
                            pe.wait_ge(h_ready, i * 6 + (j - 1))
                        x = C.HT[:, bass.ds(i * (2 * CH) + q * CH, CH)]
                        nc.tensor.matmul(C.ps[j % 2][0:n, :], L.W1[:, FI + i0:FI + i0 + n], x, start=True, stop=True).then_inc(g_ready, 1)
                        nc.tensor.matmul(C.ps[2 + j % 2][0:n, :], L.W1[:, i0:i0 + n], x, start=True, stop=True).then_inc(a_ready, 1)
                    for q in range(2):
                        for t, (i0, n) in enumerate(FIT):
                            pe.wait_ge(h_ready, i * 6 + (3 * q + t + 1))
                            mm = nc.tensor.matmul(C.ps[4 + q][:, :], L.W2[0:n, t, :], hb[0:n, q, t, :], start=(t == 0), stop=(t == 2))
                        mm.then_inc(y_ready, 1)
                    pe.wait_ge(added, i * 2 + 2)

            @block.scalar
            def _(act):
                with act.Fori(0, NCH // 2) as i:
                    for j, (q, t) in enumerate(jobs):
                        n = FIT[t][1]
                        act.wait_ge(g_ready, i * 6 + (j + 1))
                        nc.scalar.activation(ge[0:n, j % 2, :], C.ps[j % 2][0:n, :], ACT.Gelu, bias=L.b1[0:n, 1, t:t + 1]).then_inc(gelu_ready, 1)

            @block.vector
            def _(dve):
                with dve.Fori(0, NCH // 2) as i:
                    for j, (q, t) in enumerate(jobs):
                        n = FIT[t][1]
                        dve.wait_ge(gelu_ready, i * 6 + (j + 1))
                        dve.wait_ge(a_ready, i * 6 + (j + 1))
                        nc.vector.scalar_tensor_tensor(hb[0:n, q, t, :], C.ps[2 + j % 2][0:n, :], L.b1[0:n, 0, t:t + 1], ge[0:n, j % 2, :], ALU.add, ALU.mult).then_inc(h_ready, 1)
                    for q in range(2):
                        dve.wait_ge(y_ready, i * 2 + (q + 1))
                        x = C.XT[:, bass.ds(i * (2 * CH) + q * CH, CH)]
                        nc.vector.scalar_tensor_tensor(x, C.ps[4 + q][:, :], L.cols[:, 0:1], x, ALU.add, ALU.add).then_inc(added, 1)
    run_stage(nc, ["loaded", "a_ready", "g_ready", "gelu_ready", "h_ready", "y_ready", "added"], body)


def l2_ffn(nc, C):
    L = Core()
    with ExitStack() as s:
        sb = sbuf(nc, s)
        L.Wqkv, L.Wo = sb("Wqkv", [P, 3 * INNER]), sb("Wo", [P, 8, P])
        L.W1, L.W2, L.b1, L.cols = sb("W1", [P, 2 * FI]), sb("W2", [P, 3, P]), sb("b1", [P, 2, 3]), sb("cols", [P, 3])
        L.XS = sb("XS", [P, TOK])
        L.X0 = sb("X0", [P, TOK])
        keep_input(nc, C, L.X0)
        layer_norm(nc, C, C.XT, src=L.X0)
        L.scl, L.scw, L.base, L.win = sb("scl", [P, 2, LD]), sb("scw", [P, 2, LD]), sb("base", [P, 2, 2, 2, LD]), sb("win", [P, 2, 2, KW], BF16)
        first_weights(nc, C, L)

        def one_layer(layer, layer_after):
            local_attention(nc, C, L, layer)
            shift_tokens(nc, C, L)
            layer_norm(nc, C, C.HT, gain=L.cols[:, 1:2], shift=L.cols[:, 2:3], src=L.XS)
            geglu(nc, C, L, layer_after)

        with nc.Fori(0, LDEPTH - 1) as layer:
            one_layer(layer, layer + 1)
        one_layer(LDEPTH - 1, None)
        add_input(nc, C, L.X0)


def keep_input(nc, C, X0, columns=()):
    def body(kept, loaded):
        with nc.Block() as block:
            @block.sync
            def _(sp):
                for dst, src in columns:
                    sp.dma_start(dst, src.unsqueeze(1)).then_inc(loaded, 16)
                if columns:
                    sp.wait_ge(loaded, 16 * len(columns))

            @block.vector
            def _(dve):
                nc.vector.tensor_copy(X0[:, :], C.XT[:, :]).then_inc(kept, 1)
    run_stage(nc, ["kept", "loaded"], body)


def add_input(nc, C, X0):
    def body(added):
        with nc.Block() as block:
            @block.vector
            def _(dve):
                nc.vector.tensor_tensor(C.XT[:, :], C.XT[:, :], X0[:, :], ALU.add).then_inc(added, 1)
    run_stage(nc, ["added"], body)


def rotary_tables():
    half = np.arange(0, LD, 2, dtype=np.float32)
    inv_freq = (1.0 / 10000.0 ** (half.astype(np.float64) / LD)).astype(np.float32)
    t = np.arange(S, dtype=np.float32)
    f = t[:, None] * inv_freq[None, :]
    f = np.concatenate([f, f], -1).astype(np.float64)
    bs = (half.astype(np.float64) + 0.4 * LD) / (1.4 * LD)
    sc = bs[None, :] ** ((t.astype(np.float64) - S // 2) / (WIN // 2))[:, None]
    sc = np.concatenate([sc, sc], -1)
    sign = np.where(np.arange(LD) < LD // 2, -1.0, 1.0)[None, :]
    out = np.zeros((P, 2, 2, 2, LD), np.float32)
    for tile in range(2):
        r = slice(tile * P, (tile + 1) * P)
        for a, m in enumerate((sc, 1.0 / sc)):
            out[:, 0, tile, a, :] = (np.cos(f) * m)[r]
            out[:, 1, tile, a, :] = (np.sin(f) * sign * m)[r]
    return out


def window_mask():
    q, k = np.arange(P)[:, None], np.arange(KW)[None, :] - WIN
    out = np.zeros((P, 2, 2, KW), np.float32)
    for tile in range(2):
        seen = (k <= q) & (q <= k + WIN) & ((k >= 0) | (tile == 1))
        out[:, tile, :, :] = np.where(seen, 0.0, NEG)[:, None, :]
    return out


NEXP = 4
DFF = 4 * E
FT = DFF // P


def l3f_qkv(nc, C, A):
    def body(loaded, prepared, conv_ready, qk_ready, qk_kept, v_ready, v_kept, own):
        with ExitStack() as s:
            sb = sbuf(nc, s)
            cw, ta = sb("cw", [P, 3]), sb("ta", [P, 2, CH])
            aw = sb("aw", [P, 3, E])
            asw = sb("asw", [P, 2, E])
            rope = sb("rope", [P, 2, S])
            CV = sb("CV", [P, TOK])
            block = s.enter_context(nc.Block())
            jobs = [(n, c) for c in range(NCH) for n in range(2)]

            @block.sync
            def _(sp):
                sp.dma_start(cw[:, :], C.i["L3_ffn_conv_w"].rearrange("c o k -> c (o k)")).then_inc(loaded, 16)
                sp.dma_start(aw[:, :, :], C.i["L3_ffn_attn_w"].rearrange("c (n e) -> c n e", n=3)).then_inc(loaded, 16)
                sp.dma_start(rope[:, :, :], C.c["rope8"]).then_inc(loaded, 16)
                sp.dma_start(A.wo, C.i["L3_ffn_proj_w"]).then_inc(loaded, 16)
                sp.dma_start(A.MQ[:, :, :], C.c["causal_q"]).then_inc(loaded, 16)
                sp.dma_start(A.MK[:, :, :], C.c["causal_k"]).then_inc(loaded, 16)

            @block.vector
            def _(dve):
                st = Steps(dve, own)
                nc.vector.memset(A.bo, 0.0)
                nc.vector.memset(A.VA4[:, :, :, HD:HD + 1], 1.0)
                dve.wait_ge(loaded, 96)
                H2 = HD // 2
                for n in range(2):
                    w = aw[:, n, :].rearrange("p (h d) -> p h d", h=NH)
                    o = asw[:, n, :].rearrange("p (h d) -> p h d", h=NH)
                    nc.vector.tensor_scalar(o[:, :, 0:H2], w[:, :, H2:HD], -1.0, None, ALU.mult)
                    last = nc.vector.tensor_copy(o[:, :, H2:HD], w[:, :, 0:H2])
                last.then_inc(prepared, 1)
                st.then(nc.vector.tensor_scalar(CV[:, :], C.HT[:, :], cw[:, 2:3], None, ALU.mult))
                for k in (1, 2):
                    for b in range(B):
                        o = CV[:, b * S + k:(b + 1) * S]
                        last = nc.vector.scalar_tensor_tensor(o, C.HT[:, b * S:(b + 1) * S - k], cw[:, 2 - k:3 - k], o, ALU.mult, ALU.add)
                    if k == 1:
                        st.then(last)
                last.then_inc(conv_ready, 1)
                for j, (n, c) in enumerate(jobs):
                    dve.wait_ge(qk_ready, j + 1)
                    bs = lambda a: a.rearrange("p (b s) -> p b s", s=S)
                    tab = lambda k: rope[:, k, :].unsqueeze(1).to_broadcast([P, 2, S])
                    dst = (A.QT, A.KT)[n][:, c * CH:(c + 1) * CH]
                    nc.vector.tensor_tensor(bs(dst), bs(C.ps[2 * n][:, :]), tab(0), ALU.mult)
                    st.then(nc.vector.tensor_tensor(bs(ta[:, n, :]), bs(C.ps[2 * n + 1][:, :]), tab(1), ALU.mult))
                    nc.vector.tensor_tensor(dst, dst, ta[:, n, :], ALU.add).then_inc(qk_kept, 1)
                for q in range(4):
                    dve.wait_ge(v_ready, q + 1)
                    nc.vector.tensor_copy(A.VA4[:, 4 * q:4 * q + 4, :, 0:HD], C.ps[4 + q][:, :].rearrange("p (t h d) -> p t h d", t=4, h=NH)).then_inc(v_kept, 1)

            @block.tensor
            def _(pe):
                pe.wait_ge(loaded, 96)
                pe.wait_ge(prepared, 1)
                pe.wait_ge(conv_ready, 1)
                for j, (n, c) in enumerate(jobs):
                    if j >= 2:
                        pe.wait_ge(qk_kept, j - 1)
                    x = CV[:, c * CH:(c + 1) * CH]
                    nc.tensor.matmul(C.ps[2 * n][:, :], aw[:, n, :], x, start=True, stop=True)
                    nc.tensor.matmul(C.ps[2 * n + 1][:, :], asw[:, n, :], x, start=True, stop=True).then_inc(qk_ready, 1)
                for q in range(4):
                    for t in range(4):
                        n = 4 * q + t
                        mm = nc.tensor.matmul(C.ps[4 + q][:, t * P:(t + 1) * P], CV[:, n * P:(n + 1) * P], aw[:, 2, :], start=True, stop=True)
                    mm.then_inc(v_ready, 1)
    run_stage(nc, ["loaded", "prepared", "conv_ready", "qk_ready", "qk_kept", "v_ready", "v_kept", "own"], body)


def moe_prepare(nc, C, M):
    def body(loaded, routed, own):
        with ExitStack() as s:
            sb = sbuf(nc, s)
            rw = sb("rw", [P, NEXP])
            lg, eq = sb("lg", [P, NT, NEXP]), sb("eq", [P, NT, NEXP])
            mx, free = sb("mxr", [P, NT]), sb("free", [P, NT])
            block = s.enter_context(nc.Block())

            @block.sync
            def _(sp):
                sp.dma_start(rw[:, :], C.i["L3_ffn_router_w"]).then_inc(loaded, 16)
                for e in range(NEXP):
                    sp.dma_start(M.WV[:, e, :], C.i["L3_ffn_expert_wv"][e]).then_inc(loaded, 16)
                    sp.dma_start(M.WP[:, e, :, :], C.i["L3_ffn_expert_proj"][e].rearrange("(t p) n -> p t n", p=P)).then_inc(loaded, 16)
                sp.wait_ge(loaded, 16 * 9)

            @block.tensor
            def _(pe):
                pe.wait_ge(loaded, 16 * 9)
                for t in range(NT):
                    mm = nc.tensor.matmul(C.ps[0][:, t * NEXP:(t + 1) * NEXP], C.HT[:, t * P:(t + 1) * P], rw[:, :], start=(t == 0), stop=True, skip_group_check=True)
                mm.then_inc(routed, 1)

            @block.vector
            def _(dve):
                st = Steps(dve, own)
                dve.wait_ge(routed, 1)
                st.then(nc.vector.tensor_copy(lg[:, :, :].rearrange("p t e -> p (t e)"), C.ps[0][:, 0:NT * NEXP]))
                st.then(nc.vector.tensor_reduce(mx[:, :], lg[:, :, :], AX.X, ALU.max))
                st.then(nc.vector.tensor_tensor(eq[:, :, :], lg[:, :, :], mx[:, :].unsqueeze(2).to_broadcast([P, NT, NEXP]), ALU.is_equal))
                st.then(nc.vector.tensor_scalar(free[:, :], eq[:, :, 0], -1.0, 1.0, ALU.mult, ALU.add))
                nc.vector.tensor_copy(M.pick[:, :, 0], eq[:, :, 0])
                for e in range(1, NEXP):
                    st.then(nc.vector.tensor_tensor(M.pick[:, :, e], eq[:, :, e], free[:, :], ALU.mult))
                    st.then(nc.vector.tensor_tensor(free[:, :], free[:, :], M.pick[:, :, e], ALU.subtract))
    run_stage(nc, ["loaded", "routed", "own"], body)


def moe_experts(nc, C, M):
    NJ = NEXP * FT
    def body(g_ready, v_ready, silu_ready, h_ready, y_ready, y_kept, turned, added, own):
        with ExitStack() as s:
            sb = sbuf(nc, s)
            sg = sb("sgm", [P, 2, CH])
            hb = sb("hbm", [P, 2, FT, CH])
            acc = sb("accm", [P, 4, E])
            pick = sb("pickc", [P, 4, NEXP])
            block = s.enter_context(nc.Block())
            jobs = [(e, t) for e in range(NEXP) for t in range(FT)]

            @block.tensor
            def _(pe):
                with pe.Fori(0, NCH) as i:
                    def down(e):
                        pe.wait_ge(h_ready, i * NJ + FT * (e + 1))
                        if e >= 2:
                            pe.wait_ge(y_kept, i * NEXP + (e - 1))
                        for k in range(4):
                            for t in range(FT):
                                mm = nc.tensor.matmul(C.ps[4 + e % 2][:, k * P:(k + 1) * P], hb[:, e % 2, t, k * P:(k + 1) * P], M.WP[:, e, t, :], start=(t == 0), stop=(t == FT - 1), skip_group_check=True)
                        mm.then_inc(y_ready, 1)
                    x = C.HT[:, bass.ds(i * CH, CH)]
                    for j, (e, t) in enumerate(jobs):
                        if j >= 2:
                            pe.wait_ge(h_ready, i * NJ + (j - 1))
                        nc.tensor.matmul(C.ps[j % 2][:, :], M.WV[:, e, t * P:(t + 1) * P], x, start=True, stop=True).then_inc(g_ready, 1)
                        nc.tensor.matmul(C.ps[2 + j % 2][:, :], M.WV[:, e, DFF + t * P:DFF + (t + 1) * P], x, start=True, stop=True).then_inc(v_ready, 1)
                        if t == 1 and e >= 1:
                            down(e - 1)
                    down(NEXP - 1)
                    pe.wait_ge(y_kept, i * NEXP + NEXP)
                    for k in range(4):
                        mm = nc.tensor.transpose(C.ps[6][:, k * P:(k + 1) * P], acc[:, k, :], C.ident[:, :])
                    mm.then_inc(turned, 1)

            @block.scalar
            def _(act):
                with act.Fori(0, NCH) as i:
                    for j, (e, t) in enumerate(jobs):
                        act.wait_ge(g_ready, i * NJ + (j + 1))
                        nc.scalar.activation(sg[:, j % 2, :], C.ps[j % 2][:, :], ACT.Silu).then_inc(silu_ready, 1)

            @block.vector
            def _(dve):
                with dve.Fori(0, NCH) as i:
                    st = Steps(dve, own, i)

                    def keep(e):
                        dve.wait_ge(y_ready, i * NEXP + (e + 1))
                        for k in range(4):
                            y = C.ps[4 + e % 2][:, k * P:(k + 1) * P]
                            if e == 0:
                                last = nc.vector.tensor_scalar(acc[:, k, :], y, pick[:, k, e:e + 1], None, ALU.mult)
                            else:
                                last = nc.vector.scalar_tensor_tensor(acc[:, k, :], y, pick[:, k, e:e + 1], acc[:, k, :], ALU.mult, ALU.add)
                        last.then_inc(y_kept, 1)
                        dve.wait_ge(y_kept, i * NEXP + (e + 1))

                    st.then(nc.vector.tensor_copy(pick[:, :, :], M.pick[:, bass.ds(i * 4, 4), :]))
                    for j, (e, t) in enumerate(jobs):
                        dve.wait_ge(silu_ready, i * NJ + (j + 1))
                        dve.wait_ge(v_ready, i * NJ + (j + 1))
                        nc.vector.tensor_tensor(hb[:, e % 2, t, :], C.ps[2 + j % 2][:, :], sg[:, j % 2, :], ALU.mult).then_inc(h_ready, 1)
                        if t == 2 and e >= 1:
                            keep(e - 1)
                    keep(NEXP - 1)
                    dve.wait_ge(turned, i + 1)
                    xx = C.XT[:, bass.ds(i * CH, CH)]
                    nc.vector.tensor_tensor(xx, xx, C.ps[6][:, :], ALU.add).then_inc(added, 1)
    run_stage(nc, ["g_ready", "v_ready", "silu_ready", "h_ready", "y_ready", "y_kept", "turned", "added", "own"], body)


def l3_ffn(nc, C):
    with ExitStack() as s0:
        X0 = sbuf(nc, s0)("X0", [P, TOK])
        cols = sbuf(nc, s0)("ln_cols", [P, 4])
        keep_input(nc, C, X0, [(cols[:, k:k + 1], C.i[f"L3_ffn_{n}"]) for k, n in enumerate(("ln1_w", "ln1_b", "ln2_w", "ln2_b"))])
        layer_norm(nc, C, C.XT, src=X0)
        layer_norm(nc, C, C.HT, gain=cols[:, 0:1], shift=cols[:, 1:2])
        A = Core()
        with ExitStack() as s:
            sb = sbuf(nc, s)
            wo_t, bo_t = sb("wo_t", [P, E]), sb("bo_t", [P, 1])
            A.wo, A.bo = wo_t[:, :], bo_t[:, :]
            A.MQ, A.MK = sb("MQc", [P, 2, S], BF16), sb("MKc", [P, 2, S], BF16)
            VA = sb("VA", [P, NT, NH * (HD + 1)])
            A.VA, A.VA4 = VA, VA[:, :, :].rearrange("p n (h e) -> p n h e", h=NH)
            with ExitStack() as s2:
                A.QT, A.KT = sbuf(nc, s2)("QT", [P, TOK]), sbuf(nc, s2)("KT", [P, TOK])
                l3f_qkv(nc, C, A)
                split_parts(nc, C, A.QT, A.KT)
            A.scale = float(HD) ** -0.5
            A.key_mask = None
            flat = lambda m: m[:, :, :].rearrange("p t s -> p (t s)")
            A.masks = [(lambda b: flat(A.MQ), lambda b: flat(A.MK))]
            attend(nc, C, A)
        layer_norm(nc, C, C.HT, gain=cols[:, 2:3], shift=cols[:, 3:4])
        with ExitStack() as s:
            sb = sbuf(nc, s)
            M = Core()
            M.WV, M.WP, M.pick = sb("WV", [P, NEXP, 2 * DFF]), sb("WP", [P, NEXP, FT, E]), sb("pick", [P, NT, NEXP])
            moe_prepare(nc, C, M)
            moe_experts(nc, C, M)
        add_input(nc, C, X0)


def rope_rows():
    inv_freq = (1.0 / 10000.0 ** (np.arange(0, HD, 2, dtype=np.float64) / HD)).astype(np.float32)
    f = np.arange(S, dtype=np.float32)[:, None] * inv_freq[None, :]
    f = np.tile(np.concatenate([f, f], -1).astype(np.float64).T, (NH, 1))
    return np.ascontiguousarray(np.stack([np.cos(f), np.sin(f)], 1).astype(np.float32))


def causal_masks():
    hidden = np.where(np.arange(S)[None, :] > np.arange(S)[:, None], NEG, 0.0)
    rows = lambda m: np.ascontiguousarray(m.reshape(2, P, S).transpose(1, 0, 2))
    return rows(hidden), rows(hidden.T)


def program(nc, ins, consts, out, stages):
    C = Core()
    C.i, C.c, C.out = ins, consts, out
    with ExitStack() as ctx:
        def sb(name, shape, dt=F32):
            return ctx.enter_context(nc.sbuf_tensor(name, shape, dt))
        C.psum = ctx.enter_context(nc.psum_tensor("psum", [P, 8, 512], F32))
        C.ps = [C.psum[:, n, :] for n in range(8)]
        C.ident = sb("ident", [P, P])
        C.identb = sb("identb", [P, P], BF16)
        C.mean_w = sb("mean_w", [P, P])
        C.eps = sb("eps", [P, 1])
        C.one = sb("one", [P, 1])
        C.XT = sb("XT", [P, TOK])
        C.CT = sb("CT", [P, TOK])
        C.CN = sb("CN", [P, NT, E])
        C.HT = sb("HT", [P, TOK])
        C.qk_parts = nc.dram_tensor("qk_parts", (2, 3, P, TOK), BF16, kind="Internal").ap()
        C.key_bias = nc.dram_tensor("key_bias", (B, S), BF16, kind="Internal").ap()
        load_inputs(nc, C)
        for stage in stages:
            stage(nc, C)
        store_output(nc, C, C.XT)


STAGES = [l0_xattn, l0_ffn, l1_xattn, l1_ffn, l2_xattn, l2_ffn, l3_xattn, l3_ffn]


def head_places():
    out = np.zeros((P, 4, 2, P), np.float32)
    for h in range(NH):
        row, feature = 32 * (h % 4), HD * h
        out[row:row + HD, h // 4, 0, feature:feature + HD] = np.eye(HD)
        out[row + HD, h // 4, 1, feature:feature + HD] = 1.0
    return out


def constants():
    ident = np.eye(P, dtype=np.float32)
    bf16 = mybir.dt.np(BF16)
    key, query = np.arange(P)[:, None], np.arange(P)[None, :]
    return {
        "ident": ident, "identb": ident.astype(bf16),
        "causal_kq": np.where(key > query, NEG, 0.0).astype(bf16),
        "rotary": rotary_tables(), "window": window_mask().astype(bf16),
        "rope8": rope_rows(), "causal_q": causal_masks()[0].astype(bf16), "causal_k": causal_masks()[1].astype(bf16),
        "head_places": head_places(),
        "head_blocks": np.kron(np.eye(NH), np.ones((HD, HD))).astype(np.float32),
        "max_rows": np.ascontiguousarray(np.repeat(np.tile(np.eye(NH), (3, 1))[:, :, None], P, 2).astype(bf16)),
        "head_rows": np.ascontiguousarray(np.repeat(np.eye(L0_NH, dtype=np.float32)[:, :, None], P, 2)),
    }


def build(nc, inputs, stages):
    arrays, ins, consts = {}, {}, {}
    for group, values in ((ins, inputs), (consts, constants())):
        for name, a in values.items():
            a = np.ascontiguousarray(a)
            arrays[f"in_{name}_dram"] = a
            group[name] = nc.dram_tensor(f"in_{name}_dram", a.shape, mybir.dt.from_np(a.dtype), kind="ExternalInput").ap()
    out = nc.dram_tensor("out_0_dram", (B, S, E), F32, kind="ExternalOutput").ap()
    program(nc, ins, consts, out, [STAGES[n] for n in stages])
    return arrays, out


def kernel(**inputs):
    import concourse.bacc as bacc
    from concourse.bass_utils import run_bass_kernel_spmd

    nc = bacc.Bacc("TRN2", target_bir_lowering=False, num_devices=1)
    arrays, _ = build(nc, {name: np.asarray(a) for name, a in inputs.items()}, range(len(STAGES)))
    r = run_bass_kernel_spmd(nc, [arrays], core_ids=[0])
    return np.asarray(r.results[0]["out_0_dram"])
```
